# Optimizing a Trainium2 kernel written in Bass

```python
import numpy as np
import jax
import jax.numpy as jnp

def _softmax(x, axis=-1):
    return jax.nn.softmax(x, axis=axis)

def _gelu(x):
    return jax.nn.gelu(x, approximate=True)

def _silu(x):
    return jax.nn.silu(x)

def _sigmoid(x):
    return jax.nn.sigmoid(x)

def _layernorm(x, axis=-1, eps=1e-05):
    m = jnp.mean(x, axis=axis, keepdims=True)
    v = jnp.var(x, axis=axis, keepdims=True)
    return (x - m) / jnp.sqrt(v + eps)

def _scatter_add(tgt, idx, src, axis=0):
    return tgt.at[idx].add(src)

def _segment_sum(src, seg, n):
    return jax.ops.segment_sum(src, seg, n)
kernel_name = 'mk_seq_postln_d1_jaxref_r4_97ec2a'

def setup_inputs(seed: int=0):
    np.random.seed(seed)
    _w = jnp.asarray

    def _L0_attn_setup():
        import jax, jax.numpy as jnp
        import numpy as np
        HIDDEN = 512
        HEADS = 16
        HEAD_DIM = HIDDEN // HEADS
        NEG = -10000000000.0
        key = jax.random.key(seed)
        k1, k2, k3 = jax.random.split(key, 3)
        x = jax.random.normal(k1, (2, 512, HIDDEN), dtype=jnp.float32)
        w_qkv = jax.random.normal(k2, (HIDDEN, 3 * HIDDEN), dtype=jnp.float32) / np.sqrt(HIDDEN)
        w_out = jax.random.normal(k3, (HIDDEN, HIDDEN), dtype=jnp.float32) / np.sqrt(HIDDEN)
        return {'x': x, 'w_qkv': w_qkv, 'w_out': w_out}
    _L0_attn_in = _L0_attn_setup()

    def _L0_ffn_setup():
        import jax, jax.numpy as jnp
        import numpy as np
        HIDDEN = 512
        INTER = 2048
        SCALE = 64.0

        def fwht(x):
            orig_shape = x.shape
            n = orig_shape[-1]
            x = x.reshape(-1, n)
            h = 1
            while h < n:
                x = x.reshape(-1, n // (2 * h), 2, h)
                a, b = (x[:, :, 0, :], x[:, :, 1, :])
                x = jnp.stack([a + b, a - b], axis=2).reshape(-1, n)
                h *= 2
            return (x / jnp.sqrt(jnp.asarray(n, x.dtype))).reshape(orig_shape)
        key = jax.random.key(seed)
        ks = jax.random.split(key, 8)
        inp = jax.random.normal(ks[0], (4, 512, HIDDEN), dtype=jnp.float32)
        SU_ug = jnp.where(jax.random.bernoulli(ks[1], 0.5, (HIDDEN,)), 1.0, -1.0).astype(jnp.float32)
        SU_dp = jnp.where(jax.random.bernoulli(ks[2], 0.5, (INTER,)), 1.0, -1.0).astype(jnp.float32)
        Wscale_ug = jax.random.uniform(ks[3], (2 * INTER,), jnp.float32, 0.5, 1.5)
        Wscale_dp = jax.random.uniform(ks[4], (HIDDEN,), jnp.float32, 0.5, 1.5)
        W_up = jax.random.normal(ks[5], (INTER, HIDDEN), dtype=jnp.float32) * 0.02
        W_gate = jax.random.normal(ks[6], (INTER, HIDDEN), dtype=jnp.float32) * 0.02
        W_down = jax.random.normal(ks[7], (HIDDEN, INTER), dtype=jnp.float32) * 0.02
        return {'input': inp, 'SU_ug': SU_ug, 'SU_dp': SU_dp, 'Wscale_ug': Wscale_ug, 'Wscale_dp': Wscale_dp, 'W_up': W_up, 'W_gate': W_gate, 'W_down': W_down}
    _L0_ffn_in = _L0_ffn_setup()
    _d = {'L0_attn_x': _L0_attn_in['x'], 'L0_attn_w_qkv': _L0_attn_in['w_qkv'], 'L0_attn_w_out': _L0_attn_in['w_out'], 'L0_ffn_SU_ug': _L0_ffn_in['SU_ug'], 'L0_ffn_SU_dp': _L0_ffn_in['SU_dp'], 'L0_ffn_Wscale_ug': _L0_ffn_in['Wscale_ug'], 'L0_ffn_Wscale_dp': _L0_ffn_in['Wscale_dp'], 'L0_ffn_W_up': _L0_ffn_in['W_up'], 'L0_ffn_W_gate': _L0_ffn_in['W_gate'], 'L0_ffn_W_down': _L0_ffn_in['W_down']}
    _x0 = _d['L0_attn_x']
    _d['L0_attn_x'] = jax.random.normal(jax.random.fold_in(jax.random.key(seed), 1), (4, 1024, 512), dtype=_x0.dtype)
    del _x0
    return _d

def reference(L0_attn_x, L0_attn_w_qkv, L0_attn_w_out, L0_ffn_SU_ug, L0_ffn_SU_dp, L0_ffn_Wscale_ug, L0_ffn_Wscale_dp, L0_ffn_W_up, L0_ffn_W_gate, L0_ffn_W_down):

    def _L0_attn_ref(x, w_qkv, w_out):
        import jax, jax.numpy as jnp
        import numpy as np
        HIDDEN = 512
        HEADS = 16
        HEAD_DIM = HIDDEN // HEADS
        NEG = -10000000000.0
        b, s, _ = x.shape
        qkv = x @ w_qkv
        qkv = qkv.reshape(b, s, 3, HEADS, HEAD_DIM)
        q, k, v = (qkv[:, :, 0], qkv[:, :, 1], qkv[:, :, 2])
        scale = jnp.sqrt(jnp.float32(HEAD_DIM)).astype(x.dtype)
        q = q / scale
        scores = jnp.einsum('bqhd,bkhd->bhqk', q, k)
        causal_mask = jnp.arange(s)[:, None] >= jnp.arange(s)[None, :]
        scores = jnp.where(causal_mask[None, None], scores, NEG)
        attn = jax.nn.softmax(scores, axis=-1)
        out = jnp.einsum('bhqk,bkhd->bqhd', attn, v).reshape(b, s, HIDDEN)
        return out @ w_out

    def _L0_ffn_ref(input, SU_ug, SU_dp, Wscale_ug, Wscale_dp, W_up, W_gate, W_down):
        import jax, jax.numpy as jnp
        import numpy as np
        HIDDEN = 512
        INTER = 2048
        SCALE = 64.0

        def fwht(x):
            orig_shape = x.shape
            n = orig_shape[-1]
            x = x.reshape(-1, n)
            h = 1
            while h < n:
                x = x.reshape(-1, n // (2 * h), 2, h)
                a, b = (x[:, :, 0, :], x[:, :, 1, :])
                x = jnp.stack([a + b, a - b], axis=2).reshape(-1, n)
                h *= 2
            return (x / jnp.sqrt(jnp.asarray(n, x.dtype))).reshape(orig_shape)
        n = SU_ug.shape[0]
        x = input.reshape(-1, n)
        x = fwht(x * SU_ug) / SCALE
        x_up = x @ W_up.T * (Wscale_ug[:INTER] * SCALE)
        x_gate = x @ W_gate.T * (Wscale_ug[INTER:] * SCALE)
        x = jax.nn.silu(x_gate) * x_up
        x = fwht(x * SU_dp) / SCALE
        x = x @ W_down.T * (Wscale_dp * SCALE)
        return x.reshape(input.shape)
    x = L0_attn_x
    x = _layernorm(x + _L0_attn_ref(x, L0_attn_w_qkv, L0_attn_w_out), axis=-1)
    x = _layernorm(x + _L0_ffn_ref(x, L0_ffn_SU_ug, L0_ffn_SU_dp, L0_ffn_Wscale_ug, L0_ffn_Wscale_dp, L0_ffn_W_up, L0_ffn_W_gate, L0_ffn_W_down), axis=-1)
    return x

_drawn_inputs = setup_inputs


def setup_inputs(seed=0):
    import zlib

    import numpy as np

    out = dict(_drawn_inputs(seed))
    spreads = {}
    factors = {}
    for name, (base, spread) in spreads.items():
        noise = np.random.default_rng([zlib.crc32(name.encode()), seed]).standard_normal(out[name].shape)
        drawn = base * np.exp(spread * noise) if base else spread * noise
        out[name] = jnp.asarray(drawn.astype(out[name].dtype))
    for name, factor in factors.items():
        out[name] = (out[name] * factor).astype(out[name].dtype)
    return out
```

```python
import numpy as np
import concourse.bass as bass
from concourse import mybir
from contextlib import ExitStack

F32 = mybir.dt.float32
F32R = mybir.dt.float32r
BF16 = mybir.dt.bfloat16
ALU = mybir.AluOpType
ACT = mybir.ActivationFunctionType
AX = mybir.AxisListType

P = 128
B, S, D = 4, 1024, 512
H, DH = 16, 32
T = B * S
INTER = 2048
KT = D // P
FT = INTER // P
CH = 512
NCH = T // CH
EPS = 1e-5
MASKED = -1e30


PASSES = ((0, 0), (0, 1), (1, 0))


def words(ap):
    return ap.bitcast(F32)


def project_qkv(nc, sem, io):
    RING = 6
    QK0 = [("qk", 0, n) for n in range(8)]
    V0 = [("v", 0, n) for n in range(4)]
    QK1 = [("qk", 1, n) for n in range(8)]
    V1 = [("v", 1, n) for n in range(4)]
    UP = [("up", 0, n) for n in range(4)]
    GATE = [("gate", 1, n) for n in range(4)]
    DOWN = [("down", 2, n) for n in range(4)]
    JOBS = QK0 + UP + V0 + QK1[:4] + GATE + QK1[4:] + V1 + DOWN
    NJ = len(JOBS)
    FOLD = ("up", "gate", "down")
    FOLD_AT = {0: 2, 1: 14, 2: 26}
    SPLIT_AT = {1: 5, 0: 24}

    def dmas(job):
        return 2 if job[0] in FOLD else 1

    def stored(i, n):
        slot = n % RING
        each = sum(dmas(JOBS[m]) for m in range(slot, NJ, RING))
        return 16 * (i * each + sum(dmas(JOBS[m]) for m in range(slot, n, RING)))

    STEPS = (4, 8, 17)

    def last_of(kind, u):
        return max(n for n, j in enumerate(JOBS) if j[:2] == (kind, u))

    def folds_before(n):
        return sum(1 for j in JOBS[:n] if j[0] in FOLD)

    with ExitStack() as ctx:
        sb = lambda name, shape, dt: ctx.enter_context(nc.sbuf_tensor(name, shape, dt))
        wqkv = sb("wqkv_split", [P, 2, KT, 3 * D], F32R)
        x_raw = [sb(f"x_raw{s}", [P, KT, CH], F32) for s in range(2)]
        x_hi = [sb(f"x_hi{s}", [P, KT, CH], F32R) for s in range(2)]
        x_lo = [sb(f"x_lo{s}", [P, KT, CH], F32R) for s in range(2)]
        raw = [sb(f"w_raw{s}", [P, 2048], F32) for s in range(3)]
        half = sb("butterfly", [P, 2048], F32)
        rot = sb("rotated", [P, 2048], F32)
        rot_hi = sb("rotated_hi", [P, 2048], F32R)
        rot_lo = sb("rotated_lo", [P, 2048], F32R)
        scaled = [sb(f"scaled{s}", [P, CH], F32) for s in range(2)]
        stage = [sb(f"stage{s}", [P, 2 * CH], F32R) for s in range(RING)]
        had_f = sb("had_f", [P, P], F32)
        had = sb("had", [P, P], F32R)
        su_ug = sb("su_ug", [P, KT], F32)
        su_dp = sb("su_dp", [P, FT], F32)
        ws_dp = sb("ws_dp", [P, D], F32)
        bank = [ctx.enter_context(nc.psum_tensor(f"pj{s}", [P, CH], F32)) for s in range(RING)]

        raw_ld = [sem(f"raw_ld{s}") for s in range(3)]
        x_ld = [sem(f"x_ld{s}") for s in range(2)]
        const_ld = sem("const_ld")
        store_done = [sem(f"store_done{s}") for s in range(RING)]
        wsplit_hi = sem("wsplit_hi")
        wsplit_done = sem("wsplit_done")
        wo_stored = sem("wo_stored")
        had_ready = sem("had_ready")
        x_hi_done = sem("x_hi_done")
        x_split = sem("x_split")
        butter = sem("butter")
        rot_hi_done = sem("rot_hi_done")
        rot_split = sem("rot_split")
        full = sem("pj_full")
        scaled_done = sem("scaled_done")
        hi_done = sem("pj_hi_done")
        evacuated = sem("pj_evacuated")

        ITERS = B
        wqkv_in = io["wqkv"].rearrange("(k p) n -> p k n", p=P)
        wout_in = io["wout"].rearrange("(k p) n -> p k n", p=P)
        xt_in = io["xt"].rearrange("(k p) t -> p k t", p=P)
        wug_in = io["wugt"].rearrange("(k p) f -> p k f", p=P)
        wd_in = io["wdt"].rearrange("(k p) n -> p k n", p=P)

        def as_kt(t, k=KT):
            return t[:, :].rearrange("p (k n) -> p k n", k=k)

        def out_parts(job, n):
            st = stage[n % RING]
            if job[0] == "v":
                v = st[:, :].rearrange("p (h c d) -> p h c d", h=H, c=2)
                return v[:, :, 0, :], v[:, :, 1, :]
            return st[:, 0:CH], st[:, CH:2 * CH]

        def shaped(ap, job):
            return ap.rearrange("p (h d) -> p h d", h=H) if job[0] == "v" else ap

        with nc.Block() as block:
            @block.sync
            def _(sp):
                for s in range(3):
                    sp.dma_start(as_kt(raw[s]), wqkv_in[:, :, s * D:(s + 1) * D]).then_inc(raw_ld[s], 16)
                    if s == 0:
                        sp.dma_start(x_raw[0][:, :, :], xt_in[:, :, 0:CH]).then_inc(x_ld[0], 16)
                sp.dma_start(had_f[:, :], io["consts"][:, 0:P]).then_inc(const_ld, 16)
                sp.dma_start(su_ug[:, :], io["su_ug"]).then_inc(const_ld, 16)
                sp.dma_start(su_dp[:, :], io["su_dp"]).then_inc(const_ld, 16)
                sp.dma_start(ws_dp[:, :], io["ws_dp"].partition_broadcast(P)).then_inc(const_ld, 16)
                sp.dma_start(x_raw[1][:, :, :], xt_in[:, :, CH:2 * CH]).then_inc(x_ld[1], 16)
                sp.wait_ge(wsplit_done, 1)
                sp.dma_start(as_kt(raw[0]), wout_in).then_inc(raw_ld[0], 16)
                sp.wait_ge(wsplit_done, 4)
                for part, t in ((0, rot_hi), (1, rot_lo)):
                    sp.dma_start(io["wo_s"][:, :, part].rearrange("k p n -> p k n"),
                                 words(as_kt(t))).then_inc(wo_stored, 16)
                sp.dma_start(as_kt(raw[0]), wug_in[:, :, 0:CH]).then_inc(raw_ld[0], 16)
                sp.dma_start(as_kt(raw[1]), wug_in[:, :, INTER:INTER + CH]).then_inc(raw_ld[1], 16)
                sp.dma_start(as_kt(raw[2], FT), wd_in[:, :, 0:P]).then_inc(raw_ld[2], 16)

                def body(i, last):
                    for n, job in enumerate(JOBS):
                        kind, u, m = job
                        if not last and kind == "qk" and m == 0:
                            sp.wait_ge(x_split, 2 * i + u + 1)
                            sp.dma_start(x_raw[u][:, :, :],
                                         xt_in[:, :, bass.ds((2 * i + 2 + u) * CH, CH)]).then_inc(x_ld[u], 16)
                        sp.wait_ge(evacuated, NJ * i + n + 1)
                        st = stage[n % RING]
                        done = store_done[n % RING]
                        if kind == "qk":
                            dst = io["q_s"] if m < 4 else io["k_s"]
                            rows = bass.ds(i * D + (m % 4) * P, P)
                            sp.dma_start(dst[:, rows, u * CH:(u + 1) * CH].rearrange("c p t -> p c t"),
                                         words(st[:, :].rearrange("p (c t) -> p c t", c=2))).then_inc(done, 16)
                        elif kind == "v":
                            dst = io["v_s"][bass.ds(i * 8, 8), u * CH + m * P:u * CH + (m + 1) * P, :]
                            sp.dma_start(dst.rearrange("h p c -> p h c"),
                                         words(st[:, :].rearrange("p (h c) -> p h c", h=8))).then_inc(done, 16)
                        else:
                            for part in range(2):
                                src = words(st[:, part * CH:(part + 1) * CH].rearrange("p (f n) -> p f n", f=4))
                                if kind == "down":
                                    dst = io["wd_s"][4 * m:4 * m + 4, :, part, bass.ds(i * P, P)]
                                else:
                                    dst = io["wug_s"][bass.ds(4 * i, 4), :, u, part, m, :]
                                sp.dma_start(dst.rearrange("f p n -> p f n"), src).then_inc(done, 16)
                        if not last and kind in FOLD and m == 3:
                            sp.wait_ge(butter, STEPS[2] * i + STEPS[u])
                            if kind == "down":
                                src = wd_in[:, :, bass.ds((i + 1) * P, P)]
                                sp.dma_start(as_kt(raw[2], FT), src).then_inc(raw_ld[2], 16)
                            else:
                                src = wug_in[:, :, bass.ds(u * INTER + (i + 1) * CH, CH)]
                                sp.dma_start(as_kt(raw[u]), src).then_inc(raw_ld[u], 16)

                with sp.Fori(0, ITERS - 1) as i:
                    body(i, False)
                body(ITERS - 1, True)
                for s in range(RING):
                    sp.wait_ge(store_done[s], stored(ITERS, s))
                sp.wait_ge(wo_stored, 32)

            @block.gpsimd
            def _(pool):
                pool.wait_ge(wo_stored, 32)
                pool.wait_ge(const_ld, 64)

                def step(i, k, op, out, a, b):
                    nc.gpsimd.tensor_tensor(out, a, b, op).then_inc(butter, 1)
                    pool.wait_ge(butter, STEPS[2] * i + k + 1)

                with pool.Fori(0, ITERS) as i:
                    k = 0
                    for u, kind in enumerate(FOLD):
                        pool.wait_ge(raw_ld[u], 16 * i + (48 if u == 0 else 32))
                        if kind == "down":
                            cols = as_kt(raw[2], FT)
                            scale = ws_dp[:, bass.ds(i * P, P)].unsqueeze(1).to_broadcast([P, FT, P])
                            step(i, k, ALU.mult, cols, cols, scale)
                            k += 1
                        stages = 4 if kind == "down" else 2
                        src = raw[u]
                        for st in range(stages):
                            dst = rot if st == stages - 1 else (half, raw[u])[st % 2]
                            near = (2048 >> stages) << st
                            a = src[:, :].rearrange("p (g two w) -> p g two w", two=2, w=near)
                            o = dst[:, :].rearrange("p (g two w) -> p g two w", two=2, w=near)
                            for op, col in ((ALU.add, 0), (ALU.subtract, 1)):
                                step(i, k, op, o[:, :, col, :], a[:, :, 0, :], a[:, :, 1, :])
                                k += 1
                            src = dst
                        assert k == STEPS[u]
                        pool.wait_ge(rot_hi_done, 3 * i + u + 1)
                        nc.gpsimd.tensor_tensor(rot_lo[:, :], rot[:, :], rot_hi[:, :].bitcast(F32),
                                                ALU.subtract).then_inc(rot_split, 1)
                        pool.wait_ge(rot_split, 3 * i + u + 1)

            @block.scalar
            def _(act):
                for s in range(3):
                    act.wait_ge(raw_ld[s], 16)
                    nc.scalar.copy(wqkv[:, 0, :, s * D:(s + 1) * D], as_kt(raw[s])).then_inc(wsplit_hi, 1)
                    if s == 0:
                        act.wait_ge(x_ld[0], 16)
                        nc.scalar.copy(x_hi[0][:, :, :], x_raw[0][:, :, :]).then_inc(x_hi_done, 1)
                act.wait_ge(raw_ld[0], 32)
                nc.scalar.copy(rot_hi[:, :], raw[0][:, :]).then_inc(wsplit_hi, 1)

                def body(i, first, last):
                    for n, job in enumerate(JOBS):
                        kind, u, m = job
                        if not (first and n < RING):
                            act.wait_ge(store_done[n % RING], stored(i, n))
                        hi, _lo = out_parts(job, n)
                        if kind in FOLD:
                            k = folds_before(n)
                            act.wait_ge(scaled_done, 12 * i + k + 1)
                            nc.scalar.copy(hi, scaled[k % 2][:, :]).then_inc(hi_done, 1)
                        else:
                            act.wait_ge(full, NJ * i + n + 1)
                            nc.scalar.copy(hi, shaped(bank[n % RING][:, :], job)).then_inc(hi_done, 1)
                        for t, at in FOLD_AT.items():
                            if n == at:
                                act.wait_ge(butter, STEPS[2] * i + STEPS[t])
                                if not (first and t == 0):
                                    act.wait_ge(full, NJ * i + (last_of(FOLD[t - 1], t - 1) + 1 if t else 0))
                                nc.scalar.copy(rot_hi[:, :], rot[:, :]).then_inc(rot_hi_done, 1)
                        if n == SPLIT_AT[1]:
                            act.wait_ge(x_ld[1], 16 * i + 16)
                            nc.scalar.copy(x_hi[1][:, :, :], x_raw[1][:, :, :]).then_inc(x_hi_done, 1)
                        if n == SPLIT_AT[0] and not last:
                            act.wait_ge(x_ld[0], 16 * i + 32)
                            act.wait_ge(full, NJ * i + last_of("v", 0) + 1)
                            nc.scalar.copy(x_hi[0][:, :, :], x_raw[0][:, :, :]).then_inc(x_hi_done, 1)

                body(0, True, False)
                with act.Fori(1, ITERS - 1) as i:
                    body(i, False, False)
                body(ITERS - 1, False, True)

            @block.vector
            def _(dve):
                for s in range(3):
                    dve.wait_ge(wsplit_hi, s + 1)
                    nc.vector.tensor_tensor(wqkv[:, 1, :, s * D:(s + 1) * D], as_kt(raw[s]),
                                            wqkv[:, 0, :, s * D:(s + 1) * D].bitcast(F32),
                                            ALU.subtract).then_inc(wsplit_done, 1)
                    if s == 0:
                        dve.wait_ge(x_hi_done, 1)
                        nc.vector.tensor_tensor(x_lo[0][:, :, :], x_raw[0][:, :, :],
                                                x_hi[0][:, :, :].bitcast(F32), ALU.subtract).then_inc(x_split, 1)
                        dve.wait_ge(const_ld, 64)
                        nc.vector.tensor_copy(had[:, :], had_f[:, :]).then_inc(had_ready, 1)
                        nc.vector.tensor_scalar(su_ug[:, :], su_ug[:, :], float(D) ** -0.5, None,
                                                ALU.mult).then_inc(had_ready, 1)
                        nc.vector.tensor_scalar(su_dp[:, :], su_dp[:, :], float(INTER) ** -0.5, None,
                                                ALU.mult).then_inc(had_ready, 1)
                dve.wait_ge(had_ready, 3)
                dve.wait_ge(wsplit_hi, 4)
                nc.vector.tensor_tensor(rot_lo[:, :], raw[0][:, :], rot_hi[:, :].bitcast(F32),
                                        ALU.subtract).then_inc(wsplit_done, 1)

                def body(i, last):
                    for n, job in enumerate(JOBS):
                        kind, u, m = job
                        hi, lo = out_parts(job, n)
                        src = shaped(bank[n % RING][:, :], job)
                        if kind in FOLD:
                            k = folds_before(n)
                            dve.wait_ge(full, NJ * i + n + 1)
                            if kind == "down":
                                by = su_dp[:, 4 * m:4 * m + 4].unsqueeze(2).to_broadcast([P, 4, P])
                                nc.vector.tensor_tensor(as_kt(scaled[k % 2]), as_kt(bank[n % RING]), by,
                                                        ALU.mult).then_inc(scaled_done, 1)
                            else:
                                nc.vector.tensor_scalar(scaled[k % 2][:, :], src, su_ug[:, m:m + 1], None,
                                                        ALU.mult).then_inc(scaled_done, 1)
                            src = scaled[k % 2][:, :]
                        dve.wait_ge(hi_done, NJ * i + n + 1)
                        nc.vector.tensor_tensor(lo, src, hi.bitcast(F32), ALU.subtract).then_inc(evacuated, 1)
                        if n == SPLIT_AT[1]:
                            dve.wait_ge(x_hi_done, 2 * i + 2)
                            nc.vector.tensor_tensor(x_lo[1][:, :, :], x_raw[1][:, :, :],
                                                    x_hi[1][:, :, :].bitcast(F32), ALU.subtract).then_inc(x_split, 1)
                        if n == SPLIT_AT[0] and not last:
                            dve.wait_ge(x_hi_done, 2 * i + 3)
                            nc.vector.tensor_tensor(x_lo[0][:, :, :], x_raw[0][:, :, :],
                                                    x_hi[0][:, :, :].bitcast(F32), ALU.subtract).then_inc(x_split, 1)

                with dve.Fori(0, ITERS - 1) as i:
                    body(i, False)
                body(ITERS - 1, True)

            @block.tensor
            def _(pe):
                pe.wait_ge(had_ready, 1)

                def body(i, first):
                    for n, job in enumerate(JOBS):
                        kind, u, m = job
                        if not first:
                            pe.wait_ge(evacuated, NJ * i + n - RING + 1)
                        elif n >= RING:
                            pe.wait_ge(evacuated, n - RING + 1)
                        out = bank[n % RING][:, :]
                        if kind == "qk" and m == 0:
                            pe.wait_ge(x_split, 2 * i + u + 1)
                        if first and u == 0 and kind in ("qk", "v") and m in (0, 4):
                            pe.wait_ge(wsplit_done, 1 if m == 0 else 2)
                        if first and u == 0 and kind == "v" and m == 0:
                            pe.wait_ge(wsplit_done, 3)
                        if kind in FOLD and m == 0:
                            pe.wait_ge(rot_split, 3 * i + u + 1)
                        xs = (x_hi[u], x_lo[u]) if kind in ("qk", "v") else None
                        k = 0
                        if kind == "qk":
                            for kt in range(KT):
                                for wp, xp in PASSES:
                                    mm = nc.tensor.matmul(out, wqkv[:, wp, kt, m * P:(m + 1) * P],
                                                          xs[xp][:, kt, :], start=(k == 0), stop=(k == 11))
                                    k += 1
                        elif kind == "v":
                            for kt in range(KT):
                                for xp, wp in PASSES:
                                    mm = nc.tensor.matmul(out, xs[xp][:, kt, m * P:(m + 1) * P],
                                                          wqkv[:, wp, kt, 2 * D:3 * D], start=(k == 0), stop=(k == 11))
                                    k += 1
                        else:
                            for t, part in enumerate((rot_hi, rot_lo)):
                                mm = nc.tensor.matmul(out, had[:, :], part[:, m * CH:(m + 1) * CH],
                                                      start=(t == 0), stop=(t == 1))
                        mm.then_inc(full, 1)
                body(0, True)
                with pe.Fori(1, ITERS) as i:
                    body(i, False)


def attend(nc, sem, io):
    HEADS = B * H
    UNROLL = 4
    ITERS = HEADS // UNROLL
    NT = 5
    NK = NT * UNROLL
    LAG = 4
    ON_POOL = (1, 3)
    SCALE = float(1.0 / np.sqrt(np.float32(DH)))
    G = P

    TILES = (
        ((0, 3, 256, 256, 128), (256, 2, 256, 256, 256), (512, 0, 0, 512, 512)),
        ((0, 3, 512, 512, None), (512, 1, 128, 384, 512)),
        ((0, 7, 768, 256, 128), (256, 6, 768, 256, 256), (512, 4, 512, 512, 512)),
        ((0, 0, 512, 512, None), (512, 5, 640, 384, 512)),
        ((0, 1, 512, 512, None), (512, 2, 512, 512, None)),
    )
    USED = ((G, 1024), (0, 896), (G, 1024), (0, 896), (0, 1024))
    PV = ((2, 1, 0), (0, 1), (2, 1, 0), (0, 1), (0, 1))
    OPENS = {(0, 2), (1, 0)}
    CLOSES = {(1, 1), (4, 1)}

    ROWS = ((0, 0, 256, 128, 0), (1, 0, 256, 256, 128), (2, 0, 384, 384, 256), (3, 0, 512, 512, 384),
            (4, 0, 384, 384, None), (5, 0, 384, 384, None), (6, 0, 512, 512, None), (7, 0, 512, 512, None),
            (4, 384, 256, 256, 128), (5, 384, 384, 384, 256), (6, 512, 384, 384, 256), (7, 512, 512, 512, 384))
    NR = len(ROWS)
    NS = NR + 1
    AT_TILE = ((0, 1, 2), (3, 4, 5), (6, 7, 8), (9, 10, 11), ())

    with ExitStack() as ctx:
        sb = lambda name, shape, dt: ctx.enter_context(nc.sbuf_tensor(name, shape, dt))
        qs = [sb(f"q_stack{s}", [3 * DH + 1, S], F32R) for s in range(4)]
        ks = [sb(f"k_stack{s}", [3 * DH + 1, S], F32R) for s in range(4)]
        v = [sb(f"v_pair{s}", [P, 8, 4 * DH + 2], F32R) for s in range(2)]
        probs = [sb(f"probs{s}", [P, 2 * CH], F32) for s in range(4)]
        p_hi = [sb(f"p_hi{s}", [P, 2 * CH], F32R) for s in range(NT)]
        p_lo = [sb(f"p_lo{s}", [P, 2 * CH], F32R) for s in range(NT)]
        o_out = [sb(f"o_out{s}", [2 * DH + 1, S], F32) for s in range(2)]
        neg = [sb(f"neg_max{s}", [P, 12], F32) for s in range(2)]
        neg_row = [sb(f"neg_row{s}", [8, P], F32R) for s in range(2)]
        consts = sb("att_consts", [P, 3 * P], F32)
        masks = sb("att_masks", [P, 3 * P], BF16)
        eye, mask_rows, mask_cols = (masks[:, t * P:(t + 1) * P] for t in range(3))
        eye_f = consts[:, 0:P]
        ps_t = [ctx.enter_context(nc.psum_tensor(f"scores{s}", [P, 2 * CH], F32)) for s in range(2)]
        ps_r = [ctx.enter_context(nc.psum_tensor(f"rows{s}", [P, CH], F32)) for s in range(2)]
        ps_o = [ctx.enter_context(nc.psum_tensor(f"heads_out{s}", [P, CH], F32)) for s in range(2)]

        c_ld = sem("att_const_ld")
        fixed = sem("att_fixed")
        masks_ready = sem("att_masks_ready")
        qk_ld = [sem(f"qk_ld{s}") for s in range(4)]
        v_ld = [sem(f"v_ld{s}") for s in range(2)]
        m_ld = [sem(f"m_ld{s}") for s in range(2)]
        rows_full = sem("rows_full")
        rows_read = sem("rows_read")
        neg_done = sem("neg_done")
        s_full = sem("scores_full")
        exp_done = sem("exp_done")
        hi_done = sem("p_hi_done")
        lo_dve = sem("lo_dve")
        lo_pool = sem("lo_pool")
        pv_done = sem("pv_done")
        o_read = sem("o_read")
        o_st = [sem(f"o_st{s}") for s in range(2)]

        n_pool = len(ON_POOL)
        n_dve = NT - n_pool

        def lo_wait(eng, i, k):
            before = i * UNROLL + k // NT
            t = k % NT
            if t in ON_POOL:
                eng.wait_ge(lo_pool, before * n_pool + sum(1 for x in ON_POOL if x <= t))
            else:
                eng.wait_ge(lo_dve, before * n_dve + sum(1 for x in range(t + 1) if x not in ON_POOL))

        def runs(body):
            def go(eng):
                body(0, True, False)
                with eng.Fori(1, ITERS - 1) as i:
                    body(i, False, False)
                body(ITERS - 1, False, True)
            return go

        with nc.Block() as block:
            @block.sync
            def _(sp):
                def load_qk(hh, slot):
                    for stack, part_of, src in ((qs, (0, 0, 1), io["q_s"]), (ks, (0, 1, 0), io["k_s"])):
                        for row, part in enumerate(part_of):
                            sp.dma_start(words(stack[slot][row * DH:(row + 1) * DH, :]),
                                         src[part, bass.ds(hh * DH, DH), :]).then_inc(qk_ld[slot], 16)

                def load_v(pair, slot):
                    sp.dma_start(words(v[slot][:, :, 1:4 * DH + 1]),
                                 io["v_s"][bass.ds(pair, 1)].rearrange("o (b p) c -> p (o b) c", p=P)
                                 ).then_inc(v_ld[slot], 16)

                def load_max(hh, slot):
                    sp.wait_ge(rows_read, NS * hh + NS)
                    sp.dma_start(words(qs[slot][3 * DH:3 * DH + 1, :]), words(neg_row[slot % 2][:, :])).then_inc(m_ld[slot % 2], 16)

                sp.dma_start(consts[:, :], io["consts"][:, P:4 * P]).then_inc(c_ld, 16)
                for hh in range(3):
                    load_qk(hh, hh)
                load_v(0, 0)
                load_max(0, 0)
                load_max(1, 1)

                def store(i, u):
                    hh = UNROLL * i + u - 1
                    slot = (u - 1) % 2
                    sp.wait_ge(o_read, 2 * (hh + 1))
                    off = 1 if slot == 0 else 0
                    for part in range(2):
                        sp.dma_start(io["o_s"][part, bass.ds(hh * DH, DH), :],
                                     o_out[slot][off + part * DH:off + (part + 1) * DH, :]).then_inc(o_st[slot], 16)
                    row = 0 if slot == 0 else 2 * DH
                    sp.dma_start(io["sum_s"][bass.ds(hh, 1), :], o_out[slot][row:row + 1, :]).then_inc(o_st[slot], 16)

                def body(i, first, last):
                    for u in range(UNROLL):
                        hh = UNROLL * i + u
                        if not (last and u > 0):
                            if not (first and u == 0):
                                sp.wait_ge(s_full, NT * hh)
                            load_qk(hh + 3, (u + 3) % 4)
                        if u % 2 == 0 and not (last and u == 2):
                            if not (first and u == 0):
                                sp.wait_ge(pv_done, NT * hh)
                            load_v(2 * i + u // 2 + 1, (u // 2 + 1) % 2)
                        if not (last and u > 1):
                            load_max(hh + 2, (u + 2) % 4)
                        if not (first and u == 0):
                            store(i, u)
                    if last:
                        store(ITERS, 0)

                runs(body)(sp)
                for s in range(2):
                    sp.wait_ge(o_st[s], 48 * HEADS // 2)

            @block.gpsimd
            def _(pool):
                for s in range(4):
                    nc.gpsimd.memset(ks[s][3 * DH:3 * DH + 1, :].bitcast(F32), 1.0).then_inc(fixed, 1)
                pool.wait_ge(fixed, 4)
                for s in range(2):
                    nc.gpsimd.memset(v[s][:, :, 0:1].bitcast(F32), 1.0).then_inc(fixed, 1)
                    nc.gpsimd.memset(v[s][:, :, 4 * DH + 1:].bitcast(F32), 1.0).then_inc(fixed, 1)
                for t in (0, 2):
                    nc.gpsimd.memset(p_hi[t][:, 0:G].bitcast(F32), 0.0).then_inc(fixed, 1)
                    nc.gpsimd.memset(p_lo[t][:, 0:G].bitcast(F32), 0.0).then_inc(fixed, 1)

                def body(i, first, last):
                    for u in range(UNROLL):
                        for t in ON_POOL:
                            k = NT * u + t
                            a, b = USED[t]
                            pool.wait_ge(hi_done, NK * i + k + 1)
                            nc.gpsimd.tensor_tensor(p_lo[t][:, a:b], probs[k % 4][:, a:b],
                                                    p_hi[t][:, a:b].bitcast(F32), ALU.subtract).then_inc(lo_pool, 1)

                runs(body)(pool)

            @block.scalar
            def _(act):
                def body(i, first, last):
                    def high(k):
                        t = k % NT
                        a, b = USED[t]
                        act.wait_ge(exp_done, NK * i + k + 1)
                        if not (first and k < NT):
                            act.wait_ge(pv_done, NK * i + k - NT + 1)
                        nc.scalar.copy(p_hi[t][:, a:b], probs[k % 4][:, a:b]).then_inc(hi_done, 1)

                    def heads_out(k, s):
                        u = k // NT
                        act.wait_ge(pv_done, NK * i + k + 1)
                        if s == 0 and not (first and u < 2):
                            act.wait_ge(o_st[u % 2], 24 * (UNROLL * i + u - u % 2))
                        nc.scalar.copy(o_out[u % 2][:, s * CH:(s + 1) * CH],
                                       ps_o[s][0:2 * DH + 1, :]).then_inc(o_read, 1)

                    for k in range(NK):
                        t = k % NT
                        a, b = USED[t]
                        act.wait_ge(s_full, NK * i + k + 1)
                        if not (first and k < 4):
                            lo_wait(act, i, k - 4)
                        nc.scalar.activation(probs[k % 4][:, a:b], ps_t[k % 2][:, a:b], ACT.Exp,
                                             scale=SCALE).then_inc(exp_done, 1)
                        if not (first and k == 0):
                            high(k - 1)
                        if t == 1 and not (first and k < NT):
                            heads_out(k - NT, 0)
                        if t == 4 and not (first and k < NT):
                            heads_out(k - NT, 1)
                    if last:
                        high(NK - 1)
                        heads_out(NK - 4, 0)
                        heads_out(NK - 1, 1)

                runs(body)(act)

            @block.vector
            def _(dve):
                dve.wait_ge(c_ld, 16)
                nc.vector.tensor_copy(masks[:, :], consts[:, :]).then_inc(masks_ready, 1)

                def row_max(hh, w, r, base):
                    n = ROWS[r][3]
                    dve.wait_ge(rows_full, NS * hh + r + 1)
                    nc.vector.tensor_reduce(neg[w][:, r:r + 1], ps_r[(base + r) % 2][:, 0:n], AX.X, ALU.max,
                                            negate=True).then_inc(rows_read, 1)

                def combine(hh, w):
                    dve.wait_ge(rows_read, NS * hh + NR)
                    nc.vector.tensor_tensor(neg[w][:, 4:8], neg[w][:, 4:8], neg[w][:, 8:12],
                                            ALU.min).then_inc(neg_done, 1)

                def take_row(hh, w, base, first):
                    dve.wait_ge(rows_full, NS * hh + NS)
                    if not first:
                        dve.wait_ge(m_ld[w], 8 * (hh - w))
                    nc.vector.tensor_copy(neg_row[w][:, :], ps_r[(base + NR) % 2][0:8, 0:P]).then_inc(rows_read, 1)

                for hh in range(2):
                    for r in range(NR):
                        row_max(hh, hh, r, NS * hh)
                    combine(hh, hh)
                    take_row(hh, hh, NS * hh, True)

                def body(i, first, last):
                    def low(k):
                        t = k % NT
                        if t in ON_POOL:
                            return
                        a, b = USED[t]
                        dve.wait_ge(hi_done, NK * i + k + 1)
                        nc.vector.tensor_tensor(p_lo[t][:, a:b], probs[k % 4][:, a:b],
                                                p_hi[t][:, a:b].bitcast(F32), ALU.subtract).then_inc(lo_dve, 1)

                    for k in range(NK):
                        u, t = divmod(k, NT)
                        hh = UNROLL * i + u + 2
                        if not (last and u > 1):
                            for r in AT_TILE[t]:
                                row_max(hh, u % 2, r, NS * u)
                            if t == 3:
                                combine(hh, u % 2)
                            if t == 4:
                                take_row(hh, u % 2, NS * u, False)
                        if not (first and k < 2):
                            low(k - 2)
                    if last:
                        low(NK - 2)
                        low(NK - 1)

                runs(body)(dve)

            @block.tensor
            def _(pe):
                pe.wait_ge(masks_ready, 1)
                pe.wait_ge(fixed, 12)

                def rows(hh, slot, r, base, first):
                    blk, k0, n, _, diag = ROWS[r]
                    if not (first and base + r < 2):
                        pe.wait_ge(rows_read, NS * hh + r - 1)
                    out = ps_r[(base + r) % 2]
                    mm = nc.tensor.matmul(out[:, 0:n], qs[slot][0:3 * DH, blk * G:(blk + 1) * G],
                                          ks[slot][0:3 * DH, k0:k0 + n], start=True, stop=diag is None)
                    if diag is not None:
                        mm = nc.tensor.matmul(out[:, diag:diag + G], eye, mask_rows, start=False, stop=True)
                    mm.then_inc(rows_full, 1)

                def turn(hh, w, base):
                    pe.wait_ge(neg_done, hh + 1)
                    pe.wait_ge(rows_read, NS * hh + NR - 1)
                    nc.tensor.transpose(ps_r[(base + NR) % 2][0:8, 0:P], neg[w][:, 0:8], eye_f).then_inc(rows_full, 1)

                for hh in range(2):
                    pe.wait_ge(qk_ld[hh], 96)
                    for r in range(NR):
                        rows(hh, hh, r, NS * hh, hh == 0)
                    turn(hh, hh, NS * hh)

                def body(i, first, last):
                    def scores(k):
                        u, t = divmod(k, NT)
                        if t == 0:
                            pe.wait_ge(m_ld[u % 2], 8 * (UNROLL * i + u - u % 2) + 16)
                        if not (first and k < 2):
                            pe.wait_ge(exp_done, NK * i + k - 1)
                        out = ps_t[k % 2]
                        for col, kb, q0, n, diag in TILES[t]:
                            mm = nc.tensor.matmul(out[:, col:col + n], ks[u][:, kb * G:(kb + 1) * G],
                                                  qs[u][:, q0:q0 + n], start=True, stop=diag is None)
                            if diag is not None:
                                mm = nc.tensor.matmul(out[:, diag:diag + G], eye, mask_cols, start=False, stop=True)
                        mm.then_inc(s_full, 1)

                    def times_v(k):
                        u, t = divmod(k % NK, NT)
                        pair = (u // 2) % 2
                        off = 0 if u % 2 == 0 else 2 * DH + 1
                        lo_wait(pe, i, k)
                        if t == 0 and u % 2 == 0:
                            pe.wait_ge(v_ld[pair], 16 * i + 16)
                        if not (first and k < NT) and t < 2:
                            pe.wait_ge(o_read, 2 * (UNROLL * i + k // NT) - (1 if t == 0 else 0))
                        for e in PV[t]:
                            col, kb, q0, n, _ = TILES[t][e]
                            s = 0 if q0 < S // 2 else 1
                            for part in (p_hi, p_lo):
                                mm = nc.tensor.matmul(ps_o[s][0:2 * DH + 1, q0 - s * CH:q0 - s * CH + n],
                                                      v[pair][:, kb, off:off + 2 * DH + 1], part[t][:, col:col + n],
                                                      start=(t, e) in OPENS and part is p_hi,
                                                      stop=(t, e) in CLOSES and part is p_lo)
                        mm.then_inc(pv_done, 1)

                    for k in range(NK):
                        u, t = divmod(k, NT)
                        scores(k)
                        if not (last and u > 1):
                            hh = UNROLL * i + u + 2
                            if t == 0:
                                pe.wait_ge(qk_ld[(u + 2) % 4], 96 * (i + (1 if u < 2 else 2)))
                            for r in AT_TILE[t]:
                                rows(hh, (u + 2) % 4, r, NS * u, False)
                            if t == 4:
                                turn(hh, u % 2, NS * u)
                        if not (first and k < LAG):
                            times_v(k - LAG)
                    if last:
                        for k in range(NK - LAG, NK):
                            times_v(k)

                runs(body)(pe)


def project_out(nc, sem, io):
    TT = CH // P

    with ExitStack() as ctx:
        sb = lambda name, shape, dt: ctx.enter_context(nc.sbuf_tensor(name, shape, dt))
        wo = sb("wo", [P, KT, 2, D], F32R)
        sums = sb("sums", [P, S * H // P], F32)
        rsum = sb("rsum", [P, S * H // P], F32)
        o_a = [sb(f"o_a{s}", [P, KT, CH], F32) for s in range(2)]
        o_b = [sb(f"o_b{s}", [P, KT, CH], F32) for s in range(2)]
        r_b = [sb(f"r_b{s}", [P, KT, CH], F32) for s in range(2)]
        o_hi = [sb(f"o_hi{s}", [P, KT, CH], F32R) for s in range(2)]
        o_lo = [sb(f"o_lo{s}", [P, KT, CH], F32R) for s in range(2)]
        xn = [sb(f"xn{s}", [P, TT, D], F32) for s in range(2)]
        x1 = [sb(f"x1_{s}", [P, TT, D], F32) for s in range(2)]
        x1t = sb("x1t", [P, KT, 2, CH], F32R)
        stats = sb("stats", [P, TT, 6], F32)
        mv = sb("mv", [P, TT, 2], F32)
        std = sb("std", [P, TT], F32)
        rstd = sb("rstd", [P, TT], F32)
        eps = sb("eps", [P, 1], F32)
        eye = sb("po_eye", [P, P], F32)
        ps_y = [ctx.enter_context(nc.psum_tensor(f"y{s}", [P, D], F32)) for s in range(TT)]
        ps_x = [ctx.enter_context(nc.psum_tensor(f"turned{s}", [P, CH], F32)) for s in range(KT)]

        w_ld = sem("po_w_ld")
        sum_ld = sem("sum_ld")
        rsum_done = sem("rsum_done")
        rsum_st = sem("rsum_st")
        o_ld = [sem(f"o_ld{s}") for s in range(2)]
        x_ld = [sem(f"xn_ld{s}") for s in range(2)]
        joined = sem("o_joined")
        normed = sem("o_normed")
        o_hi_done = sem("o_hi_done")
        o_split = sem("o_split")
        y_full = sem("y_full")
        z_done = sem("z_done")
        rstd_done = sem("po_rstd_done")
        var_done = sem("po_var_done")
        std_done = sem("po_std_done")
        x1_done = sem("x1_done")
        turned = sem("x1_turned")
        t_hi_done = sem("x1t_hi_done")
        t_done = sem("x1t_done")
        x1_st = [sem(f"x1_st{s}") for s in range(2)]
        x1t_st = sem("x1t_st")
        eps_set = sem("po_eps_set")

        with nc.Block() as block:
            @block.sync
            def _(sp):
                def load_sums(b):
                    sp.dma_start(sums[:, :], io["sum_s"][bass.ds(b * H, H), :].rearrange(
                        "h (q w) -> (h q) w", w=S * H // P)).then_inc(sum_ld, 16)
                    sp.wait_ge(rsum_done, b + 1)
                    sp.dma_start(io["rsum_s"][bass.ds(b * H, H), :].rearrange("h (q w) -> (h q) w", w=S * H // P),
                                 rsum[:, :]).then_inc(rsum_st, 16)
                    sp.wait_ge(rsum_st, 16 * b + 16)

                def load(b, u, first):
                    if not first:
                        sp.wait_ge(o_split, 2 * b + u - 1)
                    tok = slice(u * CH, (u + 1) * CH)
                    for part, dst in ((0, o_a), (1, o_b)):
                        sp.dma_start(dst[u][:, :, :],
                                     io["o_s"][part, bass.ds(b * D, D), tok].rearrange("(k p) t -> p k t", p=P)
                                     ).then_inc(o_ld[u], 16)
                    for hl in range(4):
                        src = io["rsum_s"][bass.ds(b * H, H), tok].rearrange("(k hl) t -> hl k t", hl=4)[hl]
                        sp.dma_start(r_b[u][hl * DH:(hl + 1) * DH, :, :],
                                     src.partition_broadcast(DH)).then_inc(o_ld[u], 16)
                    if not first:
                        sp.wait_ge(z_done, TT * (2 * b + u - 1))
                    sp.dma_start(xn[u][:, :, :], io["x"][bass.ds(b * S + u * CH, CH), :].rearrange(
                        "(t p) d -> p t d", p=P)).then_inc(x_ld[u], 16)

                def store_x1(b, u):
                    sp.wait_ge(x1_done, TT * (2 * b + u + 1))
                    sp.dma_start(io["x1_s"][bass.ds(b * S + u * CH, CH), :].rearrange("(t p) d -> p t d", p=P),
                                 x1[u][:, :, :]).then_inc(x1_st[u], 16)

                def store_x1t(c):
                    sp.wait_ge(t_done, KT * (c + 1))
                    sp.dma_start(io["x1t_s"][bass.ds(c, 1)].rearrange("o p n -> p (o n)"),
                                 words(x1t[:, :, :, :].rearrange("p k c t -> p (k c t)"))).then_inc(x1t_st, 16)

                sp.dma_start(eye[:, :], io["consts"][:, P:2 * P]).then_inc(w_ld, 16)
                sp.dma_start(words(wo[:, :, :, :]), io["wo_s"].rearrange("k p c n -> p k c n")).then_inc(w_ld, 16)

                def body(b, first, last):
                    for u in range(2):
                        c = 2 * b + u
                        if u == 0 and not last:
                            load_sums(b + 1)
                        if not (last):
                            load(b + 1, u, False)
                        store_x1(b, u)
                        if not (first and u == 0):
                            store_x1t(c - 1)

                load_sums(0)
                load(0, 0, True)
                load(0, 1, True)
                body(0, True, False)
                with sp.Fori(1, B - 1) as b:
                    body(b, False, False)
                body(B - 1, False, True)
                store_x1t(NCH - 1)
                for s in range(2):
                    sp.wait_ge(x1_st[s], 16 * B)
                sp.wait_ge(x1t_st, 16 * NCH)

            @block.gpsimd
            def _(pool):
                with pool.Fori(0, B) as b:
                    for u in range(2):
                        pool.wait_ge(o_ld[u], 96 * b + 96)
                        nc.gpsimd.tensor_tensor(o_a[u][:, :, :], o_a[u][:, :, :], o_b[u][:, :, :],
                                                ALU.add).then_inc(joined, 1)
                        pool.wait_ge(joined, 2 * b + u + 1)
                        nc.gpsimd.tensor_tensor(o_a[u][:, :, :], o_a[u][:, :, :], r_b[u][:, :, :],
                                                ALU.mult).then_inc(normed, 1)

            @block.scalar
            def _(act):
                def o_high(b, u, first):
                    act.wait_ge(normed, 2 * b + u + 1)
                    if not first:
                        act.wait_ge(y_full, TT * (2 * b + u - 1))
                    nc.scalar.copy(o_hi[u][:, :, :], o_a[u][:, :, :]).then_inc(o_hi_done, 1)

                def x1t_high(c, first):
                    for k in range(KT):
                        act.wait_ge(turned, KT * c + k + 1)
                        if not first and k == 0:
                            act.wait_ge(x1t_st, 16 * c)
                        nc.scalar.copy(x1t[:, k, 0, :], ps_x[k][:, :]).then_inc(t_hi_done, 1)

                def body(b, first, last):
                    for u in range(2):
                        c = 2 * b + u
                        act.wait_ge(var_done, c + 1)
                        nc.scalar.activation(std[:, :], mv[:, :, 1], ACT.Sqrt, bias=eps[:, 0:1]).then_inc(std_done, 1)
                        if not last:
                            o_high(b + 1, u, False)
                        if not (first and u == 0):
                            x1t_high(c - 1, first and u == 1)

                act.wait_ge(eps_set, 1)
                o_high(0, 0, True)
                o_high(0, 1, True)
                body(0, True, False)
                with act.Fori(1, B - 1) as b:
                    body(b, False, False)
                body(B - 1, False, True)
                x1t_high(NCH - 1, False)

            @block.vector
            def _(dve):
                nc.vector.memset(eps[:, :], EPS).then_inc(eps_set, 1)

                def inverse(b):
                    dve.wait_ge(sum_ld, 16 * b + 16)
                    nc.vector.reciprocal(rsum[:, :], sums[:, :]).then_inc(rsum_done, 1)

                def o_low(b, u):
                    dve.wait_ge(o_hi_done, 2 * b + u + 1)
                    nc.vector.tensor_tensor(o_lo[u][:, :, :], o_a[u][:, :, :], o_hi[u][:, :, :].bitcast(F32),
                                            ALU.subtract).then_inc(o_split, 1)

                def x1t_low(c):
                    for k in range(KT):
                        dve.wait_ge(t_hi_done, KT * c + k + 1)
                        nc.vector.tensor_tensor(x1t[:, k, 1, :], ps_x[k][:, :], x1t[:, k, 0, :].bitcast(F32),
                                                ALU.subtract).then_inc(t_done, 1)

                def body(b, first, last):
                    for u in range(2):
                        c = 2 * b + u
                        dve.wait_ge(x_ld[u], 16 * b + 16)
                        if not first:
                            dve.wait_ge(x1_st[u], 16 * b)
                        for t in range(TT):
                            dve.wait_ge(y_full, TT * c + t + 1)
                            nc.vector.tensor_tensor(x1[u][:, t, :], ps_y[t][:, :], xn[u][:, t, :],
                                                    ALU.add).then_inc(z_done, 1)
                            dve.wait_ge(z_done, TT * c + t + 1)
                            nc.vector.bn_stats(stats[:, t, :], x1[u][:, t, :])
                        dve.drain()
                        for t in range(TT):
                            mm = nc.vector.bn_aggr(mv[:, t, :], stats[:, t, :])
                        mm.then_inc(var_done, 1)
                        if u == 0 and not last:
                            inverse(b + 1)
                        if not last:
                            o_low(b + 1, u)
                        dve.wait_ge(std_done, c + 1)
                        nc.vector.reciprocal(rstd[:, :], std[:, :]).then_inc(rstd_done, 1)
                        dve.wait_ge(rstd_done, c + 1)
                        for t in range(TT):
                            nc.vector.tensor_scalar(x1[u][:, t, :], x1[u][:, t, :], mv[:, t, 0:1], rstd[:, t:t + 1],
                                                    ALU.subtract, ALU.mult).then_inc(x1_done, 1)
                        if not (first and u == 0):
                            x1t_low(c - 1)

                inverse(0)
                o_low(0, 0)
                o_low(0, 1)
                body(0, True, False)
                with dve.Fori(1, B - 1) as b:
                    body(b, False, False)
                body(B - 1, False, True)
                x1t_low(NCH - 1)

            @block.tensor
            def _(pe):
                def product(c, u, first):
                    pe.wait_ge(o_split, c + 1)
                    for t in range(TT):
                        if not first:
                            pe.wait_ge(z_done, TT * (c - 1) + t + 1)
                        k = 0
                        for kt in range(KT):
                            for op, wp in PASSES:
                                mm = nc.tensor.matmul(ps_y[t][:, :], (o_hi, o_lo)[op][u][:, kt, t * P:(t + 1) * P],
                                                      wo[:, kt, wp, :], start=(k == 0), stop=(k == 11))
                                k += 1
                        mm.then_inc(y_full, 1)

                def turn(c, u, first):
                    pe.wait_ge(x1_done, TT * (c + 1))
                    for k in range(KT):
                        if not first:
                            pe.wait_ge(t_done, KT * (c - 1) + k + 1)
                        for t in range(TT):
                            mm = nc.tensor.transpose(ps_x[k][:, t * P:(t + 1) * P],
                                                     x1[u][:, t, k * P:(k + 1) * P], eye[:, :])
                        mm.then_inc(turned, 1)

                def body(b, first):
                    for u in range(2):
                        product(2 * b + u, u, first and u == 0)
                        if not (first and u == 0):
                            turn(2 * b + u - 1, 1 - u, first and u == 1)

                pe.wait_ge(w_ld, 32)
                body(0, True)
                with pe.Fori(1, B) as b:
                    body(b, False)
                turn(NCH - 1, 1, False)


def feed_forward(nc, sem, io):
    TT = CH // P
    WR = 4

    with ExitStack() as ctx:
        sb = lambda name, shape, dt: ctx.enter_context(nc.sbuf_tensor(name, shape, dt))
        wug = sb("wug", [P, FT, 2, 2, KT, P], F32R)
        wd = [sb(f"wd{s}", [P, 2, D], F32R) for s in range(WR)]
        xt = [sb(f"ff_xt{s}", [P, KT, 2, CH], F32R) for s in range(2)]
        z = sb("ff_z", [P, TT, D], F32)
        sil = [sb(f"silu{s}", [P, CH], F32) for s in range(2)]
        hid = [sb(f"hidden{s}", [P, CH], F32) for s in range(2)]
        h_hi = [sb(f"h_hi{s}", [P, CH], F32R) for s in range(2)]
        h_lo = [sb(f"h_lo{s}", [P, CH], F32R) for s in range(2)]
        ws = sb("ff_ws", [P, 2 * FT], F32)
        stats = sb("ff_stats", [P, TT, 6], F32)
        mv = sb("ff_mv", [P, TT, 2], F32)
        std = sb("ff_std", [P, TT], F32)
        rstd = sb("ff_rstd", [P, TT], F32)
        eps = sb("ff_eps", [P, 1], F32)
        ps_g = [ctx.enter_context(nc.psum_tensor(f"gate{s}", [P, CH], F32)) for s in range(2)]
        ps_u = [ctx.enter_context(nc.psum_tensor(f"up{s}", [P, CH], F32)) for s in range(2)]
        ps_y = [ctx.enter_context(nc.psum_tensor(f"ff_y{s}", [P, D], F32)) for s in range(TT)]

        wug_ld = [sem(f"wug_ld{s}") for s in range(FT)]
        wd_ld = [sem(f"wd_ld{s}") for s in range(WR)]
        xt_ld = [sem(f"ff_xt_ld{s}") for s in range(2)]
        z_ld = sem("ff_z_ld")
        ws_ld = sem("ff_ws_ld")
        gate_full = sem("gate_full")
        up_full = sem("up_full")
        sil_done = sem("silu_done")
        hid_done = sem("hidden_done")
        hhi_done = sem("h_hi_done")
        h_split = sem("h_split")
        down_done = sem("down_done")
        z_done = sem("ff_z_done")
        rstd_done = sem("ff_rstd_done")
        var_done = sem("ff_var_done")
        std_done = sem("ff_std_done")
        out_done = sem("ff_out_done")
        out_st = sem("out_st")
        eps_set = sem("ff_eps_set")

        with nc.Block() as block:
            @block.sync
            def _(sp):
                sp.dma_start(ws[:, :], io["ws_ug"]).then_inc(ws_ld, 16)

                def load_wug(f):
                    sp.dma_start(words(wug[:, f].rearrange("p g c k n -> p (g c k n)")),
                                 io["wug_s"][f].rearrange("p g c k n -> p (g c k n)")).then_inc(wug_ld[f], 16)

                def load_xt(c, s):
                    sp.dma_start(words(xt[s][:, :, :, :].rearrange("p k c t -> p (k c t)")),
                                 io["x1t_s"][bass.ds(c, 1)].rearrange("o p n -> p (o n)")).then_inc(xt_ld[s], 16)

                def load_wd(f):
                    sp.dma_start(words(wd[f % WR][:, :, :]), io["wd_s"][f]).then_inc(wd_ld[f % WR], 16)

                load_xt(0, 0)
                for f in range(4):
                    load_wug(f)
                    load_wd(f)

                def tail(c, u):
                    sp.wait_ge(out_done, TT * c + TT)
                    sp.dma_start(io["out"][bass.ds(c * CH, CH), :].rearrange("(t p) d -> p t d", p=P),
                                 z[:, :, :]).then_inc(out_st, 16)

                def load_z(c):
                    sp.dma_start(z[:, :, :], io["x1_s"][bass.ds(c * CH, CH), :].rearrange(
                        "(t p) d -> p t d", p=P)).then_inc(z_ld, 16)

                load_z(0)

                def body(i, first, last):
                    for u in range(2):
                        c = 2 * i + u
                        for f in range(FT):
                            if first and u == 0 and f + 4 < FT:
                                load_wug(f + 4)
                            if f == 1 and not (last and u == 1):
                                if not (first and u == 0):
                                    sp.wait_ge(gate_full, FT * c + 1)
                                load_xt(c + 1, 1 - u)
                            if not (last and u == 1 and f + WR >= FT):
                                sp.wait_ge(down_done, FT * c + f + 1)
                                load_wd((f + WR) % FT)
                            if f == 8 and not (first and u == 0):
                                tail(c - 1, u)
                                sp.wait_ge(out_st, 16 * c)
                                load_z(c)

                body(0, True, False)
                with sp.Fori(1, B - 1) as i:
                    body(i, False, False)
                body(B - 1, False, True)
                tail(NCH - 1, 1)
                sp.wait_ge(out_st, 16 * NCH)

            @block.scalar
            def _(act):
                act.wait_ge(ws_ld, 16)
                act.wait_ge(eps_set, 1)

                def body(i, first):
                    for u in range(2):
                        for f in range(FT):
                            c = 2 * i + u
                            n = FT * c + f
                            act.wait_ge(gate_full, n + 1)
                            if not (first and u == 0 and f < 2):
                                act.wait_ge(hid_done, n - 1)
                            nc.scalar.activation(sil[f % 2][:, :], ps_g[f % 2][:, :], ACT.Silu,
                                                 scale=ws[:, FT + f:FT + f + 1]).then_inc(sil_done, 1)
                            act.wait_ge(hid_done, n + 1)
                            if not (first and u == 0 and f < 2):
                                act.wait_ge(down_done, n - 1)
                            nc.scalar.copy(h_hi[f % 2][:, :], hid[f % 2][:, :]).then_inc(hhi_done, 1)
                            if f == 3 and not (first and u == 0):
                                act.wait_ge(var_done, c)
                                nc.scalar.activation(std[:, :], mv[:, :, 1], ACT.Sqrt,
                                                     bias=eps[:, 0:1]).then_inc(std_done, 1)

                body(0, True)
                with act.Fori(1, B) as i:
                    body(i, False)
                act.wait_ge(var_done, NCH)
                nc.scalar.activation(std[:, :], mv[:, :, 1], ACT.Sqrt, bias=eps[:, 0:1]).then_inc(std_done, 1)

            @block.vector
            def _(dve):
                nc.vector.memset(eps[:, :], EPS).then_inc(eps_set, 1)
                dve.wait_ge(ws_ld, 16)

                def sums(c):
                    dve.wait_ge(z_ld, 16 * c)
                    dve.wait_ge(down_done, FT * c)
                    for t in range(TT):
                        nc.vector.tensor_tensor(z[:, t, :], ps_y[t][:, :], z[:, t, :], ALU.add).then_inc(z_done, 1)
                    for t in range(TT):
                        dve.wait_ge(z_done, TT * (c - 1) + t + 1)
                        nc.vector.bn_stats(stats[:, t, :], z[:, t, :])
                    dve.drain()
                    for t in range(TT):
                        mm = nc.vector.bn_aggr(mv[:, t, :], stats[:, t, :])
                    mm.then_inc(var_done, 1)

                def norm(c):
                    dve.wait_ge(std_done, c)
                    nc.vector.reciprocal(rstd[:, :], std[:, :]).then_inc(rstd_done, 1)
                    dve.wait_ge(rstd_done, c)
                    for t in range(TT):
                        nc.vector.tensor_scalar(z[:, t, :], z[:, t, :], mv[:, t, 0:1], rstd[:, t:t + 1],
                                                ALU.subtract, ALU.mult).then_inc(out_done, 1)

                def body(i, first):
                    for u in range(2):
                        c = 2 * i + u
                        for f in range(FT):
                            n = FT * c + f
                            if f == 1 and not (first and u == 0):
                                sums(c)
                            dve.wait_ge(up_full, n + 1)
                            dve.wait_ge(sil_done, n + 1)
                            nc.vector.scalar_tensor_tensor(hid[f % 2][:, :], ps_u[f % 2][:, :], ws[:, f:f + 1],
                                                           sil[f % 2][:, :], ALU.mult, ALU.mult).then_inc(hid_done, 1)
                            dve.wait_ge(hhi_done, n + 1)
                            nc.vector.tensor_tensor(h_lo[f % 2][:, :], hid[f % 2][:, :],
                                                    h_hi[f % 2][:, :].bitcast(F32), ALU.subtract).then_inc(h_split, 1)
                            if f == 4 and not (first and u == 0):
                                norm(c)

                body(0, True)
                with dve.Fori(1, B) as i:
                    body(i, False)
                sums(NCH)
                norm(NCH)

            @block.tensor
            def _(pe):
                def gate_up(i, u, f, first):
                    c = 2 * i + u
                    n = FT * c + f
                    if f == 0:
                        pe.wait_ge(xt_ld[u], 16 * i + 16)
                    if first and u == 0:
                        pe.wait_ge(wug_ld[f], 16)
                    if not (first and u == 0 and f < 2):
                        pe.wait_ge(hid_done, n - 1)
                    for g, (bank, done) in ((1, (ps_g, gate_full)), (0, (ps_u, up_full))):
                        k = 0
                        for kt in range(KT):
                            for wp, xp in PASSES:
                                mm = nc.tensor.matmul(bank[f % 2][:, :], wug[:, f, g, wp, kt, :],
                                                      xt[u][:, kt, xp, :], start=(k == 0), stop=(k == 11))
                                k += 1
                        mm.then_inc(done, 1)

                def down(c, f, first):
                    pe.wait_ge(h_split, FT * c + f + 1)
                    pe.wait_ge(wd_ld[f % WR], 16 * (FT // WR) * c + 16 * (f // WR) + 16)
                    for t in range(TT):
                        if f == 0 and not first:
                            pe.wait_ge(z_done, TT * (c - 1) + t + 1)
                        for k, (hp, wp) in enumerate(PASSES):
                            mm = nc.tensor.matmul(ps_y[t][:, :], (h_hi, h_lo)[hp][f % 2][:, t * P:(t + 1) * P],
                                                  wd[f % WR][:, wp, :], start=(f == 0 and k == 0),
                                                  stop=(f == FT - 1 and k == 2))
                    mm.then_inc(down_done, 1)

                def body(i, first):
                    for u in range(2):
                        c = 2 * i + u
                        for f in range(FT):
                            gate_up(i, u, f, first)
                            if f > 0:
                                down(c, f - 1, first and u == 0)
                            elif not (first and u == 0):
                                down(c - 1, FT - 1, False)

                body(0, True)
                with pe.Fori(1, B) as i:
                    body(i, False)
                down(NCH - 1, FT - 1, False)


_HOST = ["x", "xt", "wqkv", "wout", "wugt", "wdt", "su_ug", "su_dp", "ws_ug", "ws_dp", "consts"]
_SCRATCH = {
    "q_s": [2, B * D, S], "k_s": [2, B * D, S],
    "v_s": [B * 8, S, P],
    "wo_s": [KT, P, 2, D], "wd_s": [FT, P, 2, D], "wug_s": [FT, P, 2, 2, KT, P],
    "x1t_s": [NCH, P, KT * 2 * CH],
    "o_s": [2, B * D, S], "sum_s": [B * H, S], "rsum_s": [B * H, S], "x1_s": [T, D],
}


def build(nc, io):
    for name, shape in _SCRATCH.items():
        io[name] = nc.dram_tensor(name, shape, F32, kind="Internal").ap()
    with ExitStack() as ctx:
        def sem(name):
            return ctx.enter_context(nc.semaphore(name))
        project_qkv(nc, sem, io)
        attend(nc, sem, io)
        project_out(nc, sem, io)
        feed_forward(nc, sem, io)


def constants():
    had = np.ones((1, 1), np.float32)
    while had.shape[0] < P:
        had = np.block([[had, had], [had, -had]])
    eye = np.eye(P, dtype=np.float32)
    later = np.triu(np.ones((P, P), np.float32), 1) * np.float32(MASKED)
    return np.ascontiguousarray(np.concatenate([had, eye, later, later.T], axis=1), dtype=np.float32)


def kernel(**inputs):
    import concourse.bacc as _bacc
    from concourse import mybir as _mybir
    from concourse.bass_utils import run_bass_kernel_spmd as _run

    a = {k: np.asarray(v) for k, v in inputs.items()}
    x = a["L0_attn_x"].reshape(T, D)
    arrays = {
        "x": x,
        "xt": x.T,
        "wqkv": a["L0_attn_w_qkv"],
        "wout": a["L0_attn_w_out"],
        "wugt": np.concatenate([a["L0_ffn_W_up"], a["L0_ffn_W_gate"]], axis=0).T,
        "wdt": a["L0_ffn_W_down"].T,
        "su_ug": a["L0_ffn_SU_ug"].reshape(KT, P).T,
        "su_dp": a["L0_ffn_SU_dp"].reshape(FT, P).T,
        "ws_ug": a["L0_ffn_Wscale_ug"].reshape(2 * FT, P).T,
        "ws_dp": a["L0_ffn_Wscale_dp"],
        "consts": constants(),
    }
    nc = _bacc.Bacc("TRN2", target_bir_lowering=False, num_devices=1)
    fed, io = {}, {}
    for name in _HOST:
        v = np.ascontiguousarray(arrays[name])
        fed[f"in_{name}"] = v
        io[name] = nc.dram_tensor(f"in_{name}", v.shape, _mybir.dt.from_np(v.dtype), kind="ExternalInput").ap()
    io["out"] = nc.dram_tensor("out_0", (T, D), F32, kind="ExternalOutput").ap()
    build(nc, io)
    r = _run(nc, [fed], core_ids=[0])
    return r.results[0]["out_0"].reshape(B, S, D)
```

```python
import numpy as np
import concourse.bass as bass
from concourse import mybir
from contextlib import ExitStack

F32 = mybir.dt.float32
F32R = mybir.dt.float32r
BF16 = mybir.dt.bfloat16
ALU = mybir.AluOpType
ACT = mybir.ActivationFunctionType
AX = mybir.AxisListType

P = 128
B, S, D = 4, 1024, 512
H, DH = 16, 32
T = B * S
INTER = 2048
KT = D // P
FT = INTER // P
CH = 512
NCH = T // CH
EPS = 1e-5
MASKED = -1e30


PASSES = ((0, 0), (0, 1), (1, 0))


def words(ap):
    return ap.bitcast(F32)


def project_qkv(nc, sem, io):
    RING = 6
    QK0 = [("qk", 0, n) for n in range(8)]
    V0 = [("v", 0, n) for n in range(4)]
    QK1 = [("qk", 1, n) for n in range(8)]
    V1 = [("v", 1, n) for n in range(4)]
    UP = [("up", 0, n) for n in range(4)]
    GATE = [("gate", 1, n) for n in range(4)]
    DOWN = [("down", 2, n) for n in range(4)]
    JOBS = QK0 + UP + V0 + QK1[:4] + GATE + QK1[4:] + V1 + DOWN
    NJ = len(JOBS)
    FOLD = ("up", "gate", "down")
    FOLD_AT = {0: 2, 1: 14, 2: 26}
    SPLIT_AT = {1: 5, 0: 24}

    def dmas(job):
        return 2 if job[0] in FOLD else 1

    def stored(i, n):
        slot = n % RING
        each = sum(dmas(JOBS[m]) for m in range(slot, NJ, RING))
        return 16 * (i * each + sum(dmas(JOBS[m]) for m in range(slot, n, RING)))

    STEPS = (4, 8, 17)

    def last_of(kind, u):
        return max(n for n, j in enumerate(JOBS) if j[:2] == (kind, u))

    def folds_before(n):
        return sum(1 for j in JOBS[:n] if j[0] in FOLD)

    with ExitStack() as ctx:
        sb = lambda name, shape, dt: ctx.enter_context(nc.sbuf_tensor(name, shape, dt))
        wqkv = sb("wqkv_split", [P, 2, KT, 3 * D], F32R)
        x_raw = [sb(f"x_raw{s}", [P, KT, CH], F32) for s in range(2)]
        x_hi = [sb(f"x_hi{s}", [P, KT, CH], F32R) for s in range(2)]
        x_lo = [sb(f"x_lo{s}", [P, KT, CH], F32R) for s in range(2)]
        raw = [sb(f"w_raw{s}", [P, 2048], F32) for s in range(3)]
        half = sb("butterfly", [P, 2048], F32)
        rot = sb("rotated", [P, 2048], F32)
        rot_hi = sb("rotated_hi", [P, 2048], F32R)
        rot_lo = sb("rotated_lo", [P, 2048], F32R)
        scaled = [sb(f"scaled{s}", [P, CH], F32) for s in range(2)]
        stage = [sb(f"stage{s}", [P, 2 * CH], F32R) for s in range(RING)]
        had_f = sb("had_f", [P, P], F32)
        had = sb("had", [P, P], F32R)
        su_ug = sb("su_ug", [P, KT], F32)
        su_dp = sb("su_dp", [P, FT], F32)
        ws_dp = sb("ws_dp", [P, D], F32)
        bank = [ctx.enter_context(nc.psum_tensor(f"pj{s}", [P, CH], F32)) for s in range(RING)]

        raw_ld = [sem(f"raw_ld{s}") for s in range(3)]
        x_ld = [sem(f"x_ld{s}") for s in range(2)]
        const_ld = sem("const_ld")
        store_done = [sem(f"store_done{s}") for s in range(RING)]
        wsplit_hi = sem("wsplit_hi")
        wsplit_done = sem("wsplit_done")
        wo_stored = sem("wo_stored")
        had_ready = sem("had_ready")
        x_hi_done = sem("x_hi_done")
        x_split = sem("x_split")
        butter = sem("butter")
        rot_hi_done = sem("rot_hi_done")
        rot_split = sem("rot_split")
        full = sem("pj_full")
        scaled_done = sem("scaled_done")
        hi_done = sem("pj_hi_done")
        evacuated = sem("pj_evacuated")

        ITERS = B
        wqkv_in = io["wqkv"].rearrange("(k p) n -> p k n", p=P)
        wout_in = io["wout"].rearrange("(k p) n -> p k n", p=P)
        xt_in = io["xt"].rearrange("(k p) t -> p k t", p=P)
        wug_in = io["wugt"].rearrange("(k p) f -> p k f", p=P)
        wd_in = io["wdt"].rearrange("(k p) n -> p k n", p=P)

        def as_kt(t, k=KT):
            return t[:, :].rearrange("p (k n) -> p k n", k=k)

        def out_parts(job, n):
            st = stage[n % RING]
            if job[0] == "v":
                v = st[:, :].rearrange("p (h c d) -> p h c d", h=H, c=2)
                return v[:, :, 0, :], v[:, :, 1, :]
            return st[:, 0:CH], st[:, CH:2 * CH]

        def shaped(ap, job):
            return ap.rearrange("p (h d) -> p h d", h=H) if job[0] == "v" else ap

        with nc.Block() as block:
            @block.sync
            def _(sp):
                for s in range(3):
                    sp.dma_start(as_kt(raw[s]), wqkv_in[:, :, s * D:(s + 1) * D]).then_inc(raw_ld[s], 16)
                    if s == 0:
                        sp.dma_start(x_raw[0][:, :, :], xt_in[:, :, 0:CH]).then_inc(x_ld[0], 16)
                sp.dma_start(had_f[:, :], io["consts"][:, 0:P]).then_inc(const_ld, 16)
                sp.dma_start(su_ug[:, :], io["su_ug"]).then_inc(const_ld, 16)
                sp.dma_start(su_dp[:, :], io["su_dp"]).then_inc(const_ld, 16)
                sp.dma_start(ws_dp[:, :], io["ws_dp"].partition_broadcast(P)).then_inc(const_ld, 16)
                sp.dma_start(x_raw[1][:, :, :], xt_in[:, :, CH:2 * CH]).then_inc(x_ld[1], 16)
                sp.wait_ge(wsplit_done, 1)
                sp.dma_start(as_kt(raw[0]), wout_in).then_inc(raw_ld[0], 16)
                sp.wait_ge(wsplit_done, 4)
                for part, t in ((0, rot_hi), (1, rot_lo)):
                    sp.dma_start(io["wo_s"][:, :, part].rearrange("k p n -> p k n"),
                                 words(as_kt(t))).then_inc(wo_stored, 16)
                sp.dma_start(as_kt(raw[0]), wug_in[:, :, 0:CH]).then_inc(raw_ld[0], 16)
                sp.dma_start(as_kt(raw[1]), wug_in[:, :, INTER:INTER + CH]).then_inc(raw_ld[1], 16)
                sp.dma_start(as_kt(raw[2], FT), wd_in[:, :, 0:P]).then_inc(raw_ld[2], 16)

                def body(i, last):
                    for n, job in enumerate(JOBS):
                        kind, u, m = job
                        if not last and kind == "qk" and m == 0:
                            sp.wait_ge(x_split, 2 * i + u + 1)
                            sp.dma_start(x_raw[u][:, :, :],
                                         xt_in[:, :, bass.ds((2 * i + 2 + u) * CH, CH)]).then_inc(x_ld[u], 16)
                        sp.wait_ge(evacuated, NJ * i + n + 1)
                        st = stage[n % RING]
                        done = store_done[n % RING]
                        if kind == "qk":
                            dst = io["q_s"] if m < 4 else io["k_s"]
                            rows = bass.ds(i * D + (m % 4) * P, P)
                            sp.dma_start(dst[:, rows, u * CH:(u + 1) * CH].rearrange("c p t -> p c t"),
                                         words(st[:, :].rearrange("p (c t) -> p c t", c=2))).then_inc(done, 16)
                        elif kind == "v":
                            dst = io["v_s"][bass.ds(i * 8, 8), u * CH + m * P:u * CH + (m + 1) * P, :]
                            sp.dma_start(dst.rearrange("h p c -> p h c"),
                                         words(st[:, :].rearrange("p (h c) -> p h c", h=8))).then_inc(done, 16)
                        else:
                            for part in range(2):
                                src = words(st[:, part * CH:(part + 1) * CH].rearrange("p (f n) -> p f n", f=4))
                                if kind == "down":
                                    dst = io["wd_s"][4 * m:4 * m + 4, :, part, bass.ds(i * P, P)]
                                else:
                                    dst = io["wug_s"][bass.ds(4 * i, 4), :, u, part, m, :]
                                sp.dma_start(dst.rearrange("f p n -> p f n"), src).then_inc(done, 16)
                        if not last and kind in FOLD and m == 3:
                            sp.wait_ge(butter, STEPS[2] * i + STEPS[u])
                            if kind == "down":
                                src = wd_in[:, :, bass.ds((i + 1) * P, P)]
                                sp.dma_start(as_kt(raw[2], FT), src).then_inc(raw_ld[2], 16)
                            else:
                                src = wug_in[:, :, bass.ds(u * INTER + (i + 1) * CH, CH)]
                                sp.dma_start(as_kt(raw[u]), src).then_inc(raw_ld[u], 16)

                with sp.Fori(0, ITERS - 1) as i:
                    body(i, False)
                body(ITERS - 1, True)
                for s in range(RING):
                    sp.wait_ge(store_done[s], stored(ITERS, s))
                sp.wait_ge(wo_stored, 32)

            @block.gpsimd
            def _(pool):
                pool.wait_ge(wo_stored, 32)
                pool.wait_ge(const_ld, 64)

                def step(i, k, op, out, a, b):
                    nc.gpsimd.tensor_tensor(out, a, b, op).then_inc(butter, 1)
                    pool.wait_ge(butter, STEPS[2] * i + k + 1)

                with pool.Fori(0, ITERS) as i:
                    k = 0
                    for u, kind in enumerate(FOLD):
                        pool.wait_ge(raw_ld[u], 16 * i + (48 if u == 0 else 32))
                        if kind == "down":
                            cols = as_kt(raw[2], FT)
                            scale = ws_dp[:, bass.ds(i * P, P)].unsqueeze(1).to_broadcast([P, FT, P])
                            step(i, k, ALU.mult, cols, cols, scale)
                            k += 1
                        stages = 4 if kind == "down" else 2
                        src = raw[u]
                        for st in range(stages):
                            dst = rot if st == stages - 1 else (half, raw[u])[st % 2]
                            near = (2048 >> stages) << st
                            a = src[:, :].rearrange("p (g two w) -> p g two w", two=2, w=near)
                            o = dst[:, :].rearrange("p (g two w) -> p g two w", two=2, w=near)
                            for op, col in ((ALU.add, 0), (ALU.subtract, 1)):
                                step(i, k, op, o[:, :, col, :], a[:, :, 0, :], a[:, :, 1, :])
                                k += 1
                            src = dst
                        assert k == STEPS[u]
                        pool.wait_ge(rot_hi_done, 3 * i + u + 1)
                        nc.gpsimd.tensor_tensor(rot_lo[:, :], rot[:, :], rot_hi[:, :].bitcast(F32),
                                                ALU.subtract).then_inc(rot_split, 1)
                        pool.wait_ge(rot_split, 3 * i + u + 1)

            @block.scalar
            def _(act):
                for s in range(3):
                    act.wait_ge(raw_ld[s], 16)
                    nc.scalar.copy(wqkv[:, 0, :, s * D:(s + 1) * D], as_kt(raw[s])).then_inc(wsplit_hi, 1)
                    if s == 0:
                        act.wait_ge(x_ld[0], 16)
                        nc.scalar.copy(x_hi[0][:, :, :], x_raw[0][:, :, :]).then_inc(x_hi_done, 1)
                act.wait_ge(raw_ld[0], 32)
                nc.scalar.copy(rot_hi[:, :], raw[0][:, :]).then_inc(wsplit_hi, 1)

                def body(i, first, last):
                    for n, job in enumerate(JOBS):
                        kind, u, m = job
                        if not (first and n < RING):
                            act.wait_ge(store_done[n % RING], stored(i, n))
                        hi, _lo = out_parts(job, n)
                        if kind in FOLD:
                            k = folds_before(n)
                            act.wait_ge(scaled_done, 12 * i + k + 1)
                            nc.scalar.copy(hi, scaled[k % 2][:, :]).then_inc(hi_done, 1)
                        else:
                            act.wait_ge(full, NJ * i + n + 1)
                            nc.scalar.copy(hi, shaped(bank[n % RING][:, :], job)).then_inc(hi_done, 1)
                        for t, at in FOLD_AT.items():
                            if n == at:
                                act.wait_ge(butter, STEPS[2] * i + STEPS[t])
                                if not (first and t == 0):
                                    act.wait_ge(full, NJ * i + (last_of(FOLD[t - 1], t - 1) + 1 if t else 0))
                                nc.scalar.copy(rot_hi[:, :], rot[:, :]).then_inc(rot_hi_done, 1)
                        if n == SPLIT_AT[1]:
                            act.wait_ge(x_ld[1], 16 * i + 16)
                            nc.scalar.copy(x_hi[1][:, :, :], x_raw[1][:, :, :]).then_inc(x_hi_done, 1)
                        if n == SPLIT_AT[0] and not last:
                            act.wait_ge(x_ld[0], 16 * i + 32)
                            act.wait_ge(full, NJ * i + last_of("v", 0) + 1)
                            nc.scalar.copy(x_hi[0][:, :, :], x_raw[0][:, :, :]).then_inc(x_hi_done, 1)

                body(0, True, False)
                with act.Fori(1, ITERS - 1) as i:
                    body(i, False, False)
                body(ITERS - 1, False, True)

            @block.vector
            def _(dve):
                for s in range(3):
                    dve.wait_ge(wsplit_hi, s + 1)
                    nc.vector.tensor_tensor(wqkv[:, 1, :, s * D:(s + 1) * D], as_kt(raw[s]),
                                            wqkv[:, 0, :, s * D:(s + 1) * D].bitcast(F32),
                                            ALU.subtract).then_inc(wsplit_done, 1)
                    if s == 0:
                        dve.wait_ge(x_hi_done, 1)
                        nc.vector.tensor_tensor(x_lo[0][:, :, :], x_raw[0][:, :, :],
                                                x_hi[0][:, :, :].bitcast(F32), ALU.subtract).then_inc(x_split, 1)
                        dve.wait_ge(const_ld, 64)
                        nc.vector.tensor_copy(had[:, :], had_f[:, :]).then_inc(had_ready, 1)
                        nc.vector.tensor_scalar(su_ug[:, :], su_ug[:, :], float(D) ** -0.5, None,
                                                ALU.mult).then_inc(had_ready, 1)
                        nc.vector.tensor_scalar(su_dp[:, :], su_dp[:, :], float(INTER) ** -0.5, None,
                                                ALU.mult).then_inc(had_ready, 1)
                dve.wait_ge(had_ready, 3)
                dve.wait_ge(wsplit_hi, 4)
                nc.vector.tensor_tensor(rot_lo[:, :], raw[0][:, :], rot_hi[:, :].bitcast(F32),
                                        ALU.subtract).then_inc(wsplit_done, 1)

                def body(i, last):
                    for n, job in enumerate(JOBS):
                        kind, u, m = job
                        hi, lo = out_parts(job, n)
                        src = shaped(bank[n % RING][:, :], job)
                        if kind in FOLD:
                            k = folds_before(n)
                            dve.wait_ge(full, NJ * i + n + 1)
                            if kind == "down":
                                by = su_dp[:, 4 * m:4 * m + 4].unsqueeze(2).to_broadcast([P, 4, P])
                                nc.vector.tensor_tensor(as_kt(scaled[k % 2]), as_kt(bank[n % RING]), by,
                                                        ALU.mult).then_inc(scaled_done, 1)
                            else:
                                nc.vector.tensor_scalar(scaled[k % 2][:, :], src, su_ug[:, m:m + 1], None,
                                                        ALU.mult).then_inc(scaled_done, 1)
                            src = scaled[k % 2][:, :]
                        dve.wait_ge(hi_done, NJ * i + n + 1)
                        nc.vector.tensor_tensor(lo, src, hi.bitcast(F32), ALU.subtract).then_inc(evacuated, 1)
                        if n == SPLIT_AT[1]:
                            dve.wait_ge(x_hi_done, 2 * i + 2)
                            nc.vector.tensor_tensor(x_lo[1][:, :, :], x_raw[1][:, :, :],
                                                    x_hi[1][:, :, :].bitcast(F32), ALU.subtract).then_inc(x_split, 1)
                        if n == SPLIT_AT[0] and not last:
                            dve.wait_ge(x_hi_done, 2 * i + 3)
                            nc.vector.tensor_tensor(x_lo[0][:, :, :], x_raw[0][:, :, :],
                                                    x_hi[0][:, :, :].bitcast(F32), ALU.subtract).then_inc(x_split, 1)

                with dve.Fori(0, ITERS - 1) as i:
                    body(i, False)
                body(ITERS - 1, True)

            @block.tensor
            def _(pe):
                pe.wait_ge(had_ready, 1)

                def body(i, first):
                    for n, job in enumerate(JOBS):
                        kind, u, m = job
                        if not first:
                            pe.wait_ge(evacuated, NJ * i + n - RING + 1)
                        elif n >= RING:
                            pe.wait_ge(evacuated, n - RING + 1)
                        out = bank[n % RING][:, :]
                        if kind == "qk" and m == 0:
                            pe.wait_ge(x_split, 2 * i + u + 1)
                        if first and u == 0 and kind in ("qk", "v") and m in (0, 4):
                            pe.wait_ge(wsplit_done, 1 if m == 0 else 2)
                        if first and u == 0 and kind == "v" and m == 0:
                            pe.wait_ge(wsplit_done, 3)
                        if kind in FOLD and m == 0:
                            pe.wait_ge(rot_split, 3 * i + u + 1)
                        xs = (x_hi[u], x_lo[u]) if kind in ("qk", "v") else None
                        k = 0
                        if kind == "qk":
                            for kt in range(KT):
                                for wp, xp in PASSES:
                                    mm = nc.tensor.matmul(out, wqkv[:, wp, kt, m * P:(m + 1) * P],
                                                          xs[xp][:, kt, :], start=(k == 0), stop=(k == 11))
                                    k += 1
                        elif kind == "v":
                            for kt in range(KT):
                                for xp, wp in PASSES:
                                    mm = nc.tensor.matmul(out, xs[xp][:, kt, m * P:(m + 1) * P],
                                                          wqkv[:, wp, kt, 2 * D:3 * D], start=(k == 0), stop=(k == 11))
                                    k += 1
                        else:
                            for t, part in enumerate((rot_hi, rot_lo)):
                                mm = nc.tensor.matmul(out, had[:, :], part[:, m * CH:(m + 1) * CH],
                                                      start=(t == 0), stop=(t == 1))
                        mm.then_inc(full, 1)
                body(0, True)
                with pe.Fori(1, ITERS) as i:
                    body(i, False)


def attend(nc, sem, io):
    HEADS = B * H
    UNROLL = 4
    ITERS = HEADS // UNROLL
    NT = 5
    NK = NT * UNROLL
    LAG = 6
    HIGH_LAG = 1
    LOW_LAG = 2
    NP = 10
    PR = 2 * NT
    ON_POOL = (0, 1, 2, 3)
    HIGH_ON_DVE = ()
    SCALE = float(1.0 / np.sqrt(np.float32(DH)))
    G = P

    TILES = (
        ((0, 3, 256, 256, 128), (256, 2, 256, 256, 256), (512, 0, 0, 512, 512)),
        ((0, 3, 512, 512, None), (512, 1, 128, 384, 512)),
        ((0, 7, 768, 256, 128), (256, 6, 768, 256, 256), (512, 4, 512, 512, 512)),
        ((0, 0, 512, 512, None), (512, 5, 640, 384, 512)),
        ((0, 1, 512, 512, None), (512, 2, 512, 512, None)),
    )
    USED = ((G, 1024), (0, 896), (G, 1024), (0, 896), (0, 1024))
    PV = ((2, 1, 0), (0, 1), (2, 1, 0), (0, 1), (0, 1))
    OPENS = {(0, 2), (1, 0)}
    CLOSES = {(1, 1), (4, 1)}

    ROWS = ((0, 0, 256, 128, 0), (1, 0, 256, 256, 128), (2, 0, 384, 384, 256), (3, 0, 512, 512, 384),
            (4, 0, 384, 384, None), (5, 0, 384, 384, None), (6, 0, 512, 512, None), (7, 0, 512, 512, None),
            (4, 384, 256, 256, 128), (5, 384, 384, 384, 256), (6, 512, 384, 384, 256), (7, 512, 512, 512, 384))
    NR = len(ROWS)
    NS = NR + 1
    AT_TILE = ((0, 1, 2), (3, 4, 5), (6, 7, 8), (9, 10, 11), ())

    with ExitStack() as ctx:
        sb = lambda name, shape, dt: ctx.enter_context(nc.sbuf_tensor(name, shape, dt))
        qs = [sb(f"q_stack{s}", [3 * DH + 1, S], F32R) for s in range(4)]
        ks = [sb(f"k_stack{s}", [3 * DH + 1, S], F32R) for s in range(4)]
        v = [sb(f"v_pair{s}", [P, 8, 4 * DH + 2], F32R) for s in range(2)]
        probs = [sb(f"probs{s}", [P, 2 * CH], F32) for s in range(NP)]
        p_hi = [sb(f"p_hi{s}", [P, 2 * CH], F32R) for s in range(PR)]
        p_lo = [sb(f"p_lo{s}", [P, 2 * CH], F32R) for s in range(PR)]
        o_out = [sb(f"o_out{s}", [2 * DH + 1, S], F32) for s in range(2)]
        neg = [sb(f"neg_max{s}", [P, 12], F32) for s in range(2)]
        neg_row = [sb(f"neg_row{s}", [8, P], F32R) for s in range(2)]
        consts = sb("att_consts", [P, 3 * P], F32)
        masks = sb("att_masks", [P, 3 * P], BF16)
        eye, mask_rows, mask_cols = (masks[:, t * P:(t + 1) * P] for t in range(3))
        eye_f = consts[:, 0:P]
        ps_t = [ctx.enter_context(nc.psum_tensor(f"scores{s}", [P, 2 * CH], F32)) for s in range(2)]
        ps_r = [ctx.enter_context(nc.psum_tensor(f"rows{s}", [P, CH], F32)) for s in range(2)]
        ps_o = [ctx.enter_context(nc.psum_tensor(f"heads_out{s}", [P, CH], F32)) for s in range(2)]

        c_ld = sem("att_const_ld")
        fixed = sem("att_fixed")
        masks_ready = sem("att_masks_ready")
        qk_ld = [sem(f"qk_ld{s}") for s in range(4)]
        v_ld = [sem(f"v_ld{s}") for s in range(2)]
        m_ld = [sem(f"m_ld{s}") for s in range(2)]
        rows_full = sem("rows_full")
        rows_read = sem("rows_read")
        neg_done = sem("neg_done")
        s_full = sem("scores_full")
        exp_done = sem("exp_done")
        hi_act = sem("p_hi_act")
        hi_dve = sem("p_hi_dve")
        lo_dve = sem("lo_dve")
        lo_pool = sem("lo_pool")
        pv_done = sem("pv_done")
        o_read = sem("o_read")
        o_st = [sem(f"o_st{s}") for s in range(2)]

        n_pool = len(ON_POOL)
        n_dve = NT - n_pool

        def lo_wait(eng, i, k):
            before = i * UNROLL + k // NT
            t = k % NT
            if t in ON_POOL:
                eng.wait_ge(lo_pool, before * n_pool + sum(1 for x in ON_POOL if x <= t))
            else:
                eng.wait_ge(lo_dve, before * n_dve + sum(1 for x in range(t + 1) if x not in ON_POOL))

        def high_wait(eng, i, k):
            t = k % NT
            if t in HIGH_ON_DVE:
                eng.wait_ge(hi_dve, (i * UNROLL + k // NT) * len(HIGH_ON_DVE) + HIGH_ON_DVE.index(t) + 1)
            else:
                before = sum(1 for x in range(t + 1) if x not in HIGH_ON_DVE)
                eng.wait_ge(hi_act, (i * UNROLL + k // NT) * (NT - len(HIGH_ON_DVE)) + before)

        def runs(body):
            def go(eng):
                body(0, True, False)
                with eng.Fori(1, ITERS - 1) as i:
                    body(i, False, False)
                body(ITERS - 1, False, True)
            return go

        with nc.Block() as block:
            @block.sync
            def _(sp):
                def load_qk(hh, slot):
                    for stack, part_of, src in ((qs, (0, 0, 1), io["q_s"]), (ks, (0, 1, 0), io["k_s"])):
                        for row, part in enumerate(part_of):
                            sp.dma_start(words(stack[slot][row * DH:(row + 1) * DH, :]),
                                         src[part, bass.ds(hh * DH, DH), :]).then_inc(qk_ld[slot], 16)

                def load_v(pair, slot):
                    sp.dma_start(words(v[slot][:, :, 1:4 * DH + 1]),
                                 io["v_s"][bass.ds(pair, 1)].rearrange("o (b p) c -> p (o b) c", p=P)
                                 ).then_inc(v_ld[slot], 16)

                def load_max(hh, slot):
                    sp.wait_ge(rows_read, NS * hh + NS)
                    sp.dma_start(words(qs[slot][3 * DH:3 * DH + 1, :]), words(neg_row[slot % 2][:, :])).then_inc(m_ld[slot % 2], 16)

                sp.dma_start(consts[:, :], io["consts"][:, P:4 * P]).then_inc(c_ld, 16)
                for hh in range(3):
                    load_qk(hh, hh)
                load_v(0, 0)
                load_max(0, 0)
                load_max(1, 1)

                def store(i, u):
                    hh = UNROLL * i + u
                    slot = u % 2
                    sp.wait_ge(o_read, 2 * (hh + 1))
                    off = 1 if slot == 0 else 0
                    for part in range(2):
                        sp.dma_start(io["o_s"][part, bass.ds(hh * DH, DH), :],
                                     o_out[slot][off + part * DH:off + (part + 1) * DH, :]).then_inc(o_st[slot], 16)
                    row = 0 if slot == 0 else 2 * DH
                    sp.dma_start(io["sum_s"][bass.ds(hh, 1), :], o_out[slot][row:row + 1, :]).then_inc(o_st[slot], 16)

                def body(i, first, last):
                    for u in range(UNROLL):
                        hh = UNROLL * i + u
                        if not (last and u > 0):
                            if not (first and u == 0):
                                sp.wait_ge(s_full, NT * hh)
                            load_qk(hh + 3, (u + 3) % 4)
                        if not (first and u < 2):
                            store(i, u - 2)
                        if u % 2 == 1 and not (last and u == 3):
                            if not (first and u == 1):
                                sp.wait_ge(pv_done, NT * (hh - 1))
                            load_v(2 * i + u // 2 + 1, (u // 2 + 1) % 2)
                        if not (last and u > 1):
                            load_max(hh + 2, (u + 2) % 4)
                    if last:
                        store(i, UNROLL - 2)
                        store(i, UNROLL - 1)

                runs(body)(sp)
                for s in range(2):
                    sp.wait_ge(o_st[s], 48 * HEADS // 2)

            @block.gpsimd
            def _(pool):
                for s in range(4):
                    nc.gpsimd.memset(ks[s][3 * DH:3 * DH + 1, :].bitcast(F32), 1.0).then_inc(fixed, 1)
                pool.wait_ge(fixed, 4)
                for s in range(2):
                    nc.gpsimd.memset(v[s][:, :, 0:1].bitcast(F32), 1.0).then_inc(fixed, 1)
                    nc.gpsimd.memset(v[s][:, :, 4 * DH + 1:].bitcast(F32), 1.0).then_inc(fixed, 1)
                for t in (0, 2, NT, NT + 2):
                    nc.gpsimd.memset(p_hi[t][:, 0:G].bitcast(F32), 0.0).then_inc(fixed, 1)
                    nc.gpsimd.memset(p_lo[t][:, 0:G].bitcast(F32), 0.0).then_inc(fixed, 1)

                def body(i, first, last):
                    for u in range(UNROLL):
                        for t in ON_POOL:
                            k = NT * u + t
                            a, b = USED[t]
                            high_wait(pool, i, k)
                            nc.gpsimd.tensor_tensor(p_lo[k % PR][:, a:b], probs[k % NP][:, a:b],
                                                    p_hi[k % PR][:, a:b].bitcast(F32), ALU.subtract).then_inc(lo_pool, 1)

                runs(body)(pool)

            @block.scalar
            def _(act):
                def body(i, first, last):
                    def high(k):
                        t = k % NT
                        if t in HIGH_ON_DVE:
                            return
                        a, b = USED[t]
                        act.wait_ge(exp_done, NK * i + k + 1)
                        if not (first and k < PR):
                            act.wait_ge(pv_done, NK * i + k - PR + 1)
                        nc.scalar.copy(p_hi[k % PR][:, a:b], probs[k % NP][:, a:b]).then_inc(hi_act, 1)

                    def heads_out(k, s):
                        u = k // NT
                        act.wait_ge(pv_done, NK * i + k + 1)
                        if s == 0 and not (first and u < 2):
                            act.wait_ge(o_st[u % 2], 24 * (UNROLL * i + u - u % 2))
                        nc.scalar.copy(o_out[u % 2][:, s * CH:(s + 1) * CH],
                                       ps_o[s][0:2 * DH + 1, :]).then_inc(o_read, 1)

                    for k in range(NK):
                        t = k % NT
                        a, b = USED[t]
                        act.wait_ge(s_full, NK * i + k + 1)
                        if not (first and k < NP):
                            lo_wait(act, i, k - NP)
                        nc.scalar.activation(probs[k % NP][:, a:b], ps_t[k % 2][:, a:b], ACT.Exp,
                                             scale=SCALE).then_inc(exp_done, 1)
                        if not (first and k < HIGH_LAG):
                            high(k - HIGH_LAG)
                        done = k - LAG - 1
                        if not (first and done < 0):
                            if done % NT == 1:
                                heads_out(done, 0)
                            if done % NT == NT - 1:
                                heads_out(done, 1)
                    if last:
                        for k in range(NK - HIGH_LAG, NK):
                            high(k)
                        for k in range(NK - LAG - 1, NK):
                            if k % NT == 1:
                                heads_out(k, 0)
                            if k % NT == NT - 1:
                                heads_out(k, 1)

                runs(body)(act)

            @block.vector
            def _(dve):
                dve.wait_ge(c_ld, 16)
                nc.vector.tensor_copy(masks[:, :], consts[:, :]).then_inc(masks_ready, 1)

                def row_max(hh, w, r, base):
                    n = ROWS[r][3]
                    dve.wait_ge(rows_full, NS * hh + r + 1)
                    nc.vector.tensor_reduce(neg[w][:, r:r + 1], ps_r[(base + r) % 2][:, 0:n], AX.X, ALU.max,
                                            negate=True).then_inc(rows_read, 1)

                def combine(hh, w):
                    dve.wait_ge(rows_read, NS * hh + NR)
                    nc.vector.tensor_tensor(neg[w][:, 4:8], neg[w][:, 4:8], neg[w][:, 8:12],
                                            ALU.min).then_inc(neg_done, 1)

                def take_row(hh, w, base, first):
                    dve.wait_ge(rows_full, NS * hh + NS)
                    if not first:
                        dve.wait_ge(m_ld[w], 8 * (hh - w))
                    nc.vector.tensor_copy(neg_row[w][:, :], ps_r[(base + NR) % 2][0:8, 0:P]).then_inc(rows_read, 1)

                for hh in range(2):
                    for r in range(NR):
                        row_max(hh, hh, r, NS * hh)
                    combine(hh, hh)
                    take_row(hh, hh, NS * hh, True)

                def body(i, first, last):
                    def low(k):
                        t = k % NT
                        if t in ON_POOL:
                            return
                        a, b = USED[t]
                        if t in HIGH_ON_DVE:
                            dve.wait_ge(exp_done, NK * i + k + 1)
                            if not (first and k < PR):
                                dve.wait_ge(pv_done, NK * i + k - PR + 1)
                            nc.vector.tensor_copy(p_hi[k % PR][:, a:b], probs[k % NP][:, a:b]).then_inc(hi_dve, 1)
                        high_wait(dve, i, k)
                        nc.vector.tensor_tensor(p_lo[k % PR][:, a:b], probs[k % NP][:, a:b],
                                                p_hi[k % PR][:, a:b].bitcast(F32), ALU.subtract).then_inc(lo_dve, 1)

                    for k in range(NK):
                        u, t = divmod(k, NT)
                        hh = UNROLL * i + u + 2
                        if not (last and u > 1):
                            for r in AT_TILE[t][:2]:
                                row_max(hh, u % 2, r, NS * u)
                        if not (first and k < LOW_LAG):
                            low(k - LOW_LAG)
                        if not (last and u > 1):
                            for r in AT_TILE[t][2:]:
                                row_max(hh, u % 2, r, NS * u)
                            if t == 3:
                                combine(hh, u % 2)
                            if t == 4:
                                take_row(hh, u % 2, NS * u, False)
                    if last:
                        for k in range(NK - LOW_LAG, NK):
                            low(k)

                runs(body)(dve)

            @block.tensor
            def _(pe):
                pe.wait_ge(masks_ready, 1)
                pe.wait_ge(fixed, 16)

                def rows(hh, slot, r, base, first):
                    blk, k0, n, _, diag = ROWS[r]
                    if not (first and base + r < 2):
                        pe.wait_ge(rows_read, NS * hh + r - 1)
                    out = ps_r[(base + r) % 2]
                    mm = nc.tensor.matmul(out[:, 0:n], qs[slot][0:3 * DH, blk * G:(blk + 1) * G],
                                          ks[slot][0:3 * DH, k0:k0 + n], start=True, stop=diag is None)
                    if diag is not None:
                        mm = nc.tensor.matmul(out[:, diag:diag + G], eye, mask_rows, start=False, stop=True)
                    mm.then_inc(rows_full, 1)

                def turn(hh, w, base):
                    pe.wait_ge(neg_done, hh + 1)
                    pe.wait_ge(rows_read, NS * hh + NR - 1)
                    nc.tensor.transpose(ps_r[(base + NR) % 2][0:8, 0:P], neg[w][:, 0:8], eye_f).then_inc(rows_full, 1)

                for hh in range(2):
                    pe.wait_ge(qk_ld[hh], 96)
                    for r in range(NR):
                        rows(hh, hh, r, NS * hh, hh == 0)
                    turn(hh, hh, NS * hh)

                def body(i, first, last):
                    def scores(k):
                        u, t = divmod(k, NT)
                        if t == 0:
                            pe.wait_ge(m_ld[u % 2], 8 * (UNROLL * i + u - u % 2) + 16)
                        if not (first and k < 2):
                            pe.wait_ge(exp_done, NK * i + k - 1)
                        out = ps_t[k % 2]
                        for col, kb, q0, n, diag in TILES[t]:
                            mm = nc.tensor.matmul(out[:, col:col + n], ks[u][:, kb * G:(kb + 1) * G],
                                                  qs[u][:, q0:q0 + n], start=True, stop=diag is None)
                            if diag is not None:
                                mm = nc.tensor.matmul(out[:, diag:diag + G], eye, mask_cols, start=False, stop=True)
                        mm.then_inc(s_full, 1)

                    def times_v(k, entries):
                        u, t = divmod(k % NK, NT)
                        pair = (u // 2) % 2
                        off = 0 if u % 2 == 0 else 2 * DH + 1
                        if entries == "first":
                            lo_wait(pe, i, k)
                        if entries == "first" and t == 0 and u % 2 == 0:
                            pe.wait_ge(v_ld[pair], 16 * i + 16)
                        if entries == "first" and not (first and k < NT) and t < 2:
                            pe.wait_ge(o_read, 2 * (UNROLL * i + k // NT) - (1 if t == 0 else 0))
                        for e in PV[t][:1] if entries == "first" else PV[t][1:]:
                            col, kb, q0, n, _ = TILES[t][e]
                            s = 0 if q0 < S // 2 else 1
                            for part in (p_hi, p_lo):
                                mm = nc.tensor.matmul(ps_o[s][0:2 * DH + 1, q0 - s * CH:q0 - s * CH + n],
                                                      v[pair][:, kb, off:off + 2 * DH + 1], part[k % PR][:, col:col + n],
                                                      start=(t, e) in OPENS and part is p_hi,
                                                      stop=(t, e) in CLOSES and part is p_lo)
                        if entries == "rest":
                            mm.then_inc(pv_done, 1)

                    for k in range(NK):
                        u, t = divmod(k, NT)
                        hh = UNROLL * i + u + 2
                        more = not (last and u > 1)
                        back = not (first and k < LAG)

                        def row(n):
                            if more and n < len(AT_TILE[t]):
                                rows(hh, (u + 2) % 4, AT_TILE[t][n], NS * u, False)

                        if more and t == 0:
                            pe.wait_ge(qk_ld[(u + 2) % 4], 96 * (i + (1 if u < 2 else 2)))
                        row(0)
                        scores(k)
                        row(1)
                        if back:
                            times_v(k - LAG, "first")
                        row(2)
                        if more and t == 4:
                            turn(hh, u % 2, NS * u)
                        if back:
                            times_v(k - LAG, "rest")
                    if last:
                        for k in range(NK - LAG, NK):
                            times_v(k, "first")
                            times_v(k, "rest")

                runs(body)(pe)


def project_out(nc, sem, io):
    W = CH // 2
    U = S // W
    TT = W // P
    NC = B * U
    AHEAD = 3

    with ExitStack() as ctx:
        sb = lambda name, shape, dt: ctx.enter_context(nc.sbuf_tensor(name, shape, dt))
        wo = sb("wo", [P, KT, 2, D], F32R)
        sums = sb("sums", [P, T * H // P], F32)
        rsum = sb("rsum", [P, T * H // P], F32)
        o_a = [sb(f"o_a{s}", [P, KT, W], F32) for s in range(U)]
        o_b = [sb(f"o_b{s}", [P, KT, W], F32) for s in range(U)]
        r_b = [sb(f"r_b{s}", [P, KT, W], F32) for s in range(U)]
        o_hi = [sb(f"o_hi{s}", [P, KT, W], F32R) for s in range(2)]
        o_lo = [sb(f"o_lo{s}", [P, KT, W], F32R) for s in range(2)]
        xn = [sb(f"xn{s}", [P, TT, D], F32) for s in range(U)]
        x1 = [sb(f"x1_{s}", [P, TT, D], F32) for s in range(U)]
        x1t = [sb(f"x1t{s}", [P, KT, W], F32) for s in range(2)]
        stats = sb("stats", [P, TT, 6], F32)
        mv = sb("mv", [P, TT, 2], F32)
        std = sb("std", [P, TT], F32)
        rstd = sb("rstd", [P, TT], F32)
        eps = sb("eps", [P, 1], F32)
        eye = sb("po_eye", [P, P], F32)
        ps_y = [[ctx.enter_context(nc.psum_tensor(f"y{s}_{t}", [P, D], F32)) for t in range(TT)] for s in range(2)]
        ps_x = [[ctx.enter_context(nc.psum_tensor(f"turned{s}_{j}", [P, 2, W], F32)) for j in range(KT // 2)]
                for s in range(2)]

        w_ld = sem("po_w_ld")
        sum_ld = sem("sum_ld")
        rsum_done = sem("rsum_done")
        rsum_st = sem("rsum_st")
        o_ld = [sem(f"o_ld{s}") for s in range(U)]
        x_ld = [sem(f"xn_ld{s}") for s in range(U)]
        joined = sem("o_joined")
        normed = sem("o_normed")
        o_hi_done = sem("o_hi_done")
        o_split = sem("o_split")
        y_full = sem("y_full")
        z_done = sem("z_done")
        rstd_done = sem("po_rstd_done")
        var_done = sem("po_var_done")
        std_done = sem("po_std_done")
        x1_done = sem("x1_done")
        turned = sem("x1_turned")
        t_done = sem("x1t_done")
        x1_st = [sem(f"x1_st{s}") for s in range(U)]
        x1t_st = [sem(f"x1t_st{s}") for s in range(2)]
        eps_set = sem("po_eps_set")

        with nc.Block() as block:
            @block.sync
            def _(sp):
                def load(b, u, first):
                    c = U * b + u
                    tok = slice(u * W, (u + 1) * W)
                    if not first:
                        sp.wait_ge(o_split, c - U + 1)
                    for part, dst in ((0, o_a), (1, o_b)):
                        sp.dma_start(dst[u][:, :, :],
                                     io["o_s"][part, bass.ds(b * D, D), tok].rearrange("(k p) t -> p k t", p=P)
                                     ).then_inc(o_ld[u], 16)
                    if not first:
                        sp.wait_ge(z_done, TT * (c - U + 1))
                    sp.dma_start(xn[u][:, :, :], io["x"][bass.ds(b * S + u * W, W), :].rearrange(
                        "(t p) d -> p t d", p=P)).then_inc(x_ld[u], 16)

                def load_inverse(b, u):
                    for hl in range(4):
                        src = io["rsum_s"][bass.ds(b * H, H), u * W:(u + 1) * W].rearrange(
                            "(k hl) t -> hl k t", hl=4)[hl]
                        sp.dma_start(r_b[u][hl * DH:(hl + 1) * DH, :, :],
                                     src.partition_broadcast(DH)).then_inc(o_ld[u], 16)

                def store_x1(b, u):
                    sp.wait_ge(x1_done, TT * (U * b + u + 1))
                    sp.dma_start(io["x1_s"][bass.ds(b * S + u * W, W), :].rearrange("(t p) d -> p t d", p=P),
                                 x1[u][:, :, :]).then_inc(x1_st[u], 16)

                def store_x1t(b, u):
                    sp.wait_ge(t_done, KT // 2 * (U * b + u + 1))
                    dst = io["x1t_s"][bass.ds(2 * b + u // 2, 1)].rearrange("o p k t -> p (o k) t")
                    sp.dma_start(dst[:, :, u % 2 * W:(u % 2 + 1) * W], x1t[u % 2][:, :, :]).then_inc(x1t_st[u % 2], 16)

                across = "h (q w) -> (h q) w"
                sp.dma_start(sums[:, :], io["sum_s"].rearrange(across, w=T * H // P)).then_inc(sum_ld, 16)
                load(0, 0, True)
                sp.dma_start(words(wo[:, :, :, :]), io["wo_s"].rearrange("k p c n -> p k c n")).then_inc(w_ld, 16)
                sp.dma_start(eye[:, :], io["consts"][:, P:2 * P]).then_inc(w_ld, 16)
                sp.wait_ge(rsum_done, 1)
                sp.dma_start(io["rsum_s"].rearrange(across, w=T * H // P), rsum[:, :]).then_inc(rsum_st, 16)
                sp.wait_ge(rsum_st, 16)
                load_inverse(0, 0)
                for u in range(1, AHEAD):
                    load(0, u, True)
                    load_inverse(0, u)

                def body(b, first, last):
                    for u in range(U):
                        over, nu = divmod(u + AHEAD, U)
                        if not (last and over):
                            load(b + over, nu, first and not over)
                            load_inverse(b + over, nu)
                        store_x1(b, u)
                        if u > 0:
                            store_x1t(b, u - 1)
                        elif not first:
                            store_x1t(b - 1, U - 1)

                body(0, True, False)
                with sp.Fori(1, B - 1) as b:
                    body(b, False, False)
                body(B - 1, False, True)
                store_x1t(B - 1, U - 1)
                for s in range(U):
                    sp.wait_ge(x1_st[s], 16 * B)
                for s in range(2):
                    sp.wait_ge(x1t_st[s], 16 * NC // 2)

            @block.gpsimd
            def _(pool):
                with pool.Fori(0, B) as b:
                    for u in range(U):
                        pool.wait_ge(o_ld[u], 96 * b + 96)
                        nc.gpsimd.tensor_tensor(o_a[u][:, :, :], o_a[u][:, :, :], o_b[u][:, :, :],
                                                ALU.add).then_inc(joined, 1)
                        pool.wait_ge(joined, U * b + u + 1)
                        nc.gpsimd.tensor_tensor(o_a[u][:, :, :], o_a[u][:, :, :], r_b[u][:, :, :],
                                                ALU.mult).then_inc(normed, 1)

            @block.scalar
            def _(act):
                def o_high(c, slot, first):
                    act.wait_ge(normed, c + 1)
                    if not first:
                        act.wait_ge(y_full, TT * (c - 1))
                    nc.scalar.copy(o_hi[slot % 2][:, :, :], o_a[slot][:, :, :]).then_inc(o_hi_done, 1)

                def x1t_out(b, u, first):
                    for j in range(KT // 2):
                        act.wait_ge(turned, KT // 2 * (U * b + u) + j + 1)
                        if not (first and u < 2) and j == 0:
                            act.wait_ge(x1t_st[u % 2], 16 * (U // 2 * b + u // 2))
                        nc.scalar.copy(x1t[u % 2][:, 2 * j:2 * j + 2, :], ps_x[u % 2][j][:, :, :]).then_inc(t_done, 1)

                def body(b, first, last):
                    for u in range(U):
                        c = U * b + u
                        act.wait_ge(var_done, c + 1)
                        nc.scalar.activation(std[:, :], mv[:, :, 1], ACT.Sqrt, bias=eps[:, 0:1]).then_inc(std_done, 1)
                        if not (last and u + 2 >= U):
                            o_high(c + 2, (u + 2) % U, False)
                        if u > 0:
                            x1t_out(b, u - 1, first)
                        elif not first:
                            x1t_out(b - 1, U - 1, False)

                act.wait_ge(eps_set, 1)
                o_high(0, 0, True)
                o_high(1, 1, True)
                body(0, True, False)
                with act.Fori(1, B - 1) as b:
                    body(b, False, False)
                body(B - 1, False, True)
                x1t_out(B - 1, U - 1, False)

            @block.vector
            def _(dve):
                nc.vector.memset(eps[:, :], EPS).then_inc(eps_set, 1)

                def o_low(c, slot):
                    dve.wait_ge(o_hi_done, c + 1)
                    nc.vector.tensor_tensor(o_lo[slot % 2][:, :, :], o_a[slot][:, :, :],
                                            o_hi[slot % 2][:, :, :].bitcast(F32), ALU.subtract).then_inc(o_split, 1)

                def body(b, first, last):
                    for u in range(U):
                        c = U * b + u
                        dve.wait_ge(x_ld[u], 16 * b + 16)
                        if not first:
                            dve.wait_ge(x1_st[u], 16 * b)
                        for t in range(TT):
                            dve.wait_ge(y_full, TT * c + t + 1)
                            nc.vector.tensor_tensor(x1[u][:, t, :], ps_y[u % 2][t][:, :], xn[u][:, t, :],
                                                    ALU.add).then_inc(z_done, 1)
                            dve.wait_ge(z_done, TT * c + t + 1)
                            nc.vector.bn_stats(stats[:, t, :], x1[u][:, t, :])
                        dve.drain()
                        for t in range(TT):
                            mm = nc.vector.bn_aggr(mv[:, t, :], stats[:, t, :])
                        mm.then_inc(var_done, 1)
                        dve.wait_ge(std_done, c + 1)
                        nc.vector.reciprocal(rstd[:, :], std[:, :]).then_inc(rstd_done, 1)
                        dve.wait_ge(rstd_done, c + 1)
                        for t in range(TT):
                            nc.vector.tensor_scalar(x1[u][:, t, :], x1[u][:, t, :], mv[:, t, 0:1], rstd[:, t:t + 1],
                                                    ALU.subtract, ALU.mult).then_inc(x1_done, 1)
                        if not (last and u + 2 >= U):
                            o_low(c + 2, (u + 2) % U)

                dve.wait_ge(sum_ld, 16)
                nc.vector.reciprocal(rsum[:, :], sums[:, :]).then_inc(rsum_done, 1)
                o_low(0, 0)
                o_low(1, 1)
                body(0, True, False)
                with dve.Fori(1, B - 1) as b:
                    body(b, False, False)
                body(B - 1, False, True)

            @block.tensor
            def _(pe):
                def product(c, u, first):
                    pe.wait_ge(o_split, c + 1)
                    for t in range(TT):
                        if not first:
                            pe.wait_ge(z_done, TT * (c - 2) + t + 1)
                        k = 0
                        for kt in range(KT):
                            for op, wp in PASSES:
                                mm = nc.tensor.matmul(ps_y[u % 2][t][:, :],
                                                      (o_hi, o_lo)[op][u % 2][:, kt, t * P:(t + 1) * P],
                                                      wo[:, kt, wp, :], start=(k == 0), stop=(k == 11))
                                k += 1
                        mm.then_inc(y_full, 1)

                def turn(c, slot, first):
                    pe.wait_ge(x1_done, TT * (c + 1))
                    for j in range(KT // 2):
                        if not first:
                            pe.wait_ge(t_done, KT // 2 * (c - 2) + j + 1)
                        for k in range(2):
                            for t in range(TT):
                                mm = nc.tensor.transpose(
                                    ps_x[slot % 2][j][:, k, t * P:(t + 1) * P],
                                    x1[slot][:, t, (2 * j + k) * P:(2 * j + k + 1) * P], eye[:, :])
                        mm.then_inc(turned, 1)

                def body(b, first):
                    for u in range(U):
                        c = U * b + u
                        product(c, u, first and u < 2)
                        if not (first and u == 0):
                            turn(c - 1, (u - 1) % U, first and u <= 2)

                pe.wait_ge(w_ld, 32)
                body(0, True)
                with pe.Fori(1, B) as b:
                    body(b, False)
                turn(NC - 1, U - 1, False)


def feed_forward(nc, sem, io):
    TT = CH // P
    WR = 2

    with ExitStack() as ctx:
        sb = lambda name, shape, dt: ctx.enter_context(nc.sbuf_tensor(name, shape, dt))
        wug = sb("wug", [P, FT, 2, 2, KT, P], F32R)
        wd = [sb(f"wd{s}", [P, 2, D], F32R) for s in range(WR)]
        xt_raw = sb("ff_xt_raw", [P, KT, CH], F32)
        xt = [sb(f"ff_xt{s}", [P, KT, 2, CH], F32R) for s in range(2)]
        z = sb("ff_z", [P, TT, D], F32)
        sil = [sb(f"silu{s}", [P, CH], F32) for s in range(2)]
        hid = [sb(f"hidden{s}", [P, CH], F32) for s in range(2)]
        h_hi = [sb(f"h_hi{s}", [P, CH], F32R) for s in range(2)]
        h_lo = [sb(f"h_lo{s}", [P, CH], F32R) for s in range(2)]
        ws = sb("ff_ws", [P, 2 * FT], F32)
        stats = sb("ff_stats", [P, TT, 6], F32)
        mv = sb("ff_mv", [P, TT, 2], F32)
        std = sb("ff_std", [P, TT], F32)
        rstd = sb("ff_rstd", [P, TT], F32)
        eps = sb("ff_eps", [P, 1], F32)
        ps_g = [ctx.enter_context(nc.psum_tensor(f"gate{s}", [P, CH], F32)) for s in range(2)]
        ps_u = [ctx.enter_context(nc.psum_tensor(f"up{s}", [P, CH], F32)) for s in range(2)]
        ps_y = [ctx.enter_context(nc.psum_tensor(f"ff_y{s}", [P, D], F32)) for s in range(TT)]

        wug_ld = [sem(f"wug_ld{s}") for s in range(FT)]
        wd_ld = [sem(f"wd_ld{s}") for s in range(WR)]
        xt_ld = sem("ff_xt_ld")
        xt_hi_done = sem("ff_xt_hi_done")
        xt_split = sem("ff_xt_split")
        z_ld = sem("ff_z_ld")
        ws_ld = sem("ff_ws_ld")
        gate_full = sem("gate_full")
        up_full = sem("up_full")
        sil_done = sem("silu_done")
        hid_done = sem("hidden_done")
        hhi_done = sem("h_hi_done")
        h_split = sem("h_split")
        down_done = sem("down_done")
        z_done = sem("ff_z_done")
        rstd_done = sem("ff_rstd_done")
        var_done = sem("ff_var_done")
        std_done = sem("ff_std_done")
        out_done = sem("ff_out_done")
        out_st = sem("out_st")
        eps_set = sem("ff_eps_set")

        with nc.Block() as block:
            @block.sync
            def _(sp):
                sp.dma_start(ws[:, :], io["ws_ug"]).then_inc(ws_ld, 16)

                def load_wug(f):
                    sp.dma_start(words(wug[:, f].rearrange("p g c k n -> p (g c k n)")),
                                 io["wug_s"][f].rearrange("p g c k n -> p (g c k n)")).then_inc(wug_ld[f], 16)

                def load_xt(c):
                    sp.dma_start(xt_raw[:, :, :],
                                 io["x1t_s"][bass.ds(c, 1)].rearrange("o p k t -> p (o k) t")).then_inc(xt_ld, 16)

                def load_wd(f):
                    sp.dma_start(words(wd[f % WR][:, :, :]), io["wd_s"][f]).then_inc(wd_ld[f % WR], 16)

                load_xt(0)
                for f in range(4):
                    load_wug(f)
                    if f < WR:
                        load_wd(f)

                def tail(c, u):
                    sp.wait_ge(out_done, TT * c + TT)
                    sp.dma_start(io["out"][bass.ds(c * CH, CH), :].rearrange("(t p) d -> p t d", p=P),
                                 z[:, :, :]).then_inc(out_st, 16)

                def load_z(c):
                    sp.dma_start(z[:, :, :], io["x1_s"][bass.ds(c * CH, CH), :].rearrange(
                        "(t p) d -> p t d", p=P)).then_inc(z_ld, 16)

                load_z(0)

                def body(i, first, last):
                    for u in range(2):
                        c = 2 * i + u
                        for f in range(FT):
                            if first and u == 0 and f + 4 < FT:
                                load_wug(f + 4)
                            if f == 1 and not (last and u == 1):
                                sp.wait_ge(xt_split, KT * c + KT)
                                load_xt(c + 1)
                            if not (last and u == 1 and f + WR >= FT):
                                sp.wait_ge(down_done, FT * c + f + 1)
                                load_wd((f + WR) % FT)
                            if f == 8 and not (first and u == 0):
                                tail(c - 1, u)
                                sp.wait_ge(out_st, 16 * c)
                                load_z(c)

                body(0, True, False)
                with sp.Fori(1, B - 1) as i:
                    body(i, False, False)
                body(B - 1, False, True)
                tail(NCH - 1, 1)
                sp.wait_ge(out_st, 16 * NCH)

            @block.scalar
            def _(act):
                act.wait_ge(ws_ld, 16)
                act.wait_ge(eps_set, 1)

                def xt_high(c, s, k):
                    if k == 0:
                        act.wait_ge(xt_ld, 16 * c + 16)
                    nc.scalar.copy(xt[s][:, k, 0, :], xt_raw[:, k, :]).then_inc(xt_hi_done, 1)

                for k in range(KT):
                    xt_high(0, 0, k)

                def body(i, first, last):
                    for u in range(2):
                        for f in range(FT):
                            c = 2 * i + u
                            n = FT * c + f
                            act.wait_ge(gate_full, n + 1)
                            if not (first and u == 0 and f < 2):
                                act.wait_ge(hid_done, n - 1)
                            nc.scalar.activation(sil[f % 2][:, :], ps_g[f % 2][:, :], ACT.Silu,
                                                 scale=ws[:, FT + f:FT + f + 1]).then_inc(sil_done, 1)
                            act.wait_ge(hid_done, n + 1)
                            if not (first and u == 0 and f < 2):
                                act.wait_ge(down_done, n - 1)
                            nc.scalar.copy(h_hi[f % 2][:, :], hid[f % 2][:, :]).then_inc(hhi_done, 1)
                            if 8 <= f < 8 + KT and not (last and u == 1):
                                xt_high(c + 1, 1 - u, f - 8)
                            if f == 3 and not (first and u == 0):
                                act.wait_ge(var_done, c)
                                nc.scalar.activation(std[:, :], mv[:, :, 1], ACT.Sqrt,
                                                     bias=eps[:, 0:1]).then_inc(std_done, 1)

                body(0, True, False)
                with act.Fori(1, B - 1) as i:
                    body(i, False, False)
                body(B - 1, False, True)
                act.wait_ge(var_done, NCH)
                nc.scalar.activation(std[:, :], mv[:, :, 1], ACT.Sqrt, bias=eps[:, 0:1]).then_inc(std_done, 1)

            @block.gpsimd
            def _(pool):
                def xt_low(c, s):
                    for k in range(KT):
                        pool.wait_ge(xt_hi_done, KT * c + k + 1)
                        nc.gpsimd.tensor_tensor(xt[s][:, k, 1, :], xt_raw[:, k, :], xt[s][:, k, 0, :].bitcast(F32),
                                                ALU.subtract).then_inc(xt_split, 1)

                xt_low(0, 0)
                with pool.Fori(0, B - 1) as i:
                    xt_low(2 * i + 1, 1)
                    xt_low(2 * i + 2, 0)
                xt_low(NCH - 1, 1)

            @block.vector
            def _(dve):
                nc.vector.memset(eps[:, :], EPS).then_inc(eps_set, 1)
                dve.wait_ge(ws_ld, 16)

                def sums(c):
                    dve.wait_ge(z_ld, 16 * c)
                    dve.wait_ge(down_done, FT * c)
                    for t in range(TT):
                        nc.vector.tensor_tensor(z[:, t, :], ps_y[t][:, :], z[:, t, :], ALU.add).then_inc(z_done, 1)
                    for t in range(TT):
                        dve.wait_ge(z_done, TT * (c - 1) + t + 1)
                        nc.vector.bn_stats(stats[:, t, :], z[:, t, :])
                    dve.drain()
                    for t in range(TT):
                        mm = nc.vector.bn_aggr(mv[:, t, :], stats[:, t, :])
                    mm.then_inc(var_done, 1)

                def norm(c):
                    dve.wait_ge(std_done, c)
                    nc.vector.reciprocal(rstd[:, :], std[:, :]).then_inc(rstd_done, 1)
                    dve.wait_ge(rstd_done, c)
                    for t in range(TT):
                        nc.vector.tensor_scalar(z[:, t, :], z[:, t, :], mv[:, t, 0:1], rstd[:, t:t + 1],
                                                ALU.subtract, ALU.mult).then_inc(out_done, 1)

                def body(i, first):
                    for u in range(2):
                        c = 2 * i + u
                        for f in range(FT):
                            n = FT * c + f
                            if f == 1 and not (first and u == 0):
                                sums(c)
                            dve.wait_ge(up_full, n + 1)
                            dve.wait_ge(sil_done, n + 1)
                            nc.vector.scalar_tensor_tensor(hid[f % 2][:, :], ps_u[f % 2][:, :], ws[:, f:f + 1],
                                                           sil[f % 2][:, :], ALU.mult, ALU.mult).then_inc(hid_done, 1)
                            dve.wait_ge(hhi_done, n + 1)
                            nc.vector.tensor_tensor(h_lo[f % 2][:, :], hid[f % 2][:, :],
                                                    h_hi[f % 2][:, :].bitcast(F32), ALU.subtract).then_inc(h_split, 1)
                            if f == 4 and not (first and u == 0):
                                norm(c)

                body(0, True)
                with dve.Fori(1, B) as i:
                    body(i, False)
                sums(NCH)
                norm(NCH)

            @block.tensor
            def _(pe):
                def gate_up(i, u, f, first):
                    c = 2 * i + u
                    n = FT * c + f
                    if f == 0:
                        pe.wait_ge(xt_split, KT * c + KT)
                    if first and u == 0:
                        pe.wait_ge(wug_ld[f], 16)
                    if not (first and u == 0 and f < 2):
                        pe.wait_ge(hid_done, n - 1)
                    for g, (bank, done) in ((1, (ps_g, gate_full)), (0, (ps_u, up_full))):
                        k = 0
                        for kt in range(KT):
                            for wp, xp in PASSES:
                                mm = nc.tensor.matmul(bank[f % 2][:, :], wug[:, f, g, wp, kt, :],
                                                      xt[u][:, kt, xp, :], start=(k == 0), stop=(k == 11))
                                k += 1
                        mm.then_inc(done, 1)

                def down(c, f, first):
                    pe.wait_ge(h_split, FT * c + f + 1)
                    pe.wait_ge(wd_ld[f % WR], 16 * (FT // WR) * c + 16 * (f // WR) + 16)
                    for t in range(TT):
                        if f == 0 and not first:
                            pe.wait_ge(z_done, TT * (c - 1) + t + 1)
                        for k, (hp, wp) in enumerate(PASSES):
                            mm = nc.tensor.matmul(ps_y[t][:, :], (h_hi, h_lo)[hp][f % 2][:, t * P:(t + 1) * P],
                                                  wd[f % WR][:, wp, :], start=(f == 0 and k == 0),
                                                  stop=(f == FT - 1 and k == 2))
                    mm.then_inc(down_done, 1)

                def body(i, first):
                    for u in range(2):
                        c = 2 * i + u
                        for f in range(FT):
                            gate_up(i, u, f, first)
                            if f > 0:
                                down(c, f - 1, first and u == 0)
                            elif not (first and u == 0):
                                down(c - 1, FT - 1, False)

                body(0, True)
                with pe.Fori(1, B) as i:
                    body(i, False)
                down(NCH - 1, FT - 1, False)


_HOST = ["x", "xt", "wqkv", "wout", "wugt", "wdt", "su_ug", "su_dp", "ws_ug", "ws_dp", "consts"]
_SCRATCH = {
    "q_s": [2, B * D, S], "k_s": [2, B * D, S],
    "v_s": [B * 8, S, P],
    "wo_s": [KT, P, 2, D], "wd_s": [FT, P, 2, D], "wug_s": [FT, P, 2, 2, KT, P],
    "x1t_s": [NCH, P, KT, CH],
    "o_s": [2, B * D, S], "sum_s": [B * H, S], "rsum_s": [B * H, S], "x1_s": [T, D],
}


def build(nc, io):
    for name, shape in _SCRATCH.items():
        io[name] = nc.dram_tensor(name, shape, F32, kind="Internal").ap()
    with ExitStack() as ctx:
        def sem(name):
            return ctx.enter_context(nc.semaphore(name))
        project_qkv(nc, sem, io)
        attend(nc, sem, io)
        project_out(nc, sem, io)
        feed_forward(nc, sem, io)


def constants():
    had = np.ones((1, 1), np.float32)
    while had.shape[0] < P:
        had = np.block([[had, had], [had, -had]])
    eye = np.eye(P, dtype=np.float32)
    later = np.triu(np.ones((P, P), np.float32), 1) * np.float32(MASKED)
    return np.ascontiguousarray(np.concatenate([had, eye, later, later.T], axis=1), dtype=np.float32)


def kernel(**inputs):
    import concourse.bacc as _bacc
    from concourse import mybir as _mybir
    from concourse.bass_utils import run_bass_kernel_spmd as _run

    a = {k: np.asarray(v) for k, v in inputs.items()}
    x = a["L0_attn_x"].reshape(T, D)
    arrays = {
        "x": x,
        "xt": x.T,
        "wqkv": a["L0_attn_w_qkv"],
        "wout": a["L0_attn_w_out"],
        "wugt": np.concatenate([a["L0_ffn_W_up"], a["L0_ffn_W_gate"]], axis=0).T,
        "wdt": a["L0_ffn_W_down"].T,
        "su_ug": a["L0_ffn_SU_ug"].reshape(KT, P).T,
        "su_dp": a["L0_ffn_SU_dp"].reshape(FT, P).T,
        "ws_ug": a["L0_ffn_Wscale_ug"].reshape(2 * FT, P).T,
        "ws_dp": a["L0_ffn_Wscale_dp"],
        "consts": constants(),
    }
    nc = _bacc.Bacc("TRN2", target_bir_lowering=False, num_devices=1)
    fed, io = {}, {}
    for name in _HOST:
        v = np.ascontiguousarray(arrays[name])
        fed[f"in_{name}"] = v
        io[name] = nc.dram_tensor(f"in_{name}", v.shape, _mybir.dt.from_np(v.dtype), kind="ExternalInput").ap()
    io["out"] = nc.dram_tensor("out_0", (T, D), F32, kind="ExternalOutput").ap()
    build(nc, io)
    r = _run(nc, [fed], core_ids=[0])
    return r.results[0]["out_0"].reshape(B, S, D)
```

```python
import numpy as np
import concourse.bass as bass
from concourse import mybir
from contextlib import ExitStack

F32 = mybir.dt.float32
F32R = mybir.dt.float32r
BF16 = mybir.dt.bfloat16
ALU = mybir.AluOpType
ACT = mybir.ActivationFunctionType
AX = mybir.AxisListType

P = 128
B, S, D = 4, 1024, 512
H, DH = 16, 32
T = B * S
INTER = 2048
KT = D // P
FT = INTER // P
CH = 512
NCH = T // CH
EPS = 1e-5
MASKED = -1e30


PASSES = ((0, 0), (0, 1), (1, 0))


def words(ap):
    return ap.bitcast(F32)


def project_qkv(nc, sem, io):
    RING = 6
    QK0 = [("qk", 0, n) for n in range(8)]
    V0 = [("v", 0, n) for n in range(4)]
    QK1 = [("qk", 1, n) for n in range(8)]
    V1 = [("v", 1, n) for n in range(4)]
    UP = [("up", 0, n) for n in range(4)]
    GATE = [("gate", 1, n) for n in range(4)]
    DOWN = [("down", 2, n) for n in range(4)]
    JOBS = QK0 + UP + V0 + QK1[:4] + GATE + QK1[4:] + V1 + DOWN
    NJ = len(JOBS)
    FOLD = ("up", "gate", "down")
    FOLD_AT = {0: 2, 1: 10, 2: 26}
    SPLIT_AT = {1: 5, 0: 24}

    def dmas(job):
        return 2 if job[0] in FOLD else 1

    def stored(i, n):
        slot = n % RING
        each = sum(dmas(JOBS[m]) for m in range(slot, NJ, RING))
        return 16 * (i * each + sum(dmas(JOBS[m]) for m in range(slot, n, RING)))

    STEPS = (4, 8, 17)

    def last_of(kind, u):
        return max(n for n, j in enumerate(JOBS) if j[:2] == (kind, u))

    def folds_before(n):
        return sum(1 for j in JOBS[:n] if j[0] in FOLD)

    with ExitStack() as ctx:
        sb = lambda name, shape, dt: ctx.enter_context(nc.sbuf_tensor(name, shape, dt))
        wqkv = sb("wqkv_split", [P, 2, KT, 3 * D], F32R)
        x_raw = [sb(f"x_raw{s}", [P, KT, CH], F32) for s in range(2)]
        x_hi = [sb(f"x_hi{s}", [P, KT, CH], F32R) for s in range(2)]
        x_lo = [sb(f"x_lo{s}", [P, KT, CH], F32R) for s in range(2)]
        raw = [sb(f"w_raw{s}", [P, 2048], F32) for s in range(3)]
        half = sb("butterfly", [P, 2048], F32)
        rot = sb("rotated", [P, 2048], F32)
        rot_hi = sb("rotated_hi", [P, 2048], F32R)
        rot_lo = sb("rotated_lo", [P, 2048], F32R)
        scaled = [sb(f"scaled{s}", [P, CH], F32) for s in range(2)]
        stage = [sb(f"stage{s}", [P, 2 * CH], F32R) for s in range(RING)]
        had_f = sb("had_f", [P, P], F32)
        had = sb("had", [P, P], F32R)
        su_ug = sb("su_ug", [P, KT], F32)
        su_dp = sb("su_dp", [P, FT], F32)
        ws_dp = sb("ws_dp", [P, D], F32)
        bank = [ctx.enter_context(nc.psum_tensor(f"pj{s}", [P, CH], F32)) for s in range(RING)]

        raw_ld = [sem(f"raw_ld{s}") for s in range(3)]
        x_ld = [sem(f"x_ld{s}") for s in range(2)]
        const_ld = sem("const_ld")
        store_done = [sem(f"store_done{s}") for s in range(RING)]
        wsplit_hi = sem("wsplit_hi")
        wsplit_done = sem("wsplit_done")
        had_ready = sem("had_ready")
        x_hi_done = sem("x_hi_done")
        x_split = sem("x_split")
        butter = sem("butter")
        rot_hi_done = sem("rot_hi_done")
        rot_split = sem("rot_split")
        full = sem("pj_full")
        scaled_done = sem("scaled_done")
        hi_done = sem("pj_hi_done")
        evacuated = sem("pj_evacuated")

        ITERS = B
        wqkv_in = io["wqkv"].rearrange("(k p) n -> p k n", p=P)
        xt_in = io["xt"].rearrange("(k p) t -> p k t", p=P)
        wug_in = io["wugt"].rearrange("(k p) f -> p k f", p=P)
        wd_in = io["wdt"].rearrange("(k p) n -> p k n", p=P)

        def as_kt(t, k=KT):
            return t[:, :].rearrange("p (k n) -> p k n", k=k)

        def out_parts(job, n):
            st = stage[n % RING]
            if job[0] == "v":
                v = st[:, :].rearrange("p (h c d) -> p h c d", h=H, c=2)
                return v[:, :, 0, :], v[:, :, 1, :]
            return st[:, 0:CH], st[:, CH:2 * CH]

        def shaped(ap, job):
            return ap.rearrange("p (h d) -> p h d", h=H) if job[0] == "v" else ap

        with nc.Block() as block:
            @block.sync
            def _(sp):
                for s in range(3):
                    sp.dma_start(as_kt(raw[s]), wqkv_in[:, :, s * D:(s + 1) * D]).then_inc(raw_ld[s], 16)
                    if s == 0:
                        sp.dma_start(x_raw[0][:, :, :], xt_in[:, :, 0:CH]).then_inc(x_ld[0], 16)
                sp.dma_start(had_f[:, :], io["consts"][:, 0:P]).then_inc(const_ld, 16)
                sp.dma_start(su_ug[:, :], io["su_ug"]).then_inc(const_ld, 16)
                sp.dma_start(su_dp[:, :], io["su_dp"]).then_inc(const_ld, 16)
                sp.dma_start(ws_dp[:, :], io["ws_dp"].partition_broadcast(P)).then_inc(const_ld, 16)
                sp.dma_start(x_raw[1][:, :, :], xt_in[:, :, CH:2 * CH]).then_inc(x_ld[1], 16)
                sp.wait_ge(wsplit_done, 1)
                sp.dma_start(as_kt(raw[0]), wug_in[:, :, 0:CH]).then_inc(raw_ld[0], 16)
                sp.wait_ge(wsplit_done, 2)
                sp.dma_start(as_kt(raw[1]), wug_in[:, :, INTER:INTER + CH]).then_inc(raw_ld[1], 16)
                sp.wait_ge(wsplit_done, 3)
                sp.dma_start(as_kt(raw[2], FT), wd_in[:, :, 0:P]).then_inc(raw_ld[2], 16)

                def body(i, last):
                    for n, job in enumerate(JOBS):
                        kind, u, m = job
                        if not last and kind == "qk" and m == 0:
                            sp.wait_ge(x_split, 2 * i + u + 1)
                            sp.dma_start(x_raw[u][:, :, :],
                                         xt_in[:, :, bass.ds((2 * i + 2 + u) * CH, CH)]).then_inc(x_ld[u], 16)
                        sp.wait_ge(evacuated, NJ * i + n + 1)
                        st = stage[n % RING]
                        done = store_done[n % RING]
                        if kind == "qk":
                            dst = io["q_s"] if m < 4 else io["k_s"]
                            rows = bass.ds(i * D + (m % 4) * P, P)
                            sp.dma_start(dst[:, rows, u * CH:(u + 1) * CH].rearrange("c p t -> p c t"),
                                         words(st[:, :].rearrange("p (c t) -> p c t", c=2))).then_inc(done, 16)
                        elif kind == "v":
                            dst = io["v_s"][bass.ds(i * 8, 8), u * CH + m * P:u * CH + (m + 1) * P, :]
                            sp.dma_start(dst.rearrange("h p c -> p h c"),
                                         words(st[:, :].rearrange("p (h c) -> p h c", h=8))).then_inc(done, 16)
                        else:
                            for part in range(2):
                                src = words(st[:, part * CH:(part + 1) * CH].rearrange("p (f n) -> p f n", f=4))
                                if kind == "down":
                                    dst = io["wd_s"][4 * m:4 * m + 4, :, part, bass.ds(i * P, P)]
                                else:
                                    dst = io["wug_s"][bass.ds(4 * i, 4), :, u, part, m, :]
                                sp.dma_start(dst.rearrange("f p n -> p f n"), src).then_inc(done, 16)
                        if not last and kind in FOLD and m == 3:
                            sp.wait_ge(butter, STEPS[2] * i + STEPS[u])
                            if kind == "down":
                                src = wd_in[:, :, bass.ds((i + 1) * P, P)]
                                sp.dma_start(as_kt(raw[2], FT), src).then_inc(raw_ld[2], 16)
                            else:
                                src = wug_in[:, :, bass.ds(u * INTER + (i + 1) * CH, CH)]
                                sp.dma_start(as_kt(raw[u]), src).then_inc(raw_ld[u], 16)

                with sp.Fori(0, ITERS - 1) as i:
                    body(i, False)
                body(ITERS - 1, True)
                for s in range(RING):
                    sp.wait_ge(store_done[s], stored(ITERS, s))

            @block.gpsimd
            def _(pool):
                pool.wait_ge(const_ld, 64)

                def step(i, k, op, out, a, b):
                    nc.gpsimd.tensor_tensor(out, a, b, op).then_inc(butter, 1)
                    pool.wait_ge(butter, STEPS[2] * i + k + 1)

                with pool.Fori(0, ITERS) as i:
                    k = 0
                    for u, kind in enumerate(FOLD):
                        pool.wait_ge(raw_ld[u], 16 * i + 32)
                        if kind == "down":
                            cols = as_kt(raw[2], FT)
                            scale = ws_dp[:, bass.ds(i * P, P)].unsqueeze(1).to_broadcast([P, FT, P])
                            step(i, k, ALU.mult, cols, cols, scale)
                            k += 1
                        stages = 4 if kind == "down" else 2
                        src = raw[u]
                        for st in range(stages):
                            dst = rot if st == stages - 1 else (half, raw[u])[st % 2]
                            near = (2048 >> stages) << st
                            a = src[:, :].rearrange("p (g two w) -> p g two w", two=2, w=near)
                            o = dst[:, :].rearrange("p (g two w) -> p g two w", two=2, w=near)
                            for op, col in ((ALU.add, 0), (ALU.subtract, 1)):
                                step(i, k, op, o[:, :, col, :], a[:, :, 0, :], a[:, :, 1, :])
                                k += 1
                            src = dst
                        assert k == STEPS[u]
                        pool.wait_ge(rot_hi_done, 3 * i + u + 1)
                        nc.gpsimd.tensor_tensor(rot_lo[:, :], rot[:, :], rot_hi[:, :].bitcast(F32),
                                                ALU.subtract).then_inc(rot_split, 1)
                        pool.wait_ge(rot_split, 3 * i + u + 1)

            @block.scalar
            def _(act):
                for s in range(3):
                    act.wait_ge(raw_ld[s], 16)
                    nc.scalar.copy(wqkv[:, 0, :, s * D:(s + 1) * D], as_kt(raw[s])).then_inc(wsplit_hi, 1)
                    if s == 0:
                        act.wait_ge(x_ld[0], 16)
                        nc.scalar.copy(x_hi[0][:, :, :], x_raw[0][:, :, :]).then_inc(x_hi_done, 1)

                def body(i, first, last):
                    for n, job in enumerate(JOBS):
                        kind, u, m = job
                        if not (first and n < RING):
                            act.wait_ge(store_done[n % RING], stored(i, n))
                        hi, _ = out_parts(job, n)
                        if kind in FOLD:
                            k = folds_before(n)
                            act.wait_ge(scaled_done, 12 * i + k + 1)
                            nc.scalar.copy(hi, scaled[k % 2][:, :]).then_inc(hi_done, 1)
                        else:
                            act.wait_ge(full, NJ * i + n + 1)
                            nc.scalar.copy(hi, shaped(bank[n % RING][:, :], job)).then_inc(hi_done, 1)
                        for t, at in FOLD_AT.items():
                            if n == at:
                                act.wait_ge(butter, STEPS[2] * i + STEPS[t])
                                if not (first and t == 0):
                                    act.wait_ge(full, NJ * i + (last_of(FOLD[t - 1], t - 1) + 1 if t else 0))
                                nc.scalar.copy(rot_hi[:, :], rot[:, :]).then_inc(rot_hi_done, 1)
                        if n == SPLIT_AT[1]:
                            act.wait_ge(x_ld[1], 16 * i + 16)
                            nc.scalar.copy(x_hi[1][:, :, :], x_raw[1][:, :, :]).then_inc(x_hi_done, 1)
                        if n == SPLIT_AT[0] and not last:
                            act.wait_ge(x_ld[0], 16 * i + 32)
                            act.wait_ge(full, NJ * i + last_of("v", 0) + 1)
                            nc.scalar.copy(x_hi[0][:, :, :], x_raw[0][:, :, :]).then_inc(x_hi_done, 1)

                body(0, True, False)
                with act.Fori(1, ITERS - 1) as i:
                    body(i, False, False)
                body(ITERS - 1, False, True)

            @block.vector
            def _(dve):
                for s in range(3):
                    dve.wait_ge(wsplit_hi, s + 1)
                    nc.vector.tensor_tensor(wqkv[:, 1, :, s * D:(s + 1) * D], as_kt(raw[s]),
                                            wqkv[:, 0, :, s * D:(s + 1) * D].bitcast(F32),
                                            ALU.subtract).then_inc(wsplit_done, 1)
                    if s == 0:
                        dve.wait_ge(x_hi_done, 1)
                        nc.vector.tensor_tensor(x_lo[0][:, :, :], x_raw[0][:, :, :],
                                                x_hi[0][:, :, :].bitcast(F32), ALU.subtract).then_inc(x_split, 1)
                dve.wait_ge(const_ld, 64)
                nc.vector.tensor_copy(had[:, :], had_f[:, :]).then_inc(had_ready, 1)
                nc.vector.tensor_scalar(su_ug[:, :], su_ug[:, :], float(D) ** -0.5, None,
                                        ALU.mult).then_inc(had_ready, 1)
                nc.vector.tensor_scalar(su_dp[:, :], su_dp[:, :], float(INTER) ** -0.5, None,
                                        ALU.mult).then_inc(had_ready, 1)
                dve.wait_ge(had_ready, 3)

                def scale(i, n):
                    kind, _, m = JOBS[n]
                    out = scaled[folds_before(n) % 2]
                    dve.wait_ge(full, NJ * i + n + 1)
                    dve.wait_ge(evacuated, NJ * i + n - 1)
                    if kind == "down":
                        by = su_dp[:, 4 * m:4 * m + 4].unsqueeze(2).to_broadcast([P, 4, P])
                        nc.vector.tensor_tensor(as_kt(out), as_kt(bank[n % RING]), by,
                                                ALU.mult).then_inc(scaled_done, 1)
                    else:
                        nc.vector.tensor_scalar(out[:, :], bank[n % RING][:, :], su_ug[:, m:m + 1], None,
                                                ALU.mult).then_inc(scaled_done, 1)

                def body(i, last):
                    for n, job in enumerate(JOBS):
                        kind, u, m = job
                        hi, lo = out_parts(job, n)
                        src = shaped(bank[n % RING][:, :], job)
                        if kind in FOLD:
                            src = scaled[folds_before(n) % 2][:, :]
                            if m == 0:
                                scale(i, n)
                            if m < 3:
                                scale(i, n + 1)
                        dve.wait_ge(hi_done, NJ * i + n + 1)
                        nc.vector.tensor_tensor(lo, src, hi.bitcast(F32), ALU.subtract).then_inc(evacuated, 1)
                        if n == SPLIT_AT[1]:
                            dve.wait_ge(x_hi_done, 2 * i + 2)
                            nc.vector.tensor_tensor(x_lo[1][:, :, :], x_raw[1][:, :, :],
                                                    x_hi[1][:, :, :].bitcast(F32), ALU.subtract).then_inc(x_split, 1)
                        if n == SPLIT_AT[0] and not last:
                            dve.wait_ge(x_hi_done, 2 * i + 3)
                            nc.vector.tensor_tensor(x_lo[0][:, :, :], x_raw[0][:, :, :],
                                                    x_hi[0][:, :, :].bitcast(F32), ALU.subtract).then_inc(x_split, 1)

                with dve.Fori(0, ITERS - 1) as i:
                    body(i, False)
                body(ITERS - 1, True)

            @block.tensor
            def _(pe):
                def body(i, first):
                    for n, job in enumerate(JOBS):
                        kind, u, m = job
                        if not first:
                            pe.wait_ge(evacuated, NJ * i + n - RING + 1)
                        elif n >= RING:
                            pe.wait_ge(evacuated, n - RING + 1)
                        out = bank[n % RING][:, :]
                        if kind == "qk" and m == 0:
                            pe.wait_ge(x_split, 2 * i + u + 1)
                        if first and u == 0 and kind in ("qk", "v") and m in (0, 4):
                            pe.wait_ge(wsplit_done, 1 if m == 0 else 2)
                        if first and u == 0 and kind == "v" and m == 0:
                            pe.wait_ge(wsplit_done, 3)
                        if first and kind in FOLD and m == 0:
                            pe.wait_ge(had_ready, 1)
                        if kind in FOLD and m == 0:
                            pe.wait_ge(rot_split, 3 * i + u + 1)
                        xs = (x_hi[u], x_lo[u]) if kind in ("qk", "v") else None
                        k = 0
                        if kind == "qk":
                            for kt in range(KT):
                                for wp, xp in PASSES:
                                    mm = nc.tensor.matmul(out, wqkv[:, wp, kt, m * P:(m + 1) * P],
                                                          xs[xp][:, kt, :], start=(k == 0), stop=(k == 11))
                                    k += 1
                        elif kind == "v":
                            for kt in range(KT):
                                for xp, wp in PASSES:
                                    mm = nc.tensor.matmul(out, xs[xp][:, kt, m * P:(m + 1) * P],
                                                          wqkv[:, wp, kt, 2 * D:3 * D], start=(k == 0), stop=(k == 11))
                                    k += 1
                        else:
                            for t, part in enumerate((rot_hi, rot_lo)):
                                mm = nc.tensor.matmul(out, had[:, :], part[:, m * CH:(m + 1) * CH],
                                                      start=(t == 0), stop=(t == 1))
                        mm.then_inc(full, 1)
                body(0, True)
                with pe.Fori(1, ITERS) as i:
                    body(i, False)


def attend(nc, sem, io, out_weights):
    wo_raw, wo, select, eye_out, w_ld, wo_hi_done, wo_split = out_weights
    HEADS = B * H
    UNROLL = 4
    ITERS = HEADS // UNROLL
    NT = 5
    NK = NT * UNROLL
    LAG = 6
    HIGH_LAG = 1
    LOW_LAG = 3
    NP = 10
    PR = 2 * NT
    ON_POOL = (0, 1, 2, 3)
    HIGH_ON_DVE = (4,)
    SCALE = float(1.0 / np.sqrt(np.float32(DH)))
    G = P

    TILES = (
        ((0, 3, 256, 256), (256, 2, 256, 256), (512, 0, 0, 512)),
        ((0, 3, 512, 512), (512, 1, 128, 384)),
        ((0, 7, 768, 256), (256, 6, 768, 256), (512, 4, 512, 512)),
        ((0, 0, 512, 512), (512, 5, 640, 384)),
        ((0, 1, 512, 512), (512, 2, 512, 512)),
    )
    DIAGONALS = (((G, 2 * G), (512, G)), ((512, G),), ((G, 2 * G), (512, G)), ((512, G),), ())
    USED = ((G, 1024), (0, 896), (G, 1024), (0, 896), (0, 1024))
    PV = ((2, 1, 0), (0, 1), (2, 1, 0), (0, 1), (0, 1))
    OPENS = {(0, 2), (1, 0)}
    CLOSES = {(1, 1), (4, 1)}

    ROWS = (
        (((0, 1, 0, 256), (256, 0, 0, 256)), (G, 2 * G), ((1, 0, 256), (0, 256, G))),
        (((0, 2, 0, 384),), (256, G), ((2, 0, 384),)),
        (((0, 3, 0, 512),), (384, G), ((3, 0, 512),)),
        (((0, 4, 0, 512),), None, ((4, 0, 512),)),
        (((0, 5, 0, 512),), None, ((5, 0, 512),)),
        (((0, 6, 0, 512),), None, ((6, 0, 512),)),
        (((0, 7, 0, 512),), None, ((7, 0, 512),)),
        (((0, 5, 512, 256), (256, 4, 512, 256)), (G, 2 * G), ((9, 0, 256), (8, 256, G))),
        (((0, 6, 512, 384),), (256, G), ((10, 0, 384),)),
        (((0, 7, 512, 512),), (384, G), ((11, 0, 512),)),
    )
    NR = len(ROWS)
    NS = NR + 1
    NREAD = sum(len(maxima) for _, _, maxima in ROWS) + 1
    AT_TILE = ((0, 1), (2, 3, 4), (5, 6), (7, 8, 9), ())
    EARLY = 4

    def reads(hh, r):
        if r < 0:
            return reads(hh - 1, r + NS)
        return NREAD * hh + sum(len(maxima) for _, _, maxima in ROWS[:r + 1]) + (1 if r == NR else 0)

    with ExitStack() as ctx:
        sb = lambda name, shape, dt: ctx.enter_context(nc.sbuf_tensor(name, shape, dt))
        qs = [sb(f"q_stack{s}", [3 * DH + 1, S], F32R) for s in range(4)]
        ks = [sb(f"k_stack{s}", [3 * DH + 1, S], F32R) for s in range(4)]
        v = [sb(f"v_pair{s}", [P, 8, 4 * DH + 2], F32R) for s in range(2)]
        probs = [sb(f"probs{s}", [P, 2 * CH], F32) for s in range(NP)]
        p_hi = [sb(f"p_hi{s}", [P, 2 * CH], F32R) for s in range(PR)]
        p_lo = [sb(f"p_lo{s}", [P, 2 * CH], F32R) for s in range(PR)]
        o_out = [sb(f"o_out{s}", [2 * DH + 1, S], F32) for s in range(2)]
        neg = [sb(f"neg_max{s}", [P, 12], F32) for s in range(2)]
        neg_row = [sb(f"neg_row{s}", [8, P], F32R) for s in range(2)]
        consts = sb("att_consts", [P, 3 * P], F32)
        masks = sb("att_masks", [P, 5 * P], BF16)
        eye = masks[:, 0:P]
        mask_rows = masks[:, P:3 * P]
        mask_cols = masks[:, 3 * P:5 * P]
        eye_f = consts[:, 0:P]
        ps_t = [ctx.enter_context(nc.psum_tensor(f"scores{s}", [P, 2 * CH], F32)) for s in range(2)]
        ps_r = [ctx.enter_context(nc.psum_tensor(f"rows{s}", [P, CH], F32)) for s in range(2)]
        ps_o = [ctx.enter_context(nc.psum_tensor(f"heads_out{s}", [P, CH], F32)) for s in range(2)]

        c_ld = sem("att_const_ld")
        fixed = sem("att_fixed")
        masks_ready = sem("att_masks_ready")
        qk_ld = [sem(f"qk_ld{s}") for s in range(4)]
        v_ld = [sem(f"v_ld{s}") for s in range(2)]
        m_ld = [sem(f"m_ld{s}") for s in range(2)]
        rows_full = sem("rows_full")
        rows_read = sem("rows_read")
        neg_done = sem("neg_done")
        s_full = sem("scores_full")
        exp_done = sem("exp_done")
        hi_act = sem("p_hi_act")
        hi_dve = sem("p_hi_dve")
        lo_dve = sem("lo_dve")
        lo_pool = sem("lo_pool")
        pv_done = sem("pv_done")
        o_read = sem("o_read")
        o_st = [sem(f"o_st{s}") for s in range(2)]

        n_pool = len(ON_POOL)
        n_dve = NT - n_pool

        def lo_wait(eng, i, k):
            before = i * UNROLL + k // NT
            t = k % NT
            if t in ON_POOL:
                eng.wait_ge(lo_pool, before * n_pool + sum(1 for x in ON_POOL if x <= t))
            else:
                eng.wait_ge(lo_dve, before * n_dve + sum(1 for x in range(t + 1) if x not in ON_POOL))

        def high_wait(eng, i, k):
            t = k % NT
            if t in HIGH_ON_DVE:
                eng.wait_ge(hi_dve, (i * UNROLL + k // NT) * len(HIGH_ON_DVE) + HIGH_ON_DVE.index(t) + 1)
            else:
                before = sum(1 for x in range(t + 1) if x not in HIGH_ON_DVE)
                eng.wait_ge(hi_act, (i * UNROLL + k // NT) * (NT - len(HIGH_ON_DVE)) + before)

        banks = [ps_r[0][:, :], ps_r[1][:, :], ps_t[0][:, 0:CH], ps_t[0][:, CH:2 * CH]]

        def row_bank(n, early):
            return banks[n % (EARLY if early else 2)]

        def runs(body):
            def go(eng):
                body(0, True, False)
                with eng.Fori(1, ITERS - 1) as i:
                    body(i, False, False)
                body(ITERS - 1, False, True)
            return go

        with nc.Block() as block:
            @block.sync
            def _(sp):
                def load_qk(hh, slot):
                    for stack, part_of, src in ((qs, (0, 0, 1), io["q_s"]), (ks, (0, 1, 0), io["k_s"])):
                        for row, part in enumerate(part_of):
                            sp.dma_start(words(stack[slot][row * DH:(row + 1) * DH, :]),
                                         src[part, bass.ds(hh * DH, DH), :]).then_inc(qk_ld[slot], 16)

                def load_v(pair, slot):
                    sp.dma_start(words(v[slot][:, :, 1:4 * DH + 1]),
                                 io["v_s"][bass.ds(pair, 1)].rearrange("o (b p) c -> p (o b) c", p=P)
                                 ).then_inc(v_ld[slot], 16)

                def load_max(hh, slot):
                    sp.wait_ge(rows_read, reads(hh, NR))
                    sp.dma_start(words(qs[slot][3 * DH:3 * DH + 1, :]), words(neg_row[slot % 2][:, :])).then_inc(m_ld[slot % 2], 16)

                sp.dma_start(consts[:, :], io["consts"][:, P:4 * P]).then_inc(c_ld, 16)
                for hh in range(3):
                    load_qk(hh, hh)
                load_v(0, 0)
                sp.dma_start(wo_raw[:, :, :], io["wout"].rearrange("(k p) n -> p k n", p=P)).then_inc(w_ld, 16)
                sp.dma_start(select[:, :, :], io["select"].rearrange("h (k p) -> h k p", p=P)).then_inc(w_ld, 16)
                sp.dma_start(eye_out[:, :], io["consts"][:, P:2 * P]).then_inc(w_ld, 16)
                load_max(0, 0)
                load_max(1, 1)

                def store(i, u):
                    hh = UNROLL * i + u
                    slot = u % 2
                    sp.wait_ge(o_read, 2 * (hh + 1))
                    off = 1 if slot == 0 else 0
                    for part in range(2):
                        sp.dma_start(io["o_s"][part, bass.ds(hh * DH, DH), :],
                                     o_out[slot][off + part * DH:off + (part + 1) * DH, :]).then_inc(o_st[slot], 16)
                    row = 0 if slot == 0 else 2 * DH
                    sp.dma_start(io["sum_s"][bass.ds(hh, 1), :], o_out[slot][row:row + 1, :]).then_inc(o_st[slot], 16)

                def body(i, first, last):
                    for u in range(UNROLL):
                        hh = UNROLL * i + u
                        if not (last and u > 0):
                            if not (first and u == 0):
                                sp.wait_ge(s_full, NT * hh)
                            load_qk(hh + 3, (u + 3) % 4)
                        if not (first and u < 2):
                            store(i, u - 2)
                        if u % 2 == 1 and not (last and u == 3):
                            if not (first and u == 1):
                                sp.wait_ge(pv_done, NT * (hh - 1))
                            load_v(2 * i + u // 2 + 1, (u // 2 + 1) % 2)
                        if not (last and u > 1):
                            load_max(hh + 2, (u + 2) % 4)
                    if last:
                        store(i, UNROLL - 2)
                        store(i, UNROLL - 1)

                runs(body)(sp)
                for s in range(2):
                    sp.wait_ge(o_st[s], 48 * HEADS // 2)

            @block.gpsimd
            def _(pool):
                for s in range(4):
                    nc.gpsimd.memset(ks[s][3 * DH:3 * DH + 1, :].bitcast(F32), 1.0).then_inc(fixed, 1)
                pool.wait_ge(fixed, 4)
                for s in range(2):
                    nc.gpsimd.memset(v[s][:, :, 0:1].bitcast(F32), 1.0).then_inc(fixed, 1)
                    nc.gpsimd.memset(v[s][:, :, 4 * DH + 1:].bitcast(F32), 1.0).then_inc(fixed, 1)
                for t in (0, 2, NT, NT + 2):
                    nc.gpsimd.memset(p_hi[t][:, 0:G].bitcast(F32), 0.0).then_inc(fixed, 1)
                    nc.gpsimd.memset(p_lo[t][:, 0:G].bitcast(F32), 0.0).then_inc(fixed, 1)

                pool.wait_ge(wo_hi_done, 1)
                nc.gpsimd.tensor_tensor(wo[:, :, 1, :], wo_raw[:, :, :], wo[:, :, 0, :].bitcast(F32),
                                        ALU.subtract).then_inc(wo_split, 1)

                def body(i, first, last):
                    for u in range(UNROLL):
                        for t in ON_POOL:
                            k = NT * u + t
                            a, b = USED[t]
                            high_wait(pool, i, k)
                            nc.gpsimd.tensor_tensor(p_lo[k % PR][:, a:b], probs[k % NP][:, a:b],
                                                    p_hi[k % PR][:, a:b].bitcast(F32), ALU.subtract).then_inc(lo_pool, 1)

                runs(body)(pool)

            @block.scalar
            def _(act):
                act.wait_ge(w_ld, 48)
                nc.scalar.copy(wo[:, :, 0, :], wo_raw[:, :, :]).then_inc(wo_hi_done, 1)

                def body(i, first, last):
                    def high(k):
                        t = k % NT
                        if t in HIGH_ON_DVE:
                            return
                        a, b = USED[t]
                        act.wait_ge(exp_done, NK * i + k + 1)
                        if not (first and k < PR):
                            act.wait_ge(pv_done, NK * i + k - PR + 1)
                        nc.scalar.copy(p_hi[k % PR][:, a:b], probs[k % NP][:, a:b]).then_inc(hi_act, 1)

                    def heads_out(k, s):
                        u = k // NT
                        act.wait_ge(pv_done, NK * i + k + 1)
                        if s == 0 and not (first and u < 2):
                            act.wait_ge(o_st[u % 2], 24 * (UNROLL * i + u - u % 2))
                        nc.scalar.copy(o_out[u % 2][:, s * CH:(s + 1) * CH],
                                       ps_o[s][0:2 * DH + 1, :]).then_inc(o_read, 1)

                    for k in range(NK):
                        t = k % NT
                        a, b = USED[t]
                        act.wait_ge(s_full, NK * i + k + 1)
                        if not (first and k < NP):
                            lo_wait(act, i, k - NP)
                        nc.scalar.activation(probs[k % NP][:, a:b], ps_t[k % 2][:, a:b], ACT.Exp,
                                             scale=SCALE).then_inc(exp_done, 1)
                        if not (first and k < HIGH_LAG):
                            high(k - HIGH_LAG)
                        done = k - LAG - 1
                        if not (first and done < 0):
                            if done % NT == 1:
                                heads_out(done, 0)
                            if done % NT == NT - 1:
                                heads_out(done, 1)
                    if last:
                        for k in range(NK - HIGH_LAG, NK):
                            high(k)
                        for k in range(NK - LAG - 1, NK):
                            if k % NT == 1:
                                heads_out(k, 0)
                            if k % NT == NT - 1:
                                heads_out(k, 1)

                runs(body)(act)

            @block.vector
            def _(dve):
                dve.wait_ge(c_ld, 16)
                nc.vector.tensor_copy(masks[:, 0:2 * P], consts[:, 0:2 * P]).then_inc(masks_ready, 1)
                nc.vector.tensor_copy(masks[:, 2 * P:3 * P], consts[:, P:2 * P]).then_inc(masks_ready, 1)
                nc.vector.tensor_copy(masks[:, 3 * P:4 * P], consts[:, 2 * P:3 * P]).then_inc(masks_ready, 1)
                nc.vector.tensor_copy(masks[:, 4 * P:5 * P], consts[:, 2 * P:3 * P]).then_inc(masks_ready, 1)

                def row_max(hh, w, r, base, early=False):
                    dve.wait_ge(rows_full, NS * hh + r + 1)
                    bank = row_bank(base + r, early)
                    for res, col, n in ROWS[r][2]:
                        nc.vector.tensor_reduce(neg[w][:, res:res + 1], bank[:, col:col + n], AX.X, ALU.max,
                                                negate=True).then_inc(rows_read, 1)

                def combine(hh, w):
                    dve.wait_ge(rows_read, reads(hh, NR - 1))
                    nc.vector.tensor_tensor(neg[w][:, 4:8], neg[w][:, 4:8], neg[w][:, 8:12],
                                            ALU.min).then_inc(neg_done, 1)

                def take_row(hh, w, base, early=False):
                    dve.wait_ge(rows_full, NS * hh + NS)
                    if not early:
                        dve.wait_ge(m_ld[w], 8 * (hh - w))
                    nc.vector.tensor_copy(neg_row[w][:, :], row_bank(base + NR, early)[0:8, 0:P]).then_inc(rows_read, 1)

                for hh in range(2):
                    for r in range(NR):
                        row_max(hh, hh, r, NS * hh, True)
                    combine(hh, hh)
                    take_row(hh, hh, NS * hh, True)

                def body(i, first, last):
                    def high(k):
                        t = k % NT
                        if t not in HIGH_ON_DVE:
                            return
                        a, b = USED[t]
                        dve.wait_ge(exp_done, NK * i + k + 1)
                        if not (first and k < PR):
                            dve.wait_ge(pv_done, NK * i + k - PR + 1)
                        nc.vector.tensor_copy(p_hi[k % PR][:, a:b], probs[k % NP][:, a:b]).then_inc(hi_dve, 1)

                    def low(k):
                        t = k % NT
                        if t in ON_POOL:
                            return
                        a, b = USED[t]
                        high_wait(dve, i, k)
                        nc.vector.tensor_tensor(p_lo[k % PR][:, a:b], probs[k % NP][:, a:b],
                                                p_hi[k % PR][:, a:b].bitcast(F32), ALU.subtract).then_inc(lo_dve, 1)

                    for k in range(NK):
                        u, t = divmod(k, NT)
                        hh = UNROLL * i + u + 2
                        if not (last and u > 1):
                            for r in AT_TILE[t][:1]:
                                row_max(hh, u % 2, r, NS * u)
                        if not (first and k < LOW_LAG):
                            low(k - LOW_LAG)
                        if not (first and k < HIGH_LAG):
                            high(k - HIGH_LAG)
                        if not (last and u > 1):
                            for r in AT_TILE[t][1:]:
                                row_max(hh, u % 2, r, NS * u)
                            if t == 3:
                                combine(hh, u % 2)
                            if t == 4:
                                take_row(hh, u % 2, NS * u)
                    if last:
                        for k in range(NK - HIGH_LAG, NK):
                            high(k)
                        for k in range(NK - LOW_LAG, NK):
                            low(k)

                runs(body)(dve)

            @block.tensor
            def _(pe):
                pe.wait_ge(masks_ready, 4)
                pe.wait_ge(fixed, 16)

                def rows(hh, slot, r, base, early=False):
                    if not early:
                        pe.wait_ge(rows_read, reads(hh, r - 2))
                    elif base + r >= EARLY:
                        pe.wait_ge(rows_read, reads(hh, r - EARLY))
                    out = row_bank(base + r, early)
                    products, diag, _ = ROWS[r]
                    for x, (col, blk, k0, n) in enumerate(products):
                        mm = nc.tensor.matmul(out[:, col:col + n], qs[slot][0:3 * DH, blk * G:(blk + 1) * G],
                                              ks[slot][0:3 * DH, k0:k0 + n], start=x == 0, stop=diag is None)
                    if diag is not None:
                        col, n = diag
                        mm = nc.tensor.matmul(out[:, col:col + n], eye, mask_rows[:, 0:n], start=False, stop=True)
                    mm.then_inc(rows_full, 1)

                def turn(hh, w, base, early=False):
                    pe.wait_ge(neg_done, hh + 1)
                    pe.wait_ge(rows_read, reads(hh, NR - 1))
                    nc.tensor.transpose(row_bank(base + NR, early)[0:8, 0:P], neg[w][:, 0:8], eye_f).then_inc(rows_full, 1)

                for hh in range(2):
                    pe.wait_ge(qk_ld[hh], 96)
                    for r in range(NR):
                        rows(hh, hh, r, NS * hh, True)
                    turn(hh, hh, NS * hh, True)

                def body(i, first, last):
                    def scores(k):
                        u, t = divmod(k, NT)
                        if t == 0:
                            pe.wait_ge(m_ld[u % 2], 8 * (UNROLL * i + u - u % 2) + 16)
                        if not (first and k < 2):
                            pe.wait_ge(exp_done, NK * i + k - 1)
                        out = ps_t[k % 2]
                        for bank in range(2):
                            diag = [(c, w) for c, w in DIAGONALS[t] if c // CH == bank]
                            products = [p for p in TILES[t] if p[0] // CH == bank]
                            for x, (col, kb, q0, n) in enumerate(products):
                                mm = nc.tensor.matmul(out[:, col:col + n], ks[u][:, kb * G:(kb + 1) * G],
                                                      qs[u][:, q0:q0 + n], start=x == 0, stop=not diag)
                        for c, w in reversed(DIAGONALS[t]):
                            mm = nc.tensor.matmul(out[:, c:c + w], eye, mask_cols[:, 0:w], start=False, stop=True)
                        mm.then_inc(s_full, 1)

                    def times_v(k, entries):
                        u, t = divmod(k % NK, NT)
                        pair = (u // 2) % 2
                        off = 0 if u % 2 == 0 else 2 * DH + 1
                        if entries == "first":
                            lo_wait(pe, i, k)
                        if entries == "first" and t == 0 and u % 2 == 0:
                            pe.wait_ge(v_ld[pair], 16 * i + 16)
                        if entries == "first" and not (first and k < NT) and t < 2:
                            pe.wait_ge(o_read, 2 * (UNROLL * i + k // NT) - (1 if t == 0 else 0))
                        for e in PV[t][:1] if entries == "first" else PV[t][1:]:
                            col, kb, q0, n = TILES[t][e]
                            s = 0 if q0 < S // 2 else 1
                            for part in (p_hi, p_lo):
                                mm = nc.tensor.matmul(ps_o[s][0:2 * DH + 1, q0 - s * CH:q0 - s * CH + n],
                                                      v[pair][:, kb, off:off + 2 * DH + 1], part[k % PR][:, col:col + n],
                                                      start=(t, e) in OPENS and part is p_hi,
                                                      stop=(t, e) in CLOSES and part is p_lo)
                        if entries == "rest":
                            mm.then_inc(pv_done, 1)

                    for k in range(NK):
                        u, t = divmod(k, NT)
                        hh = UNROLL * i + u + 2
                        more = not (last and u > 1)
                        back = not (first and k < LAG)

                        def row(n):
                            if more and n < len(AT_TILE[t]):
                                rows(hh, (u + 2) % 4, AT_TILE[t][n], NS * u)

                        if more and t == 0:
                            pe.wait_ge(qk_ld[(u + 2) % 4], 96 * (i + (1 if u < 2 else 2)))
                        row(0)
                        scores(k)
                        row(1)
                        if back:
                            times_v(k - LAG, "first")
                        row(2)
                        if more and t == 4:
                            turn(hh, u % 2, NS * u)
                        if back:
                            times_v(k - LAG, "rest")
                    if last:
                        for k in range(NK - LAG, NK):
                            times_v(k, "first")
                            times_v(k, "rest")

                runs(body)(pe)


def project_out(nc, sem, io, out_weights, ahead):
    _, wo, select, eye, w_ld, _, wo_split = out_weights
    W = CH // 2
    U = S // W
    TT = W // P
    NC = B * U

    with ExitStack() as ctx:
        sb = lambda name, shape, dt: ctx.enter_context(nc.sbuf_tensor(name, shape, dt))
        sums = [sb(f"sums{s}", [H, W], F32) for s in range(U)]
        rsum = [sb(f"rsum{s}", [H, W], F32) for s in range(U)]
        o_a = [sb(f"o_a{s}", [P, KT, W], F32) for s in range(U)]
        o_b = [sb(f"o_b{s}", [P, KT, W], F32) for s in range(U)]
        o_hi = [sb(f"o_hi{s}", [P, KT, W], F32R) for s in range(2)]
        o_lo = [sb(f"o_lo{s}", [P, KT, W], F32R) for s in range(2)]
        xn = [sb(f"xn{s}", [P, TT, D], F32) for s in range(U)]
        x1 = [sb(f"x1_{s}", [P, TT, D], F32) for s in range(U)]
        x1t = [sb(f"x1t{s}", [P, KT, W], F32) for s in range(2)]
        stats = sb("stats", [P, TT, 6], F32)
        mv = sb("mv", [P, TT, 2], F32)
        std = sb("std", [P, TT], F32)
        rstd = sb("rstd", [P, TT], F32)
        eps = sb("eps", [P, 1], F32)
        ps_y = [[ctx.enter_context(nc.psum_tensor(f"y{s}_{t}", [P, D], F32)) for t in range(TT)] for s in range(2)]
        ps_x = [ctx.enter_context(nc.psum_tensor(f"turned{j}", [P, 2, W], F32)) for j in range(KT // 2)]
        ps_r = ctx.enter_context(nc.psum_tensor("inverses", [P, KT, W], F32))

        sum_ld = [sem(f"sum_ld{s}") for s in range(U)]
        rsum_done = sem("rsum_done")
        r_full = sem("inverses_full")
        o_ld = [sem(f"o_ld{s}") for s in range(U)]
        x_ld = [sem(f"xn_ld{s}") for s in range(U)]
        joined = sem("o_joined")
        normed = sem("o_normed")
        o_hi_done = sem("o_hi_done")
        o_split = sem("o_split")
        y_full = sem("y_full")
        z_done = sem("z_done")
        rstd_done = sem("po_rstd_done")
        var_done = sem("po_var_done")
        std_done = sem("po_std_done")
        x1_done = sem("x1_done")
        turned = sem("x1_turned")
        t_done = sem("x1t_done")
        x1_st = [sem(f"x1_st{s}") for s in range(U)]
        x1t_st = [sem(f"x1t_st{s}") for s in range(2)]
        eps_set = sem("po_eps_set")

        def o_low(engine, queue, c, slot):
            queue.wait_ge(o_hi_done, c + 1)
            engine.tensor_tensor(o_lo[slot % 2][:, :, :], o_a[slot][:, :, :],
                                 o_hi[slot % 2][:, :, :].bitcast(F32), ALU.subtract).then_inc(o_split, 1)

        with nc.Block() as block:
            @block.sync
            def _(sp):
                def load_sums(b, u, first):
                    if not first:
                        sp.wait_ge(rsum_done, U * b + u - U + 1)
                    sp.dma_start(sums[u][:, :], io["sum_s"][bass.ds(b * H, H), u * W:(u + 1) * W]
                                 ).then_inc(sum_ld[u], 16)

                def load_o(b, u, first):
                    tok = slice(u * W, (u + 1) * W)
                    if not first:
                        sp.wait_ge(o_split, U * b + u - U + 1)
                    for part, dst in ((0, o_a), (1, o_b)):
                        sp.dma_start(dst[u][:, :, :],
                                     io["o_s"][part, bass.ds(b * D, D), tok].rearrange("(k p) t -> p k t", p=P)
                                     ).then_inc(o_ld[u], 16)

                def load_x(b, u, first):
                    if not first:
                        sp.wait_ge(z_done, TT * (U * b + u - U + 1))
                    sp.dma_start(xn[u][:, :, :], io["x"][bass.ds(b * S + u * W, W), :].rearrange(
                        "(t p) d -> p t d", p=P)).then_inc(x_ld[u], 16)

                def store_x1(b, u):
                    sp.wait_ge(x1_done, TT * (U * b + u + 1))
                    sp.dma_start(io["x1_s"][bass.ds(b * S + u * W, W), :].rearrange("(t p) d -> p t d", p=P),
                                 x1[u][:, :, :]).then_inc(x1_st[u], 16)

                def store_x1t(b, u):
                    sp.wait_ge(t_done, KT // 2 * (U * b + u + 1))
                    dst = io["x1t_s"][bass.ds(2 * b + u // 2, 1)].rearrange("o p k t -> p (o k) t")
                    sp.dma_start(dst[:, :, u % 2 * W:(u % 2 + 1) * W], x1t[u % 2][:, :, :]).then_inc(x1t_st[u % 2], 16)

                for u in range(U):
                    load_sums(0, u, True)
                load_o(0, 0, True)
                load_o(0, 1, True)
                load_x(0, 0, True)
                load_o(0, 2, True)
                load_x(0, 1, True)
                load_o(0, 3, True)
                load_x(0, 2, True)

                def load_ahead(u):
                    for f in range(u, ahead.FIRST, U):
                        sp.dma_start(words(ahead.wug[f][:, :, :, :, :].rearrange("p g c k n -> p (g c k n)")),
                                     io["wug_s"][f].rearrange("p g c k n -> p (g c k n)")).then_inc(ahead.wug_ld[f], 16)
                    if u == 0:
                        for s in range(2):
                            sp.wait_ge(x1t_st[s], 16)
                        sp.dma_start(ahead.xt_raw[:, :, :], io["x1t_s"][0]).then_inc(ahead.xt_ld, 16)
                    if u == 1:
                        for f, wd in enumerate(ahead.wd):
                            sp.dma_start(words(wd[:, :, :]), io["wd_s"][f]).then_inc(ahead.wd_ld[f], 16)

                def body(b, first, last):
                    for u in range(U):
                        if last:
                            load_ahead(u)
                        else:
                            load_sums(b + 1, u, False)
                            load_o(b + 1, u, False)
                        over, nu = divmod(u + 3, U)
                        if not (last and over):
                            load_x(b + over, nu, first and not over)
                        store_x1(b, u)
                        if u > 0:
                            store_x1t(b, u - 1)
                        elif not first:
                            store_x1t(b - 1, U - 1)

                body(0, True, False)
                with sp.Fori(1, B - 1) as b:
                    body(b, False, False)
                body(B - 1, False, True)
                store_x1t(B - 1, U - 1)
                for s in range(U):
                    sp.wait_ge(x1_st[s], 16 * B)
                for s in range(2):
                    sp.wait_ge(x1t_st[s], 16 * NC // 2)

            @block.gpsimd
            def _(pool):
                def join(b, u):
                    pool.wait_ge(o_ld[u], 32 * b + 32)
                    nc.gpsimd.tensor_tensor(o_a[u][:, :, :], o_a[u][:, :, :], o_b[u][:, :, :],
                                            ALU.add).then_inc(joined, 1)

                def body(b, last):
                    for u in range(U):
                        over, nu = divmod(u + 3, U)
                        if not (last and over):
                            join(b + over, nu)
                        over, nu = divmod(u + 2, U)
                        if not (last and over):
                            o_low(nc.gpsimd, pool, U * b + u + 2, nu)

                for u in range(3):
                    join(0, u)
                with pool.Fori(0, B - 1) as b:
                    body(b, False)
                body(B - 1, True)
                for k in range(KT):
                    pool.wait_ge(ahead.xt_hi_done, k + 1)
                    nc.gpsimd.tensor_tensor(ahead.xt[0][:, k, 1, :], ahead.xt_raw[:, k, :],
                                            ahead.xt[0][:, k, 0, :].bitcast(F32),
                                            ALU.subtract).then_inc(ahead.xt_split, 1)

            @block.scalar
            def _(act):
                def o_high(c, slot, first):
                    act.wait_ge(normed, c + 1)
                    if not first:
                        act.wait_ge(y_full, TT * (c - 1))
                    nc.scalar.copy(o_hi[slot % 2][:, :, :], o_a[slot][:, :, :]).then_inc(o_hi_done, 1)

                def x1t_out(b, u, first):
                    for j in range(KT // 2):
                        act.wait_ge(turned, KT // 2 * (U * b + u) + j + 1)
                        if not (first and u < 2) and j == 0:
                            act.wait_ge(x1t_st[u % 2], 16 * (U // 2 * b + u // 2))
                        nc.scalar.copy(x1t[u % 2][:, 2 * j:2 * j + 2, :], ps_x[j][:, :, :]).then_inc(t_done, 1)

                def body(b, first, last):
                    for u in range(U):
                        c = U * b + u
                        act.wait_ge(var_done, c + 1)
                        nc.scalar.activation(std[:, :], mv[:, :, 1], ACT.Sqrt, bias=eps[:, 0:1]).then_inc(std_done, 1)
                        if not (last and u + 2 >= U):
                            o_high(c + 2, (u + 2) % U, False)
                        if u > 0:
                            x1t_out(b, u - 1, first)
                        elif not first:
                            x1t_out(b - 1, U - 1, False)
                        if last and u > 1:
                            act.wait_ge(ahead.xt_ld, 16)
                            for k in (0, 1) if u == 2 else (2, 3):
                                nc.scalar.copy(ahead.xt[0][:, k, 0, :], ahead.xt_raw[:, k, :]
                                               ).then_inc(ahead.xt_hi_done, 1)

                act.wait_ge(eps_set, 1)
                o_high(0, 0, True)
                o_high(1, 1, True)
                body(0, True, False)
                with act.Fori(1, B - 1) as b:
                    body(b, False, False)
                body(B - 1, False, True)
                x1t_out(B - 1, U - 1, False)

            @block.vector
            def _(dve):
                nc.vector.memset(eps[:, :], EPS).then_inc(eps_set, 1)

                def inverse(b, u, first):
                    dve.wait_ge(sum_ld[u], 16 * b + 16)
                    if not first:
                        dve.wait_ge(r_full, U * b + u - U + 1)
                    nc.vector.reciprocal(rsum[u][:, :], sums[u][:, :]).then_inc(rsum_done, 1)

                def normalise(c, slot):
                    dve.wait_ge(joined, c + 1)
                    dve.wait_ge(r_full, c + 1)
                    nc.vector.tensor_tensor(o_a[slot][:, :, :], o_a[slot][:, :, :], ps_r[:, :, :],
                                            ALU.mult).then_inc(normed, 1)

                def body(b, first, last):
                    for u in range(U):
                        c = U * b + u
                        dve.wait_ge(x_ld[u], 16 * b + 16)
                        if not first:
                            dve.wait_ge(x1_st[u], 16 * b)
                        for t in range(TT):
                            dve.wait_ge(y_full, TT * c + t + 1)
                            nc.vector.tensor_tensor(x1[u][:, t, :], ps_y[u % 2][t][:, :], xn[u][:, t, :],
                                                    ALU.add).then_inc(z_done, 1)
                            dve.wait_ge(z_done, TT * c + t + 1)
                            nc.vector.bn_stats(stats[:, t, :], x1[u][:, t, :])
                        dve.drain()
                        for t in range(TT):
                            mm = nc.vector.bn_aggr(mv[:, t, :], stats[:, t, :])
                        mm.then_inc(var_done, 1)
                        if not (last and u + 3 >= U):
                            normalise(c + 3, (u + 3) % U)
                        dve.wait_ge(std_done, c + 1)
                        nc.vector.reciprocal(rstd[:, :], std[:, :]).then_inc(rstd_done, 1)
                        dve.wait_ge(rstd_done, c + 1)
                        for t in range(TT):
                            nc.vector.tensor_scalar(x1[u][:, t, :], x1[u][:, t, :], mv[:, t, 0:1], rstd[:, t:t + 1],
                                                    ALU.subtract, ALU.mult).then_inc(x1_done, 1)
                        if not last:
                            inverse(b + 1, u, False)

                inverse(0, 0, True)
                for u in range(3):
                    inverse(0, u + 1, True)
                    normalise(u, u)
                    if u < 2:
                        o_low(nc.vector, dve, u, u)
                body(0, True, False)
                with dve.Fori(1, B - 1) as b:
                    body(b, False, False)
                body(B - 1, False, True)

            @block.tensor
            def _(pe):
                def inverses(c, slot, first):
                    pe.wait_ge(rsum_done, c + 1)
                    if not first:
                        pe.wait_ge(normed, c)
                    for k in range(KT):
                        mm = nc.tensor.matmul(ps_r[:, k, :], select[:, k, :], rsum[slot][:, :], start=True, stop=True)
                    mm.then_inc(r_full, 1)

                def product(c, u, first):
                    pe.wait_ge(o_split, c + 1)
                    for t in range(TT):
                        if not first:
                            pe.wait_ge(z_done, TT * (c - 2) + t + 1)
                        k = 0
                        for kt in range(KT):
                            for op, wp in PASSES:
                                mm = nc.tensor.matmul(ps_y[u % 2][t][:, :],
                                                      (o_hi, o_lo)[op][u % 2][:, kt, t * P:(t + 1) * P],
                                                      wo[:, kt, wp, :], start=(k == 0), stop=(k == 11))
                                k += 1
                        mm.then_inc(y_full, 1)

                def turn(c, slot, first):
                    pe.wait_ge(x1_done, TT * (c + 1))
                    for j in range(KT // 2):
                        if not first:
                            pe.wait_ge(t_done, KT // 2 * (c - 1) + j + 1)
                        for k in range(2):
                            for t in range(TT):
                                mm = nc.tensor.transpose(
                                    ps_x[j][:, k, t * P:(t + 1) * P],
                                    x1[slot][:, t, (2 * j + k) * P:(2 * j + k + 1) * P], eye[:, :])
                        mm.then_inc(turned, 1)

                def body(b, first, last):
                    for u in range(U):
                        c = U * b + u
                        product(c, u, first and u < 2)
                        if first and u == 0:
                            inverses(2, 2, False)
                        if not (last and u + 3 >= U):
                            inverses(c + 3, (u + 3) % U, False)
                        if not (first and u == 0):
                            turn(c - 1, (u - 1) % U, first and u == 1)

                pe.wait_ge(w_ld, 48)
                pe.wait_ge(wo_split, 1)
                for u in range(2):
                    inverses(u, u, u == 0)
                body(0, True, False)
                with pe.Fori(1, B - 1) as b:
                    body(b, False, False)
                body(B - 1, False, True)
                turn(NC - 1, U - 1, False)


class Ahead:
    FIRST = 2
    WR = 2

    def __init__(self, sb, sem, out_weights):
        self.wug = [sb(f"wug{f}", [P, 2, 2, KT, P], F32R) for f in range(self.FIRST)]
        self.wd = [sb(f"wd{s}", [P, 2, D], F32R) for s in range(self.WR)]
        self.xt_raw = out_weights[0]
        self.xt = [sb("ff_xt0", [P, KT, 2, CH], F32R), out_weights[1]]
        self.wug_ld = [sem(f"wug_ld{f}") for f in range(self.FIRST)]
        self.wd_ld = [sem(f"wd_ld{s}") for s in range(self.WR)]
        self.xt_ld = sem("ff_xt_ld")
        self.xt_hi_done = sem("ff_xt_hi_done")
        self.xt_split = sem("ff_xt_split")


def feed_forward(nc, sem, io, ahead):
    TT = CH // P
    WR = ahead.WR
    wd, wd_ld, xt, xt_raw = ahead.wd, ahead.wd_ld, ahead.xt, ahead.xt_raw
    xt_ld, xt_hi_done, xt_split = ahead.xt_ld, ahead.xt_hi_done, ahead.xt_split

    with ExitStack() as ctx:
        sb = lambda name, shape, dt: ctx.enter_context(nc.sbuf_tensor(name, shape, dt))
        wug = ahead.wug + [sb(f"wug{f}", [P, 2, 2, KT, P], F32R) for f in range(ahead.FIRST, FT)]
        z = sb("ff_z", [P, TT, D], F32)
        sil = [sb(f"silu{s}", [P, CH], F32) for s in range(2)]
        hid = [sb(f"hidden{s}", [P, CH], F32) for s in range(2)]
        h_hi = [sb(f"h_hi{s}", [P, CH], F32R) for s in range(2)]
        h_lo = [sb(f"h_lo{s}", [P, CH], F32R) for s in range(2)]
        ws = sb("ff_ws", [P, 2 * FT], F32)
        stats = sb("ff_stats", [P, TT, 6], F32)
        mv = sb("ff_mv", [P, TT, 2], F32)
        std = sb("ff_std", [P, TT], F32)
        rstd = sb("ff_rstd", [P, TT], F32)
        eps = sb("ff_eps", [P, 1], F32)
        ps_g = [ctx.enter_context(nc.psum_tensor(f"gate{s}", [P, CH], F32)) for s in range(2)]
        ps_u = [ctx.enter_context(nc.psum_tensor(f"up{s}", [P, CH], F32)) for s in range(2)]
        ps_y = [ctx.enter_context(nc.psum_tensor(f"ff_y{s}", [P, D], F32)) for s in range(TT)]

        wug_ld = ahead.wug_ld + [sem(f"wug_ld{f}") for f in range(ahead.FIRST, FT)]
        z_ld = sem("ff_z_ld")
        ws_ld = sem("ff_ws_ld")
        gate_full = sem("gate_full")
        up_full = sem("up_full")
        sil_done = sem("silu_done")
        hid_done = sem("hidden_done")
        hhi_done = sem("h_hi_done")
        h_split = sem("h_split")
        down_done = sem("down_done")
        y_done = sem("ff_y_done")
        z_done = sem("ff_z_done")
        rstd_done = sem("ff_rstd_done")
        var_done = sem("ff_var_done")
        std_done = sem("ff_std_done")
        out_done = sem("ff_out_done")
        out_st = sem("out_st")
        eps_set = sem("ff_eps_set")

        with nc.Block() as block:
            @block.sync
            def _(sp):
                sp.dma_start(ws[:, :], io["ws_ug"]).then_inc(ws_ld, 16)

                def load_wug(f):
                    sp.dma_start(words(wug[f][:, :, :, :, :].rearrange("p g c k n -> p (g c k n)")),
                                 io["wug_s"][f].rearrange("p g c k n -> p (g c k n)")).then_inc(wug_ld[f], 16)

                def load_xt(c):
                    sp.dma_start(xt_raw[:, :, :],
                                 io["x1t_s"][bass.ds(c, 1)].rearrange("o p k t -> p (o k) t")).then_inc(xt_ld, 16)

                def load_wd(f):
                    sp.dma_start(words(wd[f % WR][:, :, :]), io["wd_s"][f]).then_inc(wd_ld[f % WR], 16)

                def tail(c, u):
                    sp.wait_ge(out_done, TT * c + TT)
                    sp.dma_start(io["out"][bass.ds(c * CH, CH), :].rearrange("(t p) d -> p t d", p=P),
                                 z[:, :, :]).then_inc(out_st, 16)

                def load_z(c):
                    sp.dma_start(z[:, :, :], io["x1_s"][bass.ds(c * CH, CH), :].rearrange(
                        "(t p) d -> p t d", p=P)).then_inc(z_ld, 16)

                load_z(0)

                def body(i, first, last):
                    for u in range(2):
                        c = 2 * i + u
                        for f in range(FT):
                            if first and u == 0 and f + ahead.FIRST < FT:
                                load_wug(f + ahead.FIRST)
                            if f == 1 and not (last and u == 1):
                                sp.wait_ge(xt_split, KT * c + KT)
                                load_xt(c + 1)
                            if not (last and u == 1 and f + WR >= FT):
                                sp.wait_ge(down_done, FT * c + f + 1)
                                load_wd((f + WR) % FT)
                            if f == 8 and not (first and u == 0):
                                tail(c - 1, u)
                                sp.wait_ge(out_st, 16 * c)
                                load_z(c)

                body(0, True, False)
                with sp.Fori(1, B - 1) as i:
                    body(i, False, False)
                body(B - 1, False, True)
                for t in range(TT):
                    sp.wait_ge(out_done, TT * (NCH - 1) + t + 1)
                    sp.dma_start(io["out"][T - CH + t * P:T - CH + (t + 1) * P, :], z[:, t, :]).then_inc(out_st, 16)
                sp.wait_ge(out_st, 16 * (NCH - 1 + TT))

            @block.scalar
            def _(act):
                act.wait_ge(ws_ld, 16)
                act.wait_ge(eps_set, 1)

                def xt_high(c, s, k):
                    if k == 0:
                        act.wait_ge(xt_ld, 16 * c + 16)
                    nc.scalar.copy(xt[s][:, k, 0, :], xt_raw[:, k, :]).then_inc(xt_hi_done, 1)

                def body(i, first, last):
                    for u in range(2):
                        for f in range(FT):
                            c = 2 * i + u
                            n = FT * c + f
                            act.wait_ge(gate_full, n + 1)
                            if not (first and u == 0 and f < 2):
                                act.wait_ge(hid_done, n - 1)
                            nc.scalar.activation(sil[f % 2][:, :], ps_g[f % 2][:, :], ACT.Silu,
                                                 scale=ws[:, FT + f:FT + f + 1]).then_inc(sil_done, 1)
                            act.wait_ge(hid_done, n + 1)
                            if not (first and u == 0 and f < 2):
                                act.wait_ge(down_done, n - 1)
                            nc.scalar.copy(h_hi[f % 2][:, :], hid[f % 2][:, :]).then_inc(hhi_done, 1)
                            if 8 <= f < 8 + KT and not (last and u == 1):
                                xt_high(c + 1, 1 - u, f - 8)
                            if f == 3 and not (first and u == 0):
                                act.wait_ge(var_done, c)
                                nc.scalar.activation(std[:, :], mv[:, :, 1], ACT.Sqrt,
                                                     bias=eps[:, 0:1]).then_inc(std_done, 1)

                body(0, True, False)
                with act.Fori(1, B - 1) as i:
                    body(i, False, False)
                body(B - 1, False, True)
                act.wait_ge(var_done, NCH)
                nc.scalar.activation(std[:, :], mv[:, :, 1], ACT.Sqrt, bias=eps[:, 0:1]).then_inc(std_done, 1)

            @block.gpsimd
            def _(pool):
                def xt_low(c, s):
                    for k in range(KT):
                        pool.wait_ge(xt_hi_done, KT * c + k + 1)
                        nc.gpsimd.tensor_tensor(xt[s][:, k, 1, :], xt_raw[:, k, :], xt[s][:, k, 0, :].bitcast(F32),
                                                ALU.subtract).then_inc(xt_split, 1)

                with pool.Fori(0, B - 1) as i:
                    xt_low(2 * i + 1, 1)
                    xt_low(2 * i + 2, 0)
                xt_low(NCH - 1, 1)

            @block.vector
            def _(dve):
                nc.vector.memset(eps[:, :], EPS).then_inc(eps_set, 1)
                dve.wait_ge(ws_ld, 16)

                def sums(c):
                    dve.wait_ge(z_ld, 16 * c)
                    for t in range(TT):
                        if t < TT - 1:
                            dve.wait_ge(y_done, (TT - 1) * (c - 1) + t + 1)
                        else:
                            dve.wait_ge(down_done, FT * c)
                        nc.vector.tensor_tensor(z[:, t, :], ps_y[t][:, :], z[:, t, :], ALU.add).then_inc(z_done, 1)
                    for t in range(TT):
                        dve.wait_ge(z_done, TT * (c - 1) + t + 1)
                        nc.vector.bn_stats(stats[:, t, :], z[:, t, :])
                    dve.drain()
                    for t in range(TT):
                        mm = nc.vector.bn_aggr(mv[:, t, :], stats[:, t, :])
                    mm.then_inc(var_done, 1)

                def norm(c):
                    dve.wait_ge(std_done, c)
                    nc.vector.reciprocal(rstd[:, :], std[:, :]).then_inc(rstd_done, 1)
                    dve.wait_ge(rstd_done, c)
                    for t in range(TT):
                        nc.vector.tensor_scalar(z[:, t, :], z[:, t, :], mv[:, t, 0:1], rstd[:, t:t + 1],
                                                ALU.subtract, ALU.mult).then_inc(out_done, 1)

                def body(i, first):
                    for u in range(2):
                        c = 2 * i + u
                        for f in range(FT):
                            n = FT * c + f
                            if f == 1 and not (first and u == 0):
                                sums(c)
                            dve.wait_ge(up_full, n + 1)
                            dve.wait_ge(sil_done, n + 1)
                            nc.vector.scalar_tensor_tensor(hid[f % 2][:, :], ps_u[f % 2][:, :], ws[:, f:f + 1],
                                                           sil[f % 2][:, :], ALU.mult, ALU.mult).then_inc(hid_done, 1)
                            dve.wait_ge(hhi_done, n + 1)
                            nc.vector.tensor_tensor(h_lo[f % 2][:, :], hid[f % 2][:, :],
                                                    h_hi[f % 2][:, :].bitcast(F32), ALU.subtract).then_inc(h_split, 1)
                            if f == 4 and not (first and u == 0):
                                norm(c)

                body(0, True)
                with dve.Fori(1, B) as i:
                    body(i, False)
                sums(NCH)
                norm(NCH)

            @block.tensor
            def _(pe):
                def gate_up(i, u, f, first):
                    c = 2 * i + u
                    n = FT * c + f
                    if f == 0:
                        pe.wait_ge(xt_split, KT * c + KT)
                    if first and u == 0:
                        pe.wait_ge(wug_ld[f], 16)
                    if not (first and u == 0 and f < 2):
                        pe.wait_ge(hid_done, n - 1)
                    for g, (bank, done) in ((1, (ps_g, gate_full)), (0, (ps_u, up_full))):
                        k = 0
                        for kt in range(KT):
                            for wp, xp in PASSES:
                                mm = nc.tensor.matmul(bank[f % 2][:, :], wug[f][:, g, wp, kt, :],
                                                      xt[u][:, kt, xp, :], start=(k == 0), stop=(k == 11))
                                k += 1
                        mm.then_inc(done, 1)

                def down(c, f, first):
                    pe.wait_ge(h_split, FT * c + f + 1)
                    pe.wait_ge(wd_ld[f % WR], 16 * (FT // WR) * c + 16 * (f // WR) + 16)
                    for t in range(TT):
                        if f == 0 and not first:
                            pe.wait_ge(z_done, TT * (c - 1) + t + 1)
                        for k, (hp, wp) in enumerate(PASSES):
                            mm = nc.tensor.matmul(ps_y[t][:, :], (h_hi, h_lo)[hp][f % 2][:, t * P:(t + 1) * P],
                                                  wd[f % WR][:, wp, :], start=(f == 0 and k == 0),
                                                  stop=(f == FT - 1 and k == 2))
                        if t == TT - 1:
                            mm.then_inc(down_done, 1)
                        elif f == FT - 1:
                            mm.then_inc(y_done, 1)

                def body(i, first):
                    for u in range(2):
                        c = 2 * i + u
                        for f in range(FT):
                            gate_up(i, u, f, first)
                            if f > 0:
                                down(c, f - 1, first and u == 0)
                            elif not (first and u == 0):
                                down(c - 1, FT - 1, False)

                body(0, True)
                with pe.Fori(1, B) as i:
                    body(i, False)
                down(NCH - 1, FT - 1, False)


_HOST = ["x", "xt", "wqkv", "wout", "wugt", "wdt", "su_ug", "su_dp", "ws_ug", "ws_dp", "consts", "select"]
_SCRATCH = {
    "q_s": [2, B * D, S], "k_s": [2, B * D, S],
    "v_s": [B * 8, S, P],
    "wd_s": [FT, P, 2, D], "wug_s": [FT, P, 2, 2, KT, P],
    "x1t_s": [NCH, P, KT, CH],
    "o_s": [2, B * D, S], "sum_s": [B * H, S], "x1_s": [T, D],
}


def build(nc, io):
    for name, shape in _SCRATCH.items():
        io[name] = nc.dram_tensor(name, shape, F32, kind="Internal").ap()
    with ExitStack() as ctx:
        def sem(name):
            return ctx.enter_context(nc.semaphore(name))
        project_qkv(nc, sem, io)
        with ExitStack() as held:
            sb = lambda name, shape, dt: held.enter_context(nc.sbuf_tensor(name, shape, dt))
            out_weights = (sb("wo_raw", [P, KT, D], F32), sb("wo", [P, KT, 2, D], F32R),
                           sb("select", [H, KT, P], F32),
                           sb("eye_out", [P, P], F32), sem("wo_ld"), sem("wo_hi_done"), sem("wo_split"))
            attend(nc, sem, io, out_weights)
            ahead = Ahead(sb, sem, out_weights)
            project_out(nc, sem, io, out_weights, ahead)
            feed_forward(nc, sem, io, ahead)


def constants():
    had = np.ones((1, 1), np.float32)
    while had.shape[0] < P:
        had = np.block([[had, had], [had, -had]])
    eye = np.eye(P, dtype=np.float32)
    later = np.triu(np.ones((P, P), np.float32), 1) * np.float32(MASKED)
    return np.ascontiguousarray(np.concatenate([had, eye, later, later.T], axis=1), dtype=np.float32)


def kernel(**inputs):
    import concourse.bacc as _bacc
    from concourse import mybir as _mybir
    from concourse.bass_utils import run_bass_kernel_spmd as _run

    a = {k: np.asarray(v) for k, v in inputs.items()}
    x = a["L0_attn_x"].reshape(T, D)
    arrays = {
        "x": x,
        "xt": x.T,
        "wqkv": a["L0_attn_w_qkv"],
        "wout": a["L0_attn_w_out"],
        "wugt": np.concatenate([a["L0_ffn_W_up"], a["L0_ffn_W_gate"]], axis=0).T,
        "wdt": a["L0_ffn_W_down"].T,
        "su_ug": a["L0_ffn_SU_ug"].reshape(KT, P).T,
        "su_dp": a["L0_ffn_SU_dp"].reshape(FT, P).T,
        "ws_ug": a["L0_ffn_Wscale_ug"].reshape(2 * FT, P).T,
        "ws_dp": a["L0_ffn_Wscale_dp"],
        "consts": constants(),
        "select": np.repeat(np.eye(H, dtype=np.float32), DH, axis=1),
    }
    nc = _bacc.Bacc("TRN2", target_bir_lowering=False, num_devices=1)
    fed, io = {}, {}
    for name in _HOST:
        v = np.ascontiguousarray(arrays[name])
        fed[f"in_{name}"] = v
        io[name] = nc.dram_tensor(f"in_{name}", v.shape, _mybir.dt.from_np(v.dtype), kind="ExternalInput").ap()
    io["out"] = nc.dram_tensor("out_0", (T, D), F32, kind="ExternalOutput").ap()
    build(nc, io)
    r = _run(nc, [fed], core_ids=[0])
    return r.results[0]["out_0"].reshape(B, S, D)
```
